# Optimizing a Trainium2 kernel written in Bass

```python
import numpy as np
import jax
import jax.numpy as jnp

def _softmax(x, axis=-1):
    return jax.nn.softmax(x, axis=axis)

def _gelu(x):
    return jax.nn.gelu(x, approximate=True)

def _silu(x):
    return jax.nn.silu(x)

def _sigmoid(x):
    return jax.nn.sigmoid(x)

def _layernorm(x, axis=-1, eps=1e-05):
    m = jnp.mean(x, axis=axis, keepdims=True)
    v = jnp.var(x, axis=axis, keepdims=True)
    return (x - m) / jnp.sqrt(v + eps)

def _scatter_add(tgt, idx, src, axis=0):
    return tgt.at[idx].add(src)

def _segment_sum(src, seg, n):
    return jax.ops.segment_sum(src, seg, n)
kernel_name = 'mk_pixart_resid_d2_seqx_r2_3b6e33'

def setup_inputs(seed: int=0):
    np.random.seed(seed)
    _w = jnp.asarray

    def _rec_inputs():
        import jax
        import jax.numpy as jnp
        _rk = jax.random.key(seed)
        x = -0.0002928 + 1 * jax.random.normal(jax.random.fold_in(_rk, 1), (4, 2048, 512), jnp.float32)
        _lenS = 2048 - jax.random.randint(jax.random.fold_in(_rk, 7), (4,), 0, max(1, 2048 // 4) + 1, jnp.int32)
        _lenS2 = 77 - jax.random.randint(jax.random.fold_in(_rk, 8), (4,), 0, max(1, 77 // 4) + 1, jnp.int32)
        _ctx_1024P = jax.random.normal(jax.random.fold_in(_rk, 11), (4, 16, 512), jnp.float32)
        _ctx_1024c = jax.random.dirichlet(jax.random.fold_in(_rk, 511), 0.3 * jnp.ones((16,), jnp.float32), (4, 77))
        _ctx_1024t = jnp.einsum('bsk,bkd->bsd', _ctx_1024c, _ctx_1024P)
        _ctx_1024t = _ctx_1024t * jax.lax.rsqrt(jnp.mean(jnp.square(_ctx_1024t)) + 1e-12) * 0.953939
        ctx_1024 = -1.39393e-06 + 0.999914 * (_ctx_1024t + 0.3 * jax.random.normal(jax.random.fold_in(_rk, 611), (4, 77, 512), jnp.float32))
        condB_tau = jax.random.uniform(jax.random.fold_in(_rk, 12), (4,), jnp.float32, 0.0, 1.23395)
        fside_BxS2_0 = -0.00205293 + 0.99739 * jax.random.normal(jax.random.fold_in(_rk, 13), (4, 77), jnp.float32)
        return (x, ctx_1024, condB_tau, fside_BxS2_0)
    x, ctx_1024, condB_tau, fside_BxS2_0 = _rec_inputs()

    def _L0_xcond_setup():
        import jax, jax.numpy as jnp
        import numpy as np
        B, S, D, H = (2, 1024, 512, 16)
        DK = D // H

        def _split_heads(x):
            b, s, _ = x.shape
            return x.reshape(b, s, H, DK).transpose(0, 2, 1, 3)
        key = jax.random.key(seed)
        ks = jax.random.split(key, 14)
        inp = {'query': jax.random.normal(ks[0], (B, S, D), jnp.float32), 'key': jax.random.normal(ks[1], (B, S, D), jnp.float32), 'value': jax.random.normal(ks[2], (B, S, D), jnp.float32), 'tau': jax.random.uniform(ks[3], (B, 1), jnp.float32, 0.5, 1.5), 'delta': jax.random.normal(ks[4], (B, S), jnp.float32)}
        sc = 1.0 / np.sqrt(D)
        for i, name in enumerate(['q', 'k', 'v', 'o']):
            inp[f'W{name}'] = jax.random.normal(ks[5 + 2 * i], (D, D), jnp.float32) * sc
            inp[f'b{name}'] = jax.random.normal(ks[6 + 2 * i], (D,), jnp.float32) * 0.01
        return inp
    _L0_xcond_all = _L0_xcond_setup()
    _L0_xcond_in = {k: v for k, v in _L0_xcond_all.items() if k in ('Wq', 'bq', 'Wk', 'bk', 'Wv', 'bv', 'Wo', 'bo')}
    del _L0_xcond_all

    def _L0_ffn_setup():
        import jax, jax.numpy as jnp
        import numpy as np
        D_MODEL = 512
        M = 64
        INNER = 16
        key = jax.random.key(seed)
        ks = jax.random.split(key, 9)

        def init(k, shape, fan_in):
            bound = 1.0 / np.sqrt(fan_in)
            return jax.random.uniform(k, shape, jnp.float32, -bound, bound)
        x = jax.random.normal(ks[0], (16, 2048, D_MODEL), dtype=jnp.float32)
        Win = init(ks[1], (D_MODEL, M), D_MODEL)
        bin_ = init(ks[2], (M,), D_MODEL)
        W1 = init(ks[3], (M, INNER), 1)
        b1 = init(ks[4], (M, INNER), 1)
        W2 = init(ks[5], (M, INNER), INNER)
        b2 = init(ks[6], (M,), INNER)
        Wout = init(ks[7], (M, D_MODEL), M)
        bout = init(ks[8], (D_MODEL,), M)
        return {'x': x, 'Win': Win, 'bin_': bin_, 'W1': W1, 'b1': b1, 'W2': W2, 'b2': b2, 'Wout': Wout, 'bout': bout}
    _L0_ffn_all = _L0_ffn_setup()
    _L0_ffn_in = {k: v for k, v in _L0_ffn_all.items() if k in ('Win', 'bin_', 'W1', 'b1', 'W2', 'b2', 'Wout', 'bout')}
    del _L0_ffn_all

    def _L1_xcond_setup():
        import jax, jax.numpy as jnp
        import numpy as np
        D_MODEL = 512
        N_HEADS = 16
        key = jax.random.key(seed)
        ks = jax.random.split(key, 16)
        B, L, S, D = (4, 1024, 1024, D_MODEL)
        inp = {'q': jax.random.normal(ks[0], (B, L, D), jnp.float32), 'k': jax.random.normal(ks[1], (B, S, D), jnp.float32), 'v': jax.random.normal(ks[2], (B, S, D), jnp.float32), 'tau': jax.random.uniform(ks[3], (B, 1), jnp.float32, 0.5, 1.5), 'delta': jax.random.normal(ks[4], (B, S), jnp.float32)}
        s = 1.0 / np.sqrt(D)
        inp['Wq'] = jax.random.normal(ks[5], (D, D), jnp.float32) * s
        inp['bq'] = jnp.zeros((D,), jnp.float32)
        inp['Wk'] = jax.random.normal(ks[6], (D, D), jnp.float32) * s
        inp['bk'] = jnp.zeros((D,), jnp.float32)
        inp['Wv'] = jax.random.normal(ks[7], (D, D), jnp.float32) * s
        inp['bv'] = jnp.zeros((D,), jnp.float32)
        inp['Wo'] = jax.random.normal(ks[8], (D, D), jnp.float32) * s
        inp['bo'] = jnp.zeros((D,), jnp.float32)
        return inp
    _L1_xcond_all = _L1_xcond_setup()
    _L1_xcond_in = {k: v for k, v in _L1_xcond_all.items() if k in ('Wq', 'bq', 'Wk', 'bk', 'Wv', 'bv', 'Wo', 'bo')}
    del _L1_xcond_all

    def _L1_ffn_setup():
        import jax, jax.numpy as jnp
        import numpy as np
        DIM = 512
        H = 8
        DH = 64
        W = 64
        NQ = 256
        NKV = 512
        EPS = 1.0
        NITERS = 50
        FETCH = 9.0 / 8.0
        SCALE = DH ** (-0.5)

        def _ln(x, w, b):
            m = x.mean(-1, keepdims=True)
            v = ((x - m) ** 2).mean(-1, keepdims=True)
            return (x - m) * jax.lax.rsqrt(v + 1e-05) * w + b

        def _rms(x, g):
            n = jnp.maximum(jnp.linalg.norm(x, axis=-1, keepdims=True), 1e-12)
            return x / n * np.sqrt(DIM).astype(np.float32) * g

        def local_attn(x, Wqkv, Wout):
            b, n, _ = x.shape
            nw = n // W
            qkv = x @ Wqkv.T
            q, k, v = jnp.split(qkv, 3, axis=-1)

            def towin(t):
                return t.reshape(b, nw, W, H, DH).transpose(0, 3, 1, 2, 4)
            q, k, v = map(towin, (q, k, v))

            def expand(t):
                tp = jnp.pad(t, ((0, 0), (0, 0), (1, 1), (0, 0), (0, 0)))
                return jnp.concatenate([tp[:, :, :-2], tp[:, :, 1:-1], tp[:, :, 2:]], axis=3)
            ke, ve = (expand(k), expand(v))
            sim = jnp.einsum('bhnid,bhnjd->bhnij', q, ke) * SCALE
            win = jnp.arange(nw)
            valid = jnp.concatenate([jnp.repeat((win > 0)[:, None], W, 1), jnp.ones((nw, W), bool), jnp.repeat((win < nw - 1)[:, None], W, 1)], axis=1)
            sim = jnp.where(valid[None, None, :, None, :], sim, -1000000000.0)
            attn = jax.nn.softmax(sim, axis=-1)
            o = jnp.einsum('bhnij,bhnjd->bhnid', attn, ve)
            o = o.transpose(0, 2, 3, 1, 4).reshape(b, n, H * DH)
            return o @ Wout.T

        def route(x, routing_token, num_tokens):
            s = jnp.einsum('bnd,rd->brn', x, routing_token).reshape(x.shape[0], x.shape[1])
            n = s.shape[-1]
            logk = jnp.log(jnp.asarray(min(num_tokens * FETCH, float(n)), s.dtype))

            def body(ab, _):
                a, bb = ab
                a = EPS * (logk - jax.nn.logsumexp((s + bb) / EPS, axis=-1, keepdims=True))
                bb = -jax.nn.relu(s + a)
                return ((a, bb), None)
            (a, bb), _ = jax.lax.scan(body, (jnp.zeros((s.shape[0], 1), s.dtype), -s), None, length=NITERS)
            scores = jnp.exp((s + a + bb) / EPS)
            sel_scores, sel_idx = jax.lax.top_k(scores, num_tokens)
            sel_scores = sel_scores + jax.lax.stop_gradient(1.0 - sel_scores)
            return (sel_scores, sel_idx)

        def heavy_attn(xq, ctx, scores_kv, gamma, Wq, Wkv, Wout, null_kv):
            b = xq.shape[0]
            xq = _rms(xq, gamma)
            ctx = _rms(ctx, gamma)
            q = (xq @ Wq.T).reshape(b, -1, H, DH).transpose(0, 2, 1, 3)
            kv = (ctx @ Wkv.T).reshape(b, -1, H, 2 * DH).transpose(0, 2, 1, 3)
            k, v = (kv[..., :DH], kv[..., DH:])
            v = v * scores_kv[:, None, :, None]
            nk = jnp.broadcast_to(null_kv[0][None, :, None, :], (b, H, 1, DH))
            nv = jnp.broadcast_to(null_kv[1][None, :, None, :], (b, H, 1, DH))
            k = jnp.concatenate([nk, k], axis=2)
            v = jnp.concatenate([nv, v], axis=2)
            sim = jnp.einsum('bhid,bhjd->bhij', q, k) * SCALE
            attn = jax.nn.softmax(sim, axis=-1)
            o = jnp.einsum('bhij,bhjd->bhid', attn, v)
            o = o.transpose(0, 2, 1, 3).reshape(b, -1, H * DH)
            return o @ Wout.T
        key = jax.random.key(seed)
        ks = jax.random.split(key, 12)
        D, IN = (DIM, H * DH)
        w = lambda k, shape: jax.random.normal(k, shape, jnp.float32) * 0.02
        return {'x': jax.random.normal(ks[0], (4, 2048, D), jnp.float32), 'ln_w': jnp.ones((D,), jnp.float32), 'ln_b': jnp.zeros((D,), jnp.float32), 'Wqkv': w(ks[1], (3 * IN, D)), 'Wout_l': w(ks[2], (D, IN)), 'rt_q': jax.random.normal(ks[3], (1, D), jnp.float32), 'rt_kv': jax.random.normal(ks[4], (1, D), jnp.float32), 'gamma': jnp.ones((D,), jnp.float32), 'Wq': w(ks[5], (IN, D)), 'Wkv': w(ks[6], (2 * IN, D)), 'Wout_h': w(ks[7], (D, IN)), 'null_kv': jax.random.normal(ks[8], (2, H, DH), jnp.float32), 'null_q': jax.random.normal(ks[9], (D,), jnp.float32)}
    _L1_ffn_all = _L1_ffn_setup()
    _L1_ffn_in = {k: v for k, v in _L1_ffn_all.items() if k in ('ln_w', 'ln_b', 'Wqkv', 'Wout_l', 'rt_q', 'rt_kv', 'gamma', 'Wq', 'Wkv', 'Wout_h', 'null_kv', 'null_q')}
    del _L1_ffn_all
    return {'x': x, 'ctx_1024': ctx_1024, 'condB_tau': condB_tau, 'fside_BxS2_0': fside_BxS2_0, 'L0_xcond_Wq': _L0_xcond_in['Wq'], 'L0_xcond_bq': _L0_xcond_in['bq'], 'L0_xcond_Wk': _L0_xcond_in['Wk'], 'L0_xcond_bk': _L0_xcond_in['bk'], 'L0_xcond_Wv': _L0_xcond_in['Wv'], 'L0_xcond_bv': _L0_xcond_in['bv'], 'L0_xcond_Wo': _L0_xcond_in['Wo'], 'L0_xcond_bo': _L0_xcond_in['bo'], 'L0_ffn_Win': _L0_ffn_in['Win'], 'L0_ffn_bin_': _L0_ffn_in['bin_'], 'L0_ffn_W1': _L0_ffn_in['W1'], 'L0_ffn_b1': _L0_ffn_in['b1'], 'L0_ffn_W2': _L0_ffn_in['W2'], 'L0_ffn_b2': _L0_ffn_in['b2'], 'L0_ffn_Wout': _L0_ffn_in['Wout'], 'L0_ffn_bout': _L0_ffn_in['bout'], 'L1_xcond_Wq': _L1_xcond_in['Wq'], 'L1_xcond_bq': _L1_xcond_in['bq'], 'L1_xcond_Wk': _L1_xcond_in['Wk'], 'L1_xcond_bk': _L1_xcond_in['bk'], 'L1_xcond_Wv': _L1_xcond_in['Wv'], 'L1_xcond_bv': _L1_xcond_in['bv'], 'L1_xcond_Wo': _L1_xcond_in['Wo'], 'L1_xcond_bo': _L1_xcond_in['bo'], 'L1_ffn_ln_w': _L1_ffn_in['ln_w'], 'L1_ffn_ln_b': _L1_ffn_in['ln_b'], 'L1_ffn_Wqkv': _L1_ffn_in['Wqkv'], 'L1_ffn_Wout_l': _L1_ffn_in['Wout_l'], 'L1_ffn_rt_q': _L1_ffn_in['rt_q'], 'L1_ffn_rt_kv': _L1_ffn_in['rt_kv'], 'L1_ffn_gamma': _L1_ffn_in['gamma'], 'L1_ffn_Wq': _L1_ffn_in['Wq'], 'L1_ffn_Wkv': _L1_ffn_in['Wkv'], 'L1_ffn_Wout_h': _L1_ffn_in['Wout_h'], 'L1_ffn_null_kv': _L1_ffn_in['null_kv'], 'L1_ffn_null_q': _L1_ffn_in['null_q']}

def reference(x, ctx_1024, condB_tau, fside_BxS2_0, L0_xcond_Wq, L0_xcond_bq, L0_xcond_Wk, L0_xcond_bk, L0_xcond_Wv, L0_xcond_bv, L0_xcond_Wo, L0_xcond_bo, L0_ffn_Win, L0_ffn_bin_, L0_ffn_W1, L0_ffn_b1, L0_ffn_W2, L0_ffn_b2, L0_ffn_Wout, L0_ffn_bout, L1_xcond_Wq, L1_xcond_bq, L1_xcond_Wk, L1_xcond_bk, L1_xcond_Wv, L1_xcond_bv, L1_xcond_Wo, L1_xcond_bo, L1_ffn_ln_w, L1_ffn_ln_b, L1_ffn_Wqkv, L1_ffn_Wout_l, L1_ffn_rt_q, L1_ffn_rt_kv, L1_ffn_gamma, L1_ffn_Wq, L1_ffn_Wkv, L1_ffn_Wout_h, L1_ffn_null_kv, L1_ffn_null_q):
    import jax
    import jax.numpy as jnp

    def _L0_xcond_ref(query, key, value, tau, delta, Wq, bq, Wk, bk, Wv, bv, Wo, bo):
        import jax, jax.numpy as jnp
        import numpy as np
        B, S, D, H = (2, 1024, 512, 16)
        DK = D // H

        def _split_heads(x):
            b, s, _ = x.shape
            return x.reshape(b, s, H, DK).transpose(0, 2, 1, 3)
        q = _split_heads(query @ Wq.T + bq)
        k = _split_heads(key @ Wk.T + bk)
        v = _split_heads(value @ Wv.T + bv)
        scores = jnp.einsum('bhqd,bhkd->bhqk', q, k)
        scores = scores * tau[:, :, None, None] + delta[:, None, None, :]
        scores = scores / jnp.sqrt(jnp.asarray(DK, scores.dtype))
        p_attn = jax.nn.softmax(scores, axis=-1)
        x = jnp.einsum('bhqk,bhkd->bhqd', p_attn, v)
        x = x.transpose(0, 2, 1, 3).reshape(query.shape[0], -1, H * DK)
        return x @ Wo.T + bo

    def _L0_ffn_ref(x, Win, bin_, W1, b1, W2, b2, Wout, bout):
        import jax, jax.numpy as jnp
        import numpy as np
        D_MODEL = 512
        M = 64
        INNER = 16
        s = jnp.einsum('btd,dm->btm', x, Win) + bin_
        h = jax.nn.relu(s[..., None] * W1 + b1)
        g = jnp.einsum('btmh,mh->btm', h, W2) + b2
        out = jnp.einsum('btm,md->btd', g, Wout) + bout
        return out

    def _L1_xcond_ref(q, k, v, tau, delta, Wq, bq, Wk, bk, Wv, bv, Wo, bo):
        import jax, jax.numpy as jnp
        import numpy as np
        D_MODEL = 512
        N_HEADS = 16
        B, L, D = q.shape
        S = k.shape[1]
        H = N_HEADS
        E = D // H
        qh = (q @ Wq.T + bq).reshape(B, L, H, E)
        kh = (k @ Wk.T + bk).reshape(B, S, H, E)
        vh = (v @ Wv.T + bv).reshape(B, S, H, E)
        scale = 1.0 / np.sqrt(E).astype(np.float32)
        scores = jnp.einsum('blhe,bshe->bhls', qh, kh)
        scores = scores * tau[:, None, None, :] + delta[:, None, None, :]
        a = jax.nn.softmax(scale * scores, axis=-1)
        out = jnp.einsum('bhls,bshd->blhd', a, vh).reshape(B, L, D)
        return out @ Wo.T + bo

    def _L1_ffn_ref(x, ln_w, ln_b, Wqkv, Wout_l, rt_q, rt_kv, gamma, Wq, Wkv, Wout_h, null_kv, null_q):
        import jax, jax.numpy as jnp
        import numpy as np
        DIM = 512
        H = 8
        DH = 64
        W = 64
        NQ = 256
        NKV = 512
        EPS = 1.0
        NITERS = 50
        FETCH = 9.0 / 8.0
        SCALE = DH ** (-0.5)

        def _ln(x, w, b):
            m = x.mean(-1, keepdims=True)
            v = ((x - m) ** 2).mean(-1, keepdims=True)
            return (x - m) * jax.lax.rsqrt(v + 1e-05) * w + b

        def _rms(x, g):
            n = jnp.maximum(jnp.linalg.norm(x, axis=-1, keepdims=True), 1e-12)
            return x / n * np.sqrt(DIM).astype(np.float32) * g

        def local_attn(x, Wqkv, Wout):
            b, n, _ = x.shape
            nw = n // W
            qkv = x @ Wqkv.T
            q, k, v = jnp.split(qkv, 3, axis=-1)

            def towin(t):
                return t.reshape(b, nw, W, H, DH).transpose(0, 3, 1, 2, 4)
            q, k, v = map(towin, (q, k, v))

            def expand(t):
                tp = jnp.pad(t, ((0, 0), (0, 0), (1, 1), (0, 0), (0, 0)))
                return jnp.concatenate([tp[:, :, :-2], tp[:, :, 1:-1], tp[:, :, 2:]], axis=3)
            ke, ve = (expand(k), expand(v))
            sim = jnp.einsum('bhnid,bhnjd->bhnij', q, ke) * SCALE
            win = jnp.arange(nw)
            valid = jnp.concatenate([jnp.repeat((win > 0)[:, None], W, 1), jnp.ones((nw, W), bool), jnp.repeat((win < nw - 1)[:, None], W, 1)], axis=1)
            sim = jnp.where(valid[None, None, :, None, :], sim, -1000000000.0)
            attn = jax.nn.softmax(sim, axis=-1)
            o = jnp.einsum('bhnij,bhnjd->bhnid', attn, ve)
            o = o.transpose(0, 2, 3, 1, 4).reshape(b, n, H * DH)
            return o @ Wout.T

        def route(x, routing_token, num_tokens):
            s = jnp.einsum('bnd,rd->brn', x, routing_token).reshape(x.shape[0], x.shape[1])
            n = s.shape[-1]
            logk = jnp.log(jnp.asarray(min(num_tokens * FETCH, float(n)), s.dtype))

            def body(ab, _):
                a, bb = ab
                a = EPS * (logk - jax.nn.logsumexp((s + bb) / EPS, axis=-1, keepdims=True))
                bb = -jax.nn.relu(s + a)
                return ((a, bb), None)
            (a, bb), _ = jax.lax.scan(body, (jnp.zeros((s.shape[0], 1), s.dtype), -s), None, length=NITERS)
            scores = jnp.exp((s + a + bb) / EPS)
            sel_scores, sel_idx = jax.lax.top_k(scores, num_tokens)
            sel_scores = sel_scores + jax.lax.stop_gradient(1.0 - sel_scores)
            return (sel_scores, sel_idx)

        def heavy_attn(xq, ctx, scores_kv, gamma, Wq, Wkv, Wout, null_kv):
            b = xq.shape[0]
            xq = _rms(xq, gamma)
            ctx = _rms(ctx, gamma)
            q = (xq @ Wq.T).reshape(b, -1, H, DH).transpose(0, 2, 1, 3)
            kv = (ctx @ Wkv.T).reshape(b, -1, H, 2 * DH).transpose(0, 2, 1, 3)
            k, v = (kv[..., :DH], kv[..., DH:])
            v = v * scores_kv[:, None, :, None]
            nk = jnp.broadcast_to(null_kv[0][None, :, None, :], (b, H, 1, DH))
            nv = jnp.broadcast_to(null_kv[1][None, :, None, :], (b, H, 1, DH))
            k = jnp.concatenate([nk, k], axis=2)
            v = jnp.concatenate([nv, v], axis=2)
            sim = jnp.einsum('bhid,bhjd->bhij', q, k) * SCALE
            attn = jax.nn.softmax(sim, axis=-1)
            o = jnp.einsum('bhij,bhjd->bhid', attn, v)
            o = o.transpose(0, 2, 1, 3).reshape(b, -1, H * DH)
            return o @ Wout.T
        b, n, d = x.shape
        light = local_attn(_ln(x, ln_w, ln_b), Wqkv, Wout_l)
        sq, iq = route(x, rt_q, NQ)
        skv, ikv = route(x, rt_kv, NKV)
        br = jnp.arange(b)[:, None]
        xq = x[br, iq]
        xkv = x[br, ikv]
        heavy = heavy_attn(xq, xkv, skv, gamma, Wq, Wkv, Wout_h, null_kv)
        heavy = heavy * sq[..., None]
        out = jnp.broadcast_to(null_q[None, None, :], (b, n, d))
        out = out.at[br, iq].set(heavy)
        return out + light
    x = x + _L0_xcond_ref(_layernorm(x, axis=-1), ctx_1024, ctx_1024, condB_tau[:, None], fside_BxS2_0, L0_xcond_Wq, L0_xcond_bq, L0_xcond_Wk, L0_xcond_bk, L0_xcond_Wv, L0_xcond_bv, L0_xcond_Wo, L0_xcond_bo)
    x = x + _L0_ffn_ref(_layernorm(x, axis=-1), L0_ffn_Win, L0_ffn_bin_, L0_ffn_W1, L0_ffn_b1, L0_ffn_W2, L0_ffn_b2, L0_ffn_Wout, L0_ffn_bout)
    x = x + _L1_xcond_ref(_layernorm(x, axis=-1), ctx_1024, ctx_1024, condB_tau[:, None], fside_BxS2_0, L1_xcond_Wq, L1_xcond_bq, L1_xcond_Wk, L1_xcond_bk, L1_xcond_Wv, L1_xcond_bv, L1_xcond_Wo, L1_xcond_bo)
    x = x + _L1_ffn_ref(_layernorm(x, axis=-1), L1_ffn_ln_w, L1_ffn_ln_b, L1_ffn_Wqkv, L1_ffn_Wout_l, L1_ffn_rt_q, L1_ffn_rt_kv, L1_ffn_gamma, L1_ffn_Wq, L1_ffn_Wkv, L1_ffn_Wout_h, L1_ffn_null_kv, L1_ffn_null_q)
    return x

_drawn_inputs = setup_inputs


def setup_inputs(seed=0):
    import zlib

    import numpy as np

    out = dict(_drawn_inputs(seed))
    spreads = {'L1_xcond_bq': (0.0, 0.37),
     'L1_xcond_bk': (0.0, 0.8),
     'L1_xcond_bv': (0.0, 0.1),
     'L1_xcond_bo': (0.0, 0.1),
     'L1_ffn_ln_w': (1.0, 0.6),
     'L1_ffn_ln_b': (0.0, 0.637),
     'L1_ffn_gamma': (1.0, 0.6)}
    factors = {'L0_xcond_bq': 5.769,
     'L0_xcond_bk': 8.0,
     'L0_xcond_bv': 4.784,
     'L0_xcond_bo': 6.069,
     'L0_ffn_bin_': 3.637,
     'L1_ffn_rt_kv': 8.0,
     'L1_ffn_Wq': 8.0,
     'L1_ffn_null_kv': 8.0}
    for name, (base, spread) in spreads.items():
        noise = np.random.default_rng([zlib.crc32(name.encode()), seed]).standard_normal(out[name].shape)
        drawn = base * np.exp(spread * noise) if base else spread * noise
        out[name] = jnp.asarray(drawn.astype(out[name].dtype))
    for name, factor in factors.items():
        out[name] = (out[name] * factor).astype(out[name].dtype)
    return out
```

```python
import math
from collections import deque
from contextlib import ExitStack

import concourse.bass as bass
from concourse import mybir

ALU = mybir.AluOpType
ACT = mybir.ActivationFunctionType
X = mybir.AxisListType.X
F = mybir.dt.float32
I32 = mybir.dt.int32

B, S, D = 4, 2048, 512
NK = 77
NQ, NKV = 256, 512
NT = B * S // 128
NB = NT // 4
ITERS = 50
OFF3 = (0, 103, 205)
SEGS = ((0, 0, 0, 77, 0, 0), (0, 1, 0, 26, 77, 33),
        (1, 1, 26, 51, 0, 0), (1, 2, 0, 52, 51, 33),
        (2, 2, 52, 25, 1, 0), (2, 3, 0, 77, 26, 33))
LOGK = (math.log(NQ * 9.0 / 8.0), math.log(NKV * 9.0 / 8.0))


class Flow:

    def __init__(self, nc, stack):
        self.nc, self.stack = nc, stack
        self.sem, self.val, self.seen = {}, {}, {}

    def tick(self, ins, name, by=1):
        if name not in self.sem:
            self.sem[name] = self.stack.enter_context(self.nc.semaphore(name))
            self.val[name] = 0
        ins.then_inc(self.sem[name], by)
        self.val[name] += by
        return (name, self.val[name])

    def need(self, eng, *tokens):
        for t in tokens:
            if t is None:
                continue
            if isinstance(t, list):
                self.need(eng, *t)
                continue
            name, v = t
            key = (str(eng.engine), name)
            if self.seen.get(key, 0) < v:
                eng.wait_ge(self.sem[name], v)
                self.seen[key] = v

    def all(self):
        return list(self.val.items())


class Slots:

    def __init__(self, n):
        self.n, self.i, self.free = n, 0, [[] for _ in range(n)]

    def take(self):
        k = self.i % self.n
        self.i += 1
        toks, self.free[k] = self.free[k], None
        assert toks is not None, "taken before it was given back"
        return k, toks

    def give(self, k, *toks):
        self.free[k] = (self.free[k] or []) + list(toks)


class Later:

    def __init__(self):
        self.q = deque()

    def add(self, gen):
        self.q.append(gen)
        return gen

    def piece(self, n=1):
        for _ in range(n):
            while self.q:
                try:
                    next(self.q[0])
                    break
                except StopIteration:
                    self.q.popleft()

    def finish(self, gen):
        while gen in self.q:
            self.piece()

    def drain(self):
        while self.q:
            for _ in self.q[0]:
                pass
            self.q.popleft()


def last(ap, n):
    return ap.unsqueeze(2).broadcast_to([ap.shape[0], ap.shape[1], n])


def mid(ap, n):
    return ap.unsqueeze(1).broadcast_to([ap.shape[0], n, ap.shape[1]])


def build(nc, a, out, parts="ABC"):
    PE, V, A, G, SY = nc.tensor, nc.vector, nc.scalar, nc.gpsimd, nc.sync
    with ExitStack() as top:
        fl = Flow(nc, top)
        tick, need = fl.tick, fl.need

        def dram(name, shape):
            return nc.dram_tensor(name, shape, F, kind="Internal").ap()

        X3d = dram("x3_scratch", (B * S, D))
        Yd = dram("y_scratch", (B * S, D))
        Vd = dram("v_scratch", (2, B, 16, NK, 33))
        cumd = dram("cum_scratch", (8, S))
        fd = dram("f_scratch", (2 * B * S, 1))

        def alloc(stack):
            return lambda name, shape, dt=F: stack.enter_context(nc.sbuf_tensor(name, shape, dt))

        def load(dst, src, name, eng=SY):
            return tick(eng.dma_start(dst, src), name, 16)

        sb = alloc(top)
        psS = top.enter_context(nc.psum_tensor("psS", [128, 4, 512], F))
        psT = top.enter_context(nc.psum_tensor("psT", [128, 2, 512], F))
        psM = top.enter_context(nc.psum_tensor("psM", [128, 2, 512], F))
        Ts, Ms = Slots(2), Slots(2)

        ident = sb("ident", [128, 128])
        grp = sb("grp", [128, 128])
        tri = sb("tri", [128, 128])
        mhalf = sb("mhalf", [128, 8])
        cols = sb("cols", [128, 16])
        scol = sb("scol", [128, 2, NT])
        mvx = sb("mvx", [128, NT, 2])
        rsx = sb("rsx", [128, NT])
        t_ident = load(ident[:, :], a["c_ident"], "ld.ident")
        t_mhalf = tick(G.memset(mhalf[:, :], -0.5), "g.mhalf")
        s_tok = []

        idx = sb("idx", [128, 24], I32)
        idxs = sb("idxs", [128, 24], I32)
        st = sb("st", [128, 2, 4, 6])
        mv = sb("mv", [128, 2, 4, 2])
        ve = sb("ve", [128, 2, 4])
        rs = sb("rs", [128, 2, 4])
        Ln = Slots(2)
        xn = sb("xn", [128, 2, D])
        Xn = Slots(2)
        On = sb("On", [128, 2, D])
        Ons = Slots(2)
        OT = sb("OT", [128, 2, 4, 128])
        OTs = Slots(2)
        rc = sb("rc", [128, 2, 8])
        Rc = Slots(2)

        def ln_stats(tiles, ready):
            k, w = Ln.take()
            need(V, w)
            for t in range(4):
                need(V, ready(t))
                tok = tick(V.bn_stats(st[:, k, t, :], tiles(t)), "v.bnstats")
            yield
            need(V, tok)
            for t in range(4):
                tok = tick(V.bn_aggr(mv[:, k, t, :], st[:, k, t, :]), "v.bnaggr")
            need(V, tok)
            tok = tick(V.tensor_scalar(ve[:, k, :], mv[:, k, :, 1], 1e-5, None, ALU.add), "v.vareps")
            need(G, tok, t_mhalf)
            tok = tick(G.tensor_tensor(rs[:, k, :], ve[:, k, :], mhalf[:, 0:4], ALU.pow), "g.rstd")
            yield
            return k, tok

        def ln_apply(k, t, x, t_rs, t_x):
            kx, w = Xn.take()
            need(V, w, t_rs, t_x)
            tok = tick(V.tensor_scalar(xn[:, kx, :], x, mv[:, k, t, 0:1], rs[:, k, t:t + 1],
                                       ALU.subtract, ALU.mult), "v.lnapply")
            if t == 3:
                Ln.give(k, tok)
            return kx, tok

        def turn4(src, t_src, give, dst, w_dst, name):
            kt, w = Ts.take()
            need(PE, w, t_src, t_ident)
            for c in range(4):
                m = PE.transpose(psT[:, kt, 128 * c:128 * c + 128], src[:, 128 * c:128 * c + 128], ident[:, :])
            tok = tick(m, "pe." + name)
            give(tok)
            need(A, tok, w_dst)
            te = tick(A.copy(dst, psT[:, kt, :].rearrange("p (c n) -> p c n", c=4)), "a." + name)
            Ts.give(kt, te)
            return te

        def mms(outp, pairs, w):
            need(PE, w)
            for i, (l, r) in enumerate(pairs):
                m = PE.matmul(outp, l, r, start=(i == 0), stop=(i == len(pairs) - 1))
            return m

        with ExitStack() as pa:
            sb = alloc(pa)
            Wq = [sb(f"Wq{L}", [128, 4, D]) for L in (0, 1)]
            Wo = [sb(f"Wo{L}", [128, 4, D]) for L in (0, 1)]
            bq = sb("bq", [128, 2, 4])
            bo = [sb(f"bo{L}", [128, D]) for L in (0, 1)]
            cF = sb("cF", [128, D])
            rt = sb("rt", [128, 2, D])
            KT = [sb(f"KT{L}", [128, 4, B * NK]) for L in (0, 1)]
            KB = [[sb(f"KB{L}{s}", [128, 4, 4 * NK]) for s in (0, 1)] for L in (0, 1)]
            VB = [[sb(f"VB{L}{s}", [103, 4, 3, 66]) for s in (0, 1)] for L in (0, 1)]
            Win = sb("Win", [128, 4, 128])
            Wout = sb("Wout", [128, D])
            fcol = sb("fcol", [128, 32])
            dlt = sb("dlt", [128, B, NK])
            XB = sb("XB", [128, 4, 4, D])
            xT = sb("xT", [128, 2, 4, D])
            QT = sb("QT", [128, 2, 4, D])
            Sb = sb("Sb", [128, 2, 16 * NK])
            PT = sb("PT", [103, 12, 128])
            mx = sb("mx", [128, 2, 16])
            sT = sb("sT", [128, 2, D])
            hh = sb("hh", [128, 2, D])
            acc = sb("acc", [128, D])
            junk = sb("junk", [128, D])
            zx = sb("zx", [128, D])
            sx = sb("sx", [128, 6])
            vx = sb("vx", [128, NT])
            XTs, QTs, Ss, STs, Hs, SPs = Slots(2), Slots(2), Slots(2), Slots(2), Slots(2), Slots(4)
            free = {"acc": [], "PT": [], "x": {}}

            t_w = {}
            for L in (0, 1):
                load(Wq[L][:, :, :], a[f"wq{L}"], f"ld.w{L}")
                load(Wo[L][:, :, :], a[f"wo{L}"], f"ld.w{L}")
                t_w[L] = load(bo[L][:, :], a[f"bo{L}"], f"ld.w{L}")
            load(bq[:, :, :], a["bq"], "ld.small")
            load(dlt[:, :, :], a["delta"], "ld.small")
            load(rt[:, :, :], a["rt"], "ld.small")
            load(Win[:, :, :], a["win"], "ld.small")
            load(Wout[:, :], a["wout"], "ld.small")
            load(fcol[:, :], a["fcol"], "ld.small")
            load(cF[:, :], a["bout"], "ld.small")
            t_small = load(cols[:, :], a["cols"], "ld.small")
            xin = a["x"].rearrange("(n t p) d -> n p t d", t=4, p=128)

            def load_x(blk):
                need(SY, free["x"].get(blk - 4))
                return load(XB[:, blk % 4, :, :], xin[blk], f"ld.x{blk % 4}")

            t_x = {0: load_x(0), 1: load_x(1)}

            ctxT = XB[:, 2, :, 0:B * NK]
            wk = xT[:, 0, :, :]
            wv = xT[:, 1, :, :]
            stage = sb("vstage", [NK, 16, 33])
            cc = XB[:, 3, :, :]
            t_c = load(ctxT, a["ctxT"], "ld.ctx")
            load(cc[0:NK, 0, :], a["bv0"], "ld.ctx")
            load(cc[0:NK, 1, :], a["bv1"], "ld.ctx")
            t_c = load(cc[:, 2, 0:16], a["kcol"], "ld.ctx")
            kc = cc[:, 2, 0:16]
            t_zero = []
            for L in (0, 1):
                for s in (0, 1):
                    t_zero.append(tick(V.memset(KB[L][s][:, :, :], 0.0), "v.zero"))
                    t_zero.append(tick(V.memset(VB[L][s][:, :, :, :], 0.0), "v.zero"))
            t_one = tick(V.memset(stage[:, :, :], 1.0), "v.one")
            need(V, t_small, t_c)
            t_d = tick(V.tensor_scalar(dlt[:, :, :], dlt[:, :, :], 1.0 / math.sqrt(32.0), None, ALU.mult), "v.setup")
            t_t = tick(V.tensor_scalar(cc[:, 2, 16:20], kc[:, 8:12], 1.0 / math.sqrt(32.0), None, ALU.mult), "v.setup")
            tau = cc[:, 2, 16:20]
            b1e = cc[:, 2, 32:40]
            t_f = tick(V.scalar_tensor_tensor(b1e, fcol[:, 0:8], fcol[:, 24:25], fcol[:, 8:16],
                                              ALU.mult, ALU.add), "v.setup")
            need(V, t_f)
            t_f = tick(V.tensor_copy(fcol[:, 8:16], b1e), "v.setup")
            t_b = tick(V.tensor_copy(cc[0:64, 2, 128:256], fcol[0:64, 25:26].broadcast_to([64, 128])), "v.setup")
            km, w = Ms.take()
            need(PE, t_b, t_small)
            tok = tick(mms(psM[:, km, :], [(cc[0:64, 2, 128:256], Wout[0:64, :])], w), "pe.setup")
            need(V, tok)
            t_cF = tick(V.tensor_tensor(cF[:, :], psM[:, km, :], cF[:, :], ALU.add), "v.setup")
            Ms.give(km, t_cF)
            t_KT, t_V, f_k, f_v, f_stage = {}, {}, [], [], [t_one]
            for L in (0, 1):
                need(SY, f_k)
                t_wk = load(wk, a[f"wk{L}"], "ld.wk")
                need(SY, f_v)
                t_wv = load(wv, a[f"wv{L}"], "ld.wv")
                for c in range(4):
                    km, w = Ms.take()
                    need(PE, t_wk, t_c)
                    tok = tick(mms(psM[:, km, 0:B * NK], [(wk[:, k, 128 * c:128 * c + 128], ctxT[:, k, :])
                                                          for k in range(4)], w), "pe.setup")
                    need(V, tok, t_t)
                    for b in range(B):
                        tok2 = tick(V.tensor_scalar(KT[L][:, c, NK * b:NK * b + NK], psM[:, km, NK * b:NK * b + NK],
                                                    kc[:, 4 * L + c:4 * L + c + 1], tau[:, b:b + 1],
                                                    ALU.add, ALU.mult), "v.KT")
                    Ms.give(km, tok2)
                f_k = [tok]
                t_KT[L] = tok2
                for b in range(B):
                    km, w = Ms.take()
                    need(PE, t_wv)
                    tok = tick(mms(psM[0:NK, km, :], [(ctxT[:, k, NK * b:NK * b + NK], wv[:, k, :])
                                                      for k in range(4)], w), "pe.setup")
                    need(V, tok, f_stage)
                    tok2 = tick(V.tensor_tensor(stage[:, :, 0:32],
                                                psM[0:NK, km, :].rearrange("p (h d) -> p h d", h=16),
                                                cc[0:NK, L, :].rearrange("p (h d) -> p h d", h=16), ALU.add), "v.V")
                    Ms.give(km, tok2)
                    need(SY, tok2)
                    tok2 = tick(SY.dma_start(Vd[L, b].rearrange("h k e -> k h e"), stage[:, :, :]), "st.V", 16)
                    f_stage = [tok2]
                    need(V, tok2)
                    t_V[L] = tok2
                f_v = [tok]
            for i in (-2, -1):
                free["x"][i] = fl.all()
            for i in (0, 1):
                XTs.give(i, f_k + f_v)

            KVs = {0: Slots(2), 1: Slots(2)}
            kv = {}

            def load_kv(L, b):
                k, w = KVs[L].take()
                need(V, w, t_zero, t_KT[L])
                for i in range(4):
                    tk = tick(V.tensor_copy(KB[L][k][32 * i:32 * i + 32, :, NK * i:NK * i + NK],
                                            KT[L][32 * i:32 * i + 32, :, NK * b:NK * b + NK]), f"v.KB{L}")
                yield
                need(SY, w, t_zero, t_V[L])
                for c, i, k0, n, r0, c0 in SEGS:
                    tv = load(VB[L][k][r0:r0 + n, :, c, c0:c0 + 33],
                              Vd[L, b].rearrange("(g i) k e -> i k g e", i=4)[i, k0:k0 + n], f"ld.VB{L}")
                kv[L, b] = (k, tk, tv)
                yield

            class Blk:
                pass

            blks = {}

            def prep(blk, L, row, t_row, proj):
                bk = blks[blk]
                xb = XB[:, blk % 4, :, :]
                k, t_rs = yield from ln_stats(lambda t: xb[:, t, :], lambda t: bk.ready[t])
                kx, w = XTs.take()
                te = []
                ready = []
                for t in range(4):
                    kn, tn = ln_apply(k, t, xb[:, t, :], t_rs, bk.ready[t])
                    need(G, tn, t_row)
                    ready.append(tick(G.tensor_tensor(xb[:, t, :], xb[:, t, :], row, ALU.add), "g.bias"))
                    te.append(turn4(xn[:, kn, :], tn, lambda tok, kn=kn: Xn.give(kn, tok),
                                    xT[:, kx, :, 128 * t:128 * t + 128], w, "xT"))
                    yield
                bk.ready = ready
                yield from proj(bk, kx, te[-1])

            def qproj(L):
                def go(bk, kx, te):
                    kq, wq_ = QTs.take()
                    for c in range(4):
                        km, w = Ms.take()
                        need(PE, te, t_w[L])
                        tok = tick(mms(psM[:, km, :], [(Wq[L][:, k, 128 * c:128 * c + 128], xT[:, kx, k, :])
                                                       for k in range(4)], w), "pe.Q")
                        need(A, tok, wq_, t_small)
                        tq = tick(A.activation(QT[:, kq, c, :], psM[:, km, :], ACT.Identity, bias=bq[:, L, c:c + 1]), "a.Q")
                        Ms.give(km, tq)
                        yield
                    XTs.give(kx, tok)
                    bk.q = (kq, tq)
                return go

            def ffn(bk, kx, te):
                ks, w1 = STs.take()
                km, w = Ms.take()
                need(PE, te, t_small)
                tok = tick(mms(psM[:, km, :], [(Win[:, k, :], xT[:, kx, k, :]) for k in range(4)], w), "pe.win")
                XTs.give(kx, tok)
                need(A, tok, w1)
                ts = tick(A.copy(sT[:, ks, :], psM[:, km, :]), "a.sT")
                Ms.give(km, ts)
                yield
                need(A, ts, t_f)
                need(V, free["acc"])
                for j in range(8):
                    kh, w = Hs.take()
                    need(A, w)
                    th = tick(A.activation(hh[:, kh, :], sT[:, ks, :], ACT.Relu, bias=fcol[:, 8 + j:9 + j],
                                           scale=fcol[:, j:j + 1]), "a.relu")
                    need(V, th)
                    if j == 0:
                        ta = tick(V.tensor_scalar(acc[:, :], hh[:, kh, :], fcol[:, 16:17], None, ALU.mult), "v.acc")
                    else:
                        need(V, ta)
                        ta = tick(V.scalar_tensor_tensor(acc[:, :], hh[:, kh, :], fcol[:, 16 + j:17 + j], acc[:, :],
                                                         ALU.mult, ALU.add), "v.acc")
                    Hs.give(kh, ta)
                    if j % 2:
                        yield
                STs.give(ks, th)
                for t in range(4):
                    km, w = Ms.take()
                    need(PE, ta)
                    tok = tick(mms(psM[:, km, :], [(acc[:, 128 * t:128 * t + 128], Wout[:, :])], w), "pe.wout")
                    need(V, tok, bk.ready[t])
                    x = XB[:, bk.i % 4, t, :]
                    bk.ready[t] = tick(V.tensor_tensor(x, psM[:, km, :], x, ALU.add), "v.x")
                    Ms.give(km, bk.ready[t])
                    yield
                free["acc"] = [tok]

            class Tile:
                pass

            def scores(t):
                L, bk, b = t.L, t.bk, t.b
                if t.tl == 0:
                    need(PE, bk.q[1])
                kb, tk, tv = kv[L, b]
                t.s, w_s = Ss.take()
                kq = bk.q[0]
                for g in range(4):
                    kp, w = SPs.take()
                    need(PE, tk)
                    t.tq = tick(mms(psS[:, kp, 0:308], [(QT[:, kq, g, 128 * t.tl:128 * t.tl + 128],
                                                         KB[L][kb][:, g, :])], w), "pe.S")
                    need(V, t.tq, w_s, t_d)
                    tok = tick(V.tensor_tensor(Sb[:, t.s, 308 * g:308 * g + 308].rearrange("p (i k) -> p i k", i=4),
                                               psS[:, kp, 0:308].rearrange("p (i k) -> p i k", i=4),
                                               mid(dlt[:, b, :], 4), ALU.add), "v.Sadd")
                    SPs.give(kp, tok)
                if t.tl == 3:
                    QTs.give(kq, t.tq)
                sv = Sb[:, t.s, :].rearrange("p (h k) -> p h k", h=16)
                need(V, tok)
                tok = tick(V.tensor_reduce(mx[:, t.s, :], sv, X, ALU.max), "v.max")
                need(G, tok)
                t.sub = tick(G.tensor_tensor(sv, sv, last(mx[:, t.s, :], NK), ALU.subtract), "g.sub")

            def softexp(t):
                need(A, t.sub)
                t.exp = tick(A.activation(Sb[:, t.s, :], Sb[:, t.s, :], ACT.Exp), "a.exp")

            def ptrans(t, g):
                kt, w = Ts.take()
                need(PE, w, t.exp)
                for c in range(3):
                    o = 308 * g + OFF3[c]
                    m = PE.transpose(psT[0:103, kt, 128 * c:128 * c + 128], Sb[:, t.s, o:o + 103], ident[:, :])
                tok = tick(m, "pe.PT")
                if g == 3:
                    Ss.give(t.s, tok)
                need(A, tok, free["PT"])
                t.pt = tick(A.copy(PT[:, 3 * g:3 * g + 3, :],
                                   psT[0:103, kt, 0:384].rearrange("p (c n) -> p c n", c=3)), "a.PT")
                Ts.give(kt, t.pt)

            def pv(t):
                kb, tk, tv = kv[t.L, t.b]
                t.o, w_o = Ons.take()
                for hf in range(2):
                    km, w = Ms.take()
                    need(PE, w, t.pt, tv)
                    for j in range(2):
                        g = 2 * hf + j
                        for c in range(3):
                            o = 132 * j + 33 * c
                            m = PE.matmul(psM[:, km, o:o + 66], PT[:, 3 * g + c, :], VB[t.L][kb][:, g, c, :],
                                          start=(j == 0 and c == 0), stop=(j == 1 and c == 2), skip_group_check=True)
                    tok = tick(m, "pe.PV")
                    ov = psM[:, km, 0:264].rearrange("p (h e) -> p h e", e=33)
                    kr, wr = Rc.take()
                    need(V, tok, w_o, wr)
                    tr = tick(V.reciprocal(rc[:, kr, :], ov[:, :, 32]), "v.rc")
                    need(V, tr)
                    t.on = tick(V.tensor_tensor(On[:, t.o, 256 * hf:256 * hf + 256].rearrange("p (h d) -> p h d", h=8),
                                                ov[:, :, 0:32], last(rc[:, kr, :], 32), ALU.mult), "v.On")
                    Rc.give(kr, t.on)
                    Ms.give(km, t.on)
                free["PT"] = [tok]
                if t.lastkv:
                    KVs[t.L].give(kb, tok, t.tq)

            def otrans(t):
                t.ot, w = OTs.take()
                t.te = turn4(On[:, t.o, :], t.on, lambda tok: Ons.give(t.o, tok), OT[:, t.ot, :, :], w, "OT")

            def wo(t):
                km, w = Ms.take()
                need(PE, t.te, t_w[t.L])
                tok = tick(mms(psM[:, km, :], [(OT[:, t.ot, c, :], Wo[t.L][:, c, :]) for c in range(4)], w), "pe.Wo")
                OTs.give(t.ot, tok)
                bk = t.bk
                x = XB[:, bk.i % 4, t.tl, :]
                need(V, tok, bk.ready[t.tl])
                tx = tick(V.tensor_tensor(x, psM[:, km, :], x, ALU.add), "v.x")
                Ms.give(km, tx)
                if t.L == 0:
                    bk.new[t.tl] = tx
                    if t.tl == 3:
                        bk.ready = bk.new
                    return
                n = 4 * bk.i + t.tl
                need(SY, tx, x3_tok.get(n - 8))
                x3_tok[n] = tick(SY.dma_start(X3d[128 * n:128 * n + 128, :], x), f"st.x3{n % 8}", 16)
                need(V, tx, free.get("sx"))
                tok = tick(V.bn_stats(sx[:, :], x), "v.sx")
                need(V, tok)
                tok = tick(V.bn_aggr(mvx[:, n, :], sx[:, :]), "v.sx")
                need(V, tok)
                tok = tick(V.tensor_scalar(vx[:, n:n + 1], mvx[:, n, 1:2], 1e-5, None, ALU.add), "v.sx")
                free["sx"] = [tok]
                need(G, tok, t_mhalf)
                t.rx = tick(G.tensor_tensor(rsx[:, n:n + 1], vx[:, n:n + 1], mhalf[:, 0:1], ALU.pow), "g.rx")

            def route_scores(t):
                if t.L == 0:
                    return
                n = 4 * t.bk.i + t.tl
                x = XB[:, t.bk.i % 4, t.tl, :]
                need(V, t.rx, free.get("junk"))
                ts = tick(V.tensor_scalar(zx[:, :], x, mvx[:, n, 0:1], rsx[:, n:n + 1], ALU.subtract, ALU.mult), "v.s")
                for r in range(2):
                    need(V, ts)
                    ts = tick(V.tensor_tensor_reduce(junk[:, :], zx[:, :], rt[:, r, :], 1.0, 0.0, ALU.mult, ALU.add,
                                                     scol[:, r, n:n + 1]), "v.s")
                free["junk"] = [ts]
                s_tok[:] = [ts]
                free["x"].setdefault(t.bk.i, []).extend([x3_tok[n], ts])

            x3_tok = {}
            units = [(0, 0), (0, 1)]
            for i in range(NB):
                units.append((1, i))
                if i + 2 < NB:
                    units.append((0, i + 2))
            for i in range(NB):
                blks[i] = Blk()
                blks[i].i, blks[i].new = i, [None] * 4
            seq = []
            for L, i in units:
                for tl in range(4):
                    t = Tile()
                    t.L, t.bk, t.tl, t.b = L, blks[i], tl, i // 4
                    t.lastkv = tl == 3 and i % 4 == 3
                    seq.append(t)
            bg = Later()
            made = {}

            def queue_first(i):
                if i % 4 == 0:
                    bg.add(load_kv(0, i // 4))
                blks[i].ready = [t_x[i]] * 4
                if 2 <= i + 1 < NB:
                    t_x[i + 1] = load_x(i + 1)
                made[0, i] = bg.add(prep(i, 0, bo[0][:, :], t_w[0], qproj(0)))

            def queue_second(i):
                if i % 4 == 0:
                    bg.add(load_kv(1, i // 4))
                bg.add(prep(i, 0, cF[:, :], t_cF, ffn))
                made[1, i] = bg.add(prep(i, 1, bo[1][:, :], t_w[1], qproj(1)))

            queue_first(0)
            for n in range(len(seq) + 3):
                cur = seq[n] if n < len(seq) else None
                p1 = seq[n - 1] if 1 <= n <= len(seq) else None
                p2 = seq[n - 2] if 2 <= n < len(seq) + 2 else None
                if n >= 3:
                    route_scores(seq[n - 3])
                if cur is not None:
                    if cur.tl == 0:
                        bg.finish(made[cur.L, cur.bk.i])
                        if n // 4 + 1 < len(units) and units[n // 4 + 1][0] == 0:
                            queue_first(units[n // 4 + 1][1])
                    scores(cur)
                if p2 is not None:
                    otrans(p2)
                bg.piece()
                if p1 is not None:
                    ptrans(p1, 0)
                    ptrans(p1, 1)
                bg.piece()
                if p1 is not None:
                    ptrans(p1, 2)
                    ptrans(p1, 3)
                bg.piece()
                if p2 is not None:
                    wo(p2)
                    if p2.L == 0 and p2.tl == 3:
                        queue_second(p2.bk.i)
                bg.piece()
                if p1 is not None:
                    pv(p1)
                if cur is not None:
                    softexp(cur)
                bg.piece()
            bg.drain()
            done = fl.all()
        for e in (PE, V, A, G, SY):
            need(e, done)
        if "B" not in parts:
            return
        with ExitStack() as pb:
            sb = alloc(pb)
            Wl = sb("Wl", [128, 4, 3 * D])
            Wlo = sb("Wlo", [128, 4, D])
            bl = sb("bl", [128, 8])
            bvl = sb("bvl", [128, D])
            msk = sb("msk", [128, 3, 256])
            nulq = sb("nulq", [128, D])
            lnwb = sb("lnwb", [128, 8])
            XL = sb("XL", [128, 13, D])
            xU = sb("xU", [128, 4, 576])
            QU = sb("QU", [128, 3, 4, D])
            KU = sb("KU", [128, 3, 4, 640])
            VU = sb("VU", [128, 12, 8, 65])
            Sw = sb("Sw", [128, 2, 2048])
            PU = sb("PU", [128, 16, 128])
            mw = sb("mw", [128, 2, 8])
            yo = sb("yo", [128, 2, D])
            sr = sb("sr", [128, 128])
            zr = sb("zr", [128, 128])
            er = sb("er", [128, 128])
            rcol = sb("rcol", [128, 16])
            comb = sb("comb", [128, NT])
            idxf = sb("idxf", [128, 24])
            cb = sb("cb", [128, S])
            junk2 = sb("junk2", [128, S], mybir.dt.uint8)
            QUs, KUs, VUs, Sws, SPs, Yos = Slots(3), Slots(3), Slots(12), Slots(2), Slots(2), Slots(2)
            free = {"PU": []}

            load(Wl[:, :, :], a["wqkv"], "ld.wl")
            load(lnwb[:, :], a["lnwb"], "ld.wl")
            t_wl = load(grp[:, :], a["c_grp"], "ld.wl")
            load(Wlo[:, :, :], a["wlo"], "ld.wl2")
            load(msk[:, :, :], a["c_mask"], "ld.wl2")
            load(tri[:, :], a["c_tri"], "ld.wl2")
            t_wl2 = load(nulq[:, :], a["nulq"], "ld.wl2")
            xt = {}
            xlfree = {}

            def load_xl(n):
                k = n % 13
                need(SY, xlfree.get(n - 13))
                xt[n] = load(XL[:, k, :], X3d[128 * n:128 * n + 128, :], f"ld.xl{k}")

            for n in range(8):
                load_xl(n)
            tz = tick(V.memset(VU[:, :, :, :], 1.0), "v.setup2")
            need(V, t_wl)
            for k in range(4):
                tl_ = tick(V.tensor_copy(Sw[:, 0, 128 * k:128 * k + 128], lnwb[:, 4 + k:5 + k].broadcast_to([128, 128])), "v.setup2")
            km, w = Ms.take()
            need(PE, tl_, t_wl)
            tok = tick(mms(psM[:, km, :], [(Sw[:, 0, 128 * k:128 * k + 128], Wl[:, k, 2 * D:3 * D]) for k in range(4)], w),
                       "pe.setup2")
            need(V, tok)
            t_bv = tick(V.tensor_copy(bvl[:, :], psM[:, km, :]), "v.setup2")
            Ms.give(km, t_bv)
            km, w = Ms.take()
            need(PE, w)
            for c in range(8):
                for k in range(4):
                    m = PE.matmul(psM[:, km, c:c + 1], Wl[:, k, 128 * c:128 * c + 128], lnwb[:, 4 + k:5 + k],
                                  start=(k == 0), stop=(k == 3))
            tok = tick(m, "pe.setup2")
            need(V, tok)
            t_bl = tick(V.tensor_scalar(bl[:, 0:4], psM[:, km, 0:4], 0.125, None, ALU.mult), "v.setup2")
            t_bl = tick(V.tensor_copy(bl[:, 4:8], psM[:, km, 4:8]), "v.setup2")
            Ms.give(km, t_bl)
            for k in range(4):
                t_wls = tick(V.tensor_scalar(Wl[:, k, :], Wl[:, k, :], lnwb[:, k:k + 1], None, ALU.mult), "v.setup2")

            tok = tick(V.tensor_tensor(comb[:, :], rsx[:, :], rsx[:, :], ALU.mult), "v.setup2")
            need(V, tok)
            tok = tick(V.tensor_tensor(comb[:, :], comb[:, :], mvx[:, :, 1], ALU.mult), "v.setup2")
            need(V, tok)
            tok = tick(V.tensor_scalar(comb[:, :], comb[:, :], 1e-5, None, ALU.add), "v.setup2")
            need(G, tok)
            tok = tick(G.tensor_tensor(comb[:, :], comb[:, :], mhalf[:, 0:1].broadcast_to([128, NT]), ALU.pow), "g.comb")
            need(V, tok)
            t_comb = tick(V.tensor_tensor(comb[:, :], comb[:, :], rsx[:, :], ALU.mult), "v.setup2")
            xu = {"read": [], "tail": None}
            vt = {}
            blocks = {}

            def prep_b(bi):
                i = bi % 4
                o = {}
                blocks[bi] = o
                need(G, xu["read"], xu["tail"])
                if i == 0:
                    t_tail = tick(G.memset(xU[:, :, 0:64], 0.0), "g.tail")
                else:
                    t_tail = tick(G.tensor_copy(xU[:, :, 0:64], xU[:, :, 512:576]), "g.tail")
                for t in range(4):
                    n = 4 * bi + t
                    kn, w = Xn.take()
                    need(V, w, t_comb, xt[n])
                    tn = tick(V.tensor_scalar(xn[:, kn, :], XL[:, n % 13, :], mvx[:, n, 0:1], comb[:, n:n + 1],
                                              ALU.subtract, ALU.mult), "v.lnapply")
                    te = turn4(xn[:, kn, :], tn, lambda tok, kn=kn: Xn.give(kn, tok),
                               xU[:, :, 64 + 128 * t:192 + 128 * t], [t_tail] + xu["read"], "xT")
                    yield
                xu["tail"] = te
                kq, wq_ = QUs.take()
                for c in range(4):
                    km, w = Ms.take()
                    need(PE, te, t_wls)
                    tok = tick(mms(psM[:, km, :], [(Wl[:, k, 128 * c:128 * c + 128], xU[:, k, 64:576])
                                                   for k in range(4)], w), "pe.Q")
                    need(A, tok, wq_, t_bl)
                    tq = tick(A.activation(QU[:, kq, c, :], psM[:, km, :], ACT.Identity, bias=bl[:, c:c + 1],
                                           scale=0.125), "a.Q")
                    Ms.give(km, tq)
                    yield
                kk, wk_ = KUs.take()
                for c in range(4):
                    km, w = Ms.take()
                    need(PE, w)
                    tok = tick(mms(psM[:, km, :], [(Wl[:, k, D + 128 * c:D + 128 * c + 128], xU[:, k, 64:576])
                                                   for k in range(4)], w), "pe.K")
                    need(A, tok, wk_)
                    tk = tick(A.activation(KU[:, kk, c, 64:576], psM[:, km, :], ACT.Identity, bias=bl[:, 4 + c:5 + c]),
                              "a.K")
                    Ms.give(km, tk)
                    yield
                need(G, tk, wk_)
                if i == 0:
                    te1 = tick(G.memset(KU[:, kk, :, 0:64], 0.0), "g.edge")
                else:
                    pk = blocks[bi - 1]["k"]
                    tick(G.tensor_copy(KU[:, pk, :, 576:640], KU[:, kk, :, 64:128]), "g.edge")
                    te1 = tick(G.tensor_copy(KU[:, kk, :, 0:64], KU[:, pk, :, 512:576]), "g.edge")
                    blocks[bi - 1]["tk"].append(te1)
                if i == 3:
                    te1 = tick(G.memset(KU[:, kk, :, 576:640], 0.0), "g.edge")
                o["tk"] = [tk, te1]
                o["q"], o["tq"], o["k"] = kq, tq, kk
                for j in range(5 if i == 3 else 4):
                    M = 128 if j < 4 else 64
                    kv_, wv_ = VUs.take()
                    km, w = Ms.take()
                    need(PE, te, t_tail)
                    tok = tick(mms(psM[0:M, km, :], [(xU[:, k, 128 * j:128 * j + M], Wl[:, k, 2 * D:3 * D])
                                                     for k in range(4)], w), "pe.V")
                    need(V, tok, wv_, t_bv, tz)
                    tv = tick(V.tensor_tensor(VU[0:M, kv_, :, 0:64],
                                              psM[0:M, km, :].rearrange("p (h d) -> p h d", h=8),
                                              bvl[0:M, :].rearrange("p (h d) -> p h d", h=8), ALU.add), "v.V")
                    Ms.give(km, tv)
                    vt[bi // 4, 4 * i + j] = (kv_, tv)
                    yield
                xu["read"] = [tok]

            class W:
                pass

            def scores_b(t):
                o = blocks[t.n // 4]
                tl = t.n % 4
                t.s, w_s = Sws.take()
                which = 1 if t.n % 16 == 0 else 2 if t.n % 16 == 15 else 0
                for p in range(2):
                    ks, w = SPs.take()
                    need(PE, w, o["tq"], o["tk"])
                    for k in range(2):
                        c = 2 * p + k
                        for h in range(2):
                            m = PE.matmul(psS[:, 2 * ks + h, 256 * k:256 * k + 256],
                                          QU[64 * h:64 * h + 64, o["q"], c, 128 * tl:128 * tl + 128],
                                          KU[64 * h:64 * h + 64, o["k"], c, 128 * tl:128 * tl + 256],
                                          start=True, stop=True)
                    t.tq = tick(m, "pe.S")
                    need(V, t.tq, w_s, t_wl2)
                    tok = tick(V.tensor_tensor(Sw[:, t.s, 1024 * p:1024 * p + 1024].rearrange("p (j n) -> p j n", j=4),
                                               psS[:, 2 * ks:2 * ks + 2, :].rearrange("p b (k n) -> p (b k) n", k=2),
                                               mid(msk[:, which, :], 4), ALU.add), "v.Sadd")
                    SPs.give(ks, tok)
                if tl == 3:
                    QUs.give(o["q"], t.tq)
                    KUs.give(o["k"], t.tq)
                sv = Sw[:, t.s, :].rearrange("p (h n) -> p h n", h=8)
                need(V, tok)
                tok = tick(V.tensor_reduce(mw[:, t.s, :], sv, X, ALU.max), "v.max")
                need(G, tok)
                t.sub = tick(G.tensor_tensor(sv, sv, last(mw[:, t.s, :], 256), ALU.subtract), "g.sub")

            def exp_b(t):
                need(A, t.sub)
                t.exp = tick(A.activation(Sw[:, t.s, :], Sw[:, t.s, :], ACT.Exp), "a.exp")

            def ptrans_b(t, q):
                kt, w = Ts.take()
                need(PE, w, t.exp)
                for c in range(4):
                    o = 512 * q + 128 * c
                    m = PE.transpose(psT[:, kt, 128 * c:128 * c + 128], Sw[:, t.s, o:o + 128], ident[:, :])
                tok = tick(m, "pe.PT")
                if q == 3:
                    Sws.give(t.s, tok)
                need(A, tok, free["PU"])
                t.pt = tick(A.copy(PU[:, 4 * q:4 * q + 4, :], psT[:, kt, :].rearrange("p (c n) -> p c n", c=4)), "a.PT")
                Ts.give(kt, t.pt)

            def pv_b(t):
                b, j = t.n // 16, t.n % 16
                v0, v1 = vt[b, j], vt[b, j + 1]
                t.o, w_o = Ons.take()
                for p in range(2):
                    km, w = Ms.take()
                    need(PE, w, t.pt, v0[1], v1[1])
                    for jj in range(4):
                        bank, k = jj % 2, jj // 2
                        pos = 4 * p + 2 * bank + k
                        for ck, v in ((0, v0), (1, v1)):
                            m = PE.matmul(psM[:, km, 65 * jj:65 * jj + 65], PU[:, 2 * pos + ck, :],
                                          VU[:, v[0], 4 * p + jj, :], start=(ck == 0), stop=(ck == 1))
                    tok = tick(m, "pe.PV")
                    ov = psM[:, km, 0:260].rearrange("p (h e) -> p h e", e=65)
                    kr, wr = Rc.take()
                    need(V, tok, w_o, wr)
                    tr = tick(V.reciprocal(rc[:, kr, 0:4], ov[:, :, 64]), "v.rc")
                    need(V, tr)
                    t.on = tick(V.tensor_tensor(On[:, t.o, 256 * p:256 * p + 256].rearrange("p (h d) -> p h d", h=4),
                                                ov[:, :, 0:64], last(rc[:, kr, 0:4], 64), ALU.mult), "v.On")
                    Rc.give(kr, t.on)
                    Ms.give(km, t.on)
                free["PU"] = [tok]
                VUs.give(v0[0], tok)
                if j == 15:
                    VUs.give(v1[0], tok)

            def wo_b(t):
                km, w = Ms.take()
                need(PE, t.te, t_wl2)
                tok = tick(mms(psM[:, km, :], [(OT[:, t.ot, c, :], Wlo[:, c, :]) for c in range(4)], w), "pe.Wo")
                OTs.give(t.ot, tok)
                x = XL[:, t.n % 13, :]
                need(V, tok)
                ty = tick(V.tensor_tensor(x, psM[:, km, :], x, ALU.add), "v.y")
                Ms.give(km, ty)
                need(SY, ty)
                t_st = tick(SY.dma_start(Yd[128 * t.n:128 * t.n + 128, :], x), f"st.y{t.n % 13}", 16)
                ko, w = Yos.take()
                need(G, ty, w, t_wl2)
                to = tick(G.tensor_tensor(yo[:, ko, :], x, nulq[:, :], ALU.add), "g.yo")
                need(SY, to)
                Yos.give(ko, tick(SY.dma_start(out[128 * t.n:128 * t.n + 128, :], yo[:, ko, :]), f"st.o{ko}", 16))
                xlfree[t.n] = [t_st, to]

            idx_tok = {}

            def routing():
                kt, w = Ts.take()
                need(PE, w, s_tok, t_ident)
                tok = tick(PE.transpose(psT[:, kt, 0:128], scol[:, :, :].rearrange("p r n -> p (r n)"), ident[:, :]), "pe.rt")
                need(V, tok)
                tok = tick(V.tensor_copy(sr[:, :], psT[:, kt, 0:128]), "v.rt")
                Ts.give(kt, tok)
                need(V, tok)
                tok = tick(V.tensor_reduce(rcol[:, 0:1], sr[:, :], X, ALU.max), "v.rt")
                smax, na, M, part, lnv, T, cand, dd, sel = (rcol[:, i:i + 1] for i in (1, 2, 3, 4, 5, 6, 7, 8, 9))
                logk, kcol = cols[:, 4:5], cols[:, 5:6]
                yield
                kt, w = Ts.take()
                need(PE, w, tok)
                tok = tick(PE.transpose(psT[0:1, kt, 0:128], rcol[:, 0:1], ident[:, :]), "pe.rt")
                need(V, tok)
                tok = tick(V.tensor_reduce(er[0:1, 0:8], psT[0:1, kt, 0:128].rearrange("o (g i) -> o g i", i=16), X,
                                           ALU.max), "v.rt")
                Ts.give(kt, tok)
                need(V, tok)
                tok = tick(V.tensor_copy(zr[0:1, :].rearrange("o (g i) -> o g i", i=16), last(er[0:1, 0:8], 16)), "v.rt")
                yield
                kt, w = Ts.take()
                need(PE, w, tok)
                tok = tick(PE.matmul(psT[:, kt, 0:1], zr[0:1, :], ident[0:1, 0:1], start=True, stop=True), "pe.rt")
                need(V, tok)
                tok = tick(V.tensor_copy(smax, psT[:, kt, 0:1]), "v.rt")
                Ts.give(kt, tok)
                tok2 = tick(V.tensor_scalar(na, logk, -1.0, math.log(S), ALU.mult, ALU.add), "v.rt")
                need(V, tok, tok2)
                yield
                for it in range(1, ITERS):
                    tok = tick(V.tensor_tensor(M, smax, na, ALU.min), "v.rt")
                    need(V, tok)
                    tok = tick(V.tensor_scalar(zr[:, :], sr[:, :], na, M, ALU.min, ALU.subtract), "v.rt")
                    need(A, tok)
                    yield
                    te = tick(A.activation(er[:, :], zr[:, :], ACT.Exp, accum_out=part), "a.rt")
                    yield
                    km, w = Ms.take()
                    need(PE, te, w)
                    tok = tick(PE.matmul(psM[:, km, 0:1], grp[:, :], part, start=True, stop=True), "pe.rt")
                    need(A, tok)
                    tl2 = tick(A.activation(lnv, psM[:, km, 0:1], ACT.Ln), "a.rt")
                    Ms.give(km, tl2)
                    yield
                    need(V, tl2)
                    tok = tick(V.tensor_scalar(na, lnv, M, logk, ALU.add, ALU.subtract), "v.rt")
                    need(V, tok)
                tok = tick(V.tensor_scalar(zr[:, :], sr[:, :], na, None, ALU.subtract), "v.rt")
                need(V, tok)
                tok = tick(V.tensor_scalar(er[:, :], zr[:, :], 0.0, None, ALU.max), "v.rt")
                need(V, tok)
                tok = tick(V.tensor_tensor(zr[:, :], zr[:, :], er[:, :], ALU.subtract), "v.rt")
                yield
                need(A, tok)
                tok = tick(A.activation(sr[:, :], zr[:, :], ACT.Exp), "a.rt")
                need(V, tok)
                yield
                tok = tick(V.memset(T, 0.0), "v.rt")
                for bit in range(29, -1, -1):
                    need(V, tok)
                    tok = tick(V.tensor_scalar(cand.bitcast(I32), T.bitcast(I32), 1 << bit, None, ALU.bitwise_or), "v.rt")
                    need(V, tok)
                    tok = tick(V.tensor_scalar(zr[:, :], sr[:, :], cand, 0.0, ALU.is_ge, ALU.add, accum_out=part), "v.rt")
                    tok2 = tick(V.tensor_tensor(dd, cand, T, ALU.subtract), "v.rt")
                    yield
                    km, w = Ms.take()
                    need(PE, tok, w)
                    tok = tick(PE.matmul(psM[:, km, 0:1], grp[:, :], part, start=True, stop=True), "pe.rt")
                    need(V, tok, tok2)
                    tok = tick(V.tensor_scalar(sel, psM[:, km, 0:1], kcol, None, ALU.is_ge), "v.rt")
                    Ms.give(km, tok)
                    need(V, tok)
                    tok = tick(V.scalar_tensor_tensor(T, dd, sel, T, ALU.mult, ALU.add), "v.rt")
                need(V, tok)
                tok = tick(V.tensor_scalar(zr[:, :], sr[:, :], T, 0.0, ALU.is_gt, ALU.add, accum_out=rcol[:, 10:11]), "v.rt")
                tok = tick(V.tensor_scalar(er[:, :], sr[:, :], T, 0.0, ALU.is_equal, ALU.add, accum_out=rcol[:, 11:12]),
                           "v.rt")
                yield
                km, w = Ms.take()
                need(PE, tok, w)
                PE.matmul(psM[:, km, 0:1], grp[:, :], rcol[:, 10:11], start=True, stop=True)
                tok = tick(PE.matmul(psM[:, km, 1:2], tri[:, :], rcol[:, 11:12], start=True, stop=True), "pe.rt")
                need(V, tok)
                tok = tick(V.tensor_scalar(rcol[:, 12:13], psM[:, km, 0:1], -1.0, kcol, ALU.mult, ALU.add), "v.rt")
                need(V, tok)
                tok = tick(V.tensor_tensor(rcol[:, 13:14], rcol[:, 12:13], psM[:, km, 1:2], ALU.subtract), "v.rt")
                Ms.give(km, tok)
                yield
                t1 = tick(V.memset(cb[:, 128:256], 1.0), "v.rt")
                need(V, t1)
                tok = tick(V.tensor_tensor_scan(cb[:, 0:128], cb[:, 128:256], er[:, :], 0.0, ALU.mult, ALU.add), "v.rt")
                need(V, tok)
                tok = tick(V.tensor_scalar(cb[:, 0:128], cb[:, 0:128], rcol[:, 13:14], None, ALU.is_le), "v.rt")
                need(V, tok)
                tok = tick(V.tensor_tensor(er[:, :], er[:, :], cb[:, 0:128], ALU.mult), "v.rt")
                need(V, tok)
                tok = tick(V.tensor_tensor(er[:, :], er[:, :], zr[:, :], ALU.add), "v.rt")
                need(V, tok)
                tok = tick(V.tensor_tensor_scan(cb[:, 0:128], cb[:, 128:256], er[:, :], 0.0, ALU.mult, ALU.add), "v.rt")
                t1 = tick(V.tensor_scalar(zr[:, :], sr[:, :], -1.0, 1.0, ALU.mult, ALU.add), "v.rt")
                need(V, t1, tok)
                tf = tick(V.tensor_tensor(zr[:, :], zr[:, :], sr[:, :], ALU.add), "v.rt")
                yield
                km, w = Ms.take()
                need(PE, tok, w)
                tok = tick(PE.matmul(psM[:, km, 0:1], tri[:, :], cb[:, 127:128], start=True, stop=True), "pe.rt")
                need(V, tok)
                tok = tick(V.tensor_scalar(er[:, :], cb[:, 0:128], psM[:, km, 0:1], None, ALU.add), "v.rt")
                Ms.give(km, tok)
                need(SY, tok, tf)
                tick(SY.dma_start(cumd.rearrange("g (i n) -> (g i) n", i=16), er[:, :]), "st.rt", 16)
                t_f = tick(SY.dma_start(fd.rearrange("(p n) o -> p (n o)", n=128), zr[:, :]), "st.rt", 16)
                need(SY, t_f, tok)
                yield
                tb = []
                for g in range(8):
                    r, b = g // 4, g % 4
                    need(SY, tb)
                    tl_ = load(cb[:, :], cumd[g:g + 1, :].broadcast_to([128, S]), "ld.cb")
                    yield
                    for j in range((2, 4)[r]):
                        c = (2 * b + j) if r == 0 else (8 + 4 * b + j)
                        need(V, tl_)
                        tok = tick(V.tensor_scalar(Jk, cb[:, :], cols[:, j:j + 1], 0.0, ALU.is_le, ALU.add,
                                                   accum_out=idxf[:, c:c + 1]), "v.idx")
                        tb = [tok]
                        need(V, tok)
                        yield
                    c0 = 2 * b if r == 0 else 8 + 4 * b
                    c1 = c0 + (2, 4)[r]
                    tok = tick(V.tensor_scalar(idxf[:, c0:c1], idxf[:, c0:c1], float(S * b), None, ALU.add), "v.idx")
                    need(V, tok)
                    tick(V.tensor_copy(idx[:, c0:c1], idxf[:, c0:c1]), "v.idx")
                    tok = tick(V.tensor_scalar(idxf[:, c0:c1], idxf[:, c0:c1], float(B * S * r), None, ALU.add), "v.idx")
                    need(V, tok)
                    tok = tick(V.tensor_copy(idxs[:, c0:c1], idxf[:, c0:c1]), "v.idx")
                    tb.append(tok)
                    idx_tok[0] = tok
                    yield

            Jk = junk2[:, :]
            bg, rt_ = Later(), Later()
            rt_.add(routing())
            bg.add(prep_b(0))
            bg.drain()
            made = {1: bg.add(prep_b(1))}
            tiles = []
            for n in range(NT):
                t = W()
                t.n = n
                tiles.append(t)
            for n in range(8, 10):
                load_xl(n)
            for n in range(NT + 2):
                cur = tiles[n] if n < NT else None
                p1 = tiles[n - 1] if 1 <= n <= NT else None
                p2 = tiles[n - 2] if n >= 2 else None
                if cur is not None:
                    if n % 4 == 2:
                        bi = (n + 2) // 4
                        if bi < NB:
                            bg.finish(made[bi])
                        if bi + 1 < NB:
                            made[bi + 1] = bg.add(prep_b(bi + 1))
                    if n + 10 < NT:
                        load_xl(n + 10)
                    scores_b(cur)
                if p2 is not None:
                    p2.ot, w = OTs.take()
                    p2.te = turn4(On[:, p2.o, :], p2.on, lambda tok: Ons.give(p2.o, tok), OT[:, p2.ot, :, :], w, "OT")
                bg.piece()
                rt_.piece()
                if p1 is not None:
                    ptrans_b(p1, 0)
                    ptrans_b(p1, 1)
                bg.piece()
                rt_.piece()
                if p1 is not None:
                    ptrans_b(p1, 2)
                    ptrans_b(p1, 3)
                bg.piece()
                rt_.piece()
                if p2 is not None:
                    wo_b(p2)
                bg.piece()
                rt_.piece()
                if p1 is not None:
                    pv_b(p1)
                if cur is not None:
                    exp_b(cur)
                bg.piece()
                rt_.piece()
            bg.drain()
            rt_.drain()
            done = fl.all()
        for e in (PE, V, A, G, SY):
            need(e, done)
        if "C" not in parts:
            return

        with ExitStack() as pc:
            sb = alloc(pc)
            Wh = sb("Wh", [128, 4, D])
            Wkv = sb("Wkv", [128, 4, 2 * D])
            Who = sb("Who", [128, 4, D])
            gam = sb("gam", [128, 4])
            nkb = sb("nkb", [128, 4, 8])
            nvb = sb("nvb", [128, 8, 65])
            XH = sb("XH", [128, 6, D])
            yg = sb("yg", [128, 2, 2, D])
            fg = sb("fg", [128, 2, 6])
            ss = sb("ss", [128, 2, 8])
            sq = sb("sq", [128, D])
            sth = sb("sth", [128, 6, 6])
            mvh = sb("mvh", [128, 6, 2])
            rsh = sb("rsh", [128, 6])
            xh = sb("xh", [128, 4, 768])
            QH = sb("QH", [128, 2, 4, 256])
            KH = sb("KH", [128, 2, 4, 512])
            VH = sb("VH", [128, 2, 4, 8, 65])
            PH = sb("PH", [128, 3, D])
            PTH = sb("PTH", [128, 2, 4, 128])
            sn = sb("sn", [128, 2, 8])
            nm = sb("nm", [128, 2, 8])
            m0 = sb("m0", [128, 2, 8])
            pn = sb("pn", [128, 2, 8])
            on2 = sb("on2", [128, 2, 4, 65])
            oh = sb("oh", [128, 2, D])
            half = sb("half", [128, 8])
            Bs, XHs, PHs, PTs, Qt, O2s, SHs, OHs = (Slots(2), Slots(6), Slots(3), Slots(2), Slots(2), Slots(2), Slots(3),
                                                    Slots(2))
            load(Wh[:, :, :], a["wh"], "ld.wh")
            load(Wkv[:, :, :], a["wkv"], "ld.wh")
            load(Who[:, :, :], a["who"], "ld.wh")
            load(nkb[:, :, :], a["nkb"], "ld.wh")
            load(nvb[:, :, :], a["nvb"], "ld.wh")
            t_wh = load(gam[:, :], a["gam"], "ld.wh")
            t_half = tick(G.memset(half[:, :], 0.5), "g.half")
            tzh = tick(V.memset(VH[:, :, :, :, :], 1.0), "v.setup3")
            need(V, t_wh)
            for k in range(4):
                tick(V.tensor_scalar(Wh[:, k, :], Wh[:, k, :], gam[:, k:k + 1], None, ALU.mult), "v.setup3")
                t_g = tick(V.tensor_scalar(Wkv[:, k, :], Wkv[:, k, :], gam[:, k:k + 1], None, ALU.mult), "v.setup3")
            xhr = {"read": []}
            hb = {}

            def gather(dst, src, col, name):
                return tick(G.indirect_dma_start(dst, None, src, bass.IndirectOffsetOnAxis(col, 0)), name, 16)

            def prep_c(b):
                o = {}
                hb[b] = o
                k, wb = Bs.take()
                o["k"] = k
                ci = [2 * b, 2 * b + 1] + [8 + 4 * b + j for j in range(4)]
                need(G, wb)
                o["f"], o["y"] = [], []
                slots = []
                for j in range(6):
                    kx, w = XHs.take()
                    need(G, w)
                    tg = gather(XH[:, kx, :], X3d, idx[:, ci[j]:ci[j] + 1], f"gx{kx}")
                    tf = gather(fg[:, k, j:j + 1], fd, idxs[:, ci[j]:ci[j] + 1], f"gf{k}{j}")
                    o["f"].append(tf)
                    slots.append((kx, tg))
                    if j < 2:
                        o["y"].append(gather(yg[:, k, j, :], Yd, idx[:, ci[j]:ci[j] + 1], f"gy{k}{j}"))
                yield
                need(V, wb)
                for j, (kx, tg) in enumerate(slots):
                    need(V, tg)
                    tok = tick(V.bn_stats(sth[:, j, :], XH[:, kx, :]), "v.bnstats")
                need(V, tok)
                for j in range(6):
                    tok = tick(V.bn_aggr(mvh[:, j, :], sth[:, j, :]), "v.bnaggr")
                need(V, tok)
                tok = tick(V.tensor_scalar(rsh[:, :], mvh[:, :, 1], 1e-5, None, ALU.add), "v.vareps")
                need(G, tok)
                t_rs = tick(G.tensor_tensor(rsh[:, :], rsh[:, :], mhalf[:, 0:6], ALU.pow), "g.rstd")
                yield
                need(V, t_rs)
                for j, (kx, tg) in enumerate(slots):
                    slots[j] = (kx, tick(V.tensor_scalar(XH[:, kx, :], XH[:, kx, :], mvh[:, j, 0:1], rsh[:, j:j + 1],
                                                         ALU.subtract, ALU.mult), "v.zh"))
                yield
                need(A, wb)
                for j, (kx, tg) in enumerate(slots):
                    need(A, tg, ta if j else None)
                    ta = tick(A.activation(sq[:, :], XH[:, kx, :], ACT.Square, accum_out=ss[:, k, j:j + 1]), "a.sq")
                need(G, ta, t_half)
                tok = tick(G.tensor_tensor(ss[:, k, 0:6], ss[:, k, 0:6], half[:, 0:6], ALU.pow), "g.norm")
                need(V, tok)
                tok = tick(V.tensor_scalar(ss[:, k, 0:6], ss[:, k, 0:6], 1e-12, None, ALU.max), "v.norm")
                need(V, tok)
                tok = tick(V.reciprocal(ss[:, k, 0:6], ss[:, k, 0:6]), "v.norm")
                need(V, tok)
                t_n = tick(V.tensor_scalar(ss[:, k, 0:6], ss[:, k, 0:6], math.sqrt(float(D)), None, ALU.mult), "v.norm")
                yield
                for j, (kx, tg) in enumerate(slots):
                    kn, w = Xn.take()
                    need(V, w, t_n, tg)
                    tn = tick(V.tensor_scalar(xn[:, kn, :], XH[:, kx, :], ss[:, k, j:j + 1], None, ALU.mult), "v.rms")
                    XHs.give(kx, tn)
                    te = turn4(xn[:, kn, :], tn, lambda tok, kn=kn: Xn.give(kn, tok),
                               xh[:, :, 128 * j:128 * j + 128], xhr["read"], "xT")
                    yield
                for c in range(4):
                    km, w = Ms.take()
                    need(PE, te, t_g)
                    tok = tick(mms(psM[:, km, 0:256], [(Wh[:, i, 128 * c:128 * c + 128], xh[:, i, 0:256])
                                                       for i in range(4)], w), "pe.Q")
                    need(A, tok, wb)
                    o["tq"] = tick(A.mul(QH[:, k, c, :], psM[:, km, 0:256], 0.125), "a.Q")
                    Ms.give(km, o["tq"])
                    yield
                for c in range(4):
                    km, w = Ms.take()
                    tok = tick(mms(psM[:, km, :],
                                   [(Wkv[:, i, 128 * c:128 * c + 128],
                                     xh[:, i, 256:768]) for i in range(4)], w), "pe.K")
                    need(A, tok, wb)
                    o["tk"] = tick(A.copy(KH[:, k, c, :], psM[:, km, :]), "a.K")
                    Ms.give(km, o["tk"])
                    yield
                for j in range(4):
                    km, w = Ms.take()
                    tok = tick(mms(psM[:, km, :],
                                   [(xh[:, i, 256 + 128 * j:384 + 128 * j],
                                     Wkv[:, i, D:2 * D]) for i in range(4)], w),
                               "pe.V")
                    need(V, tok, wb, tzh, o["f"])
                    o["tv"] = tick(V.tensor_scalar(VH[:, k, j, :, 0:64], psM[:, km, :].rearrange("p (h d) -> p h d", h=8),
                                                   fg[:, k, 2 + j:3 + j], None, ALU.mult), "v.V")
                    Ms.give(km, o["tv"])
                    yield
                xhr["read"] = [tok]

            def null_scores(b, qt):
                o = hb[b]
                kq, w_q = Qt.take()
                km, w = Ms.take()
                need(PE, o["tq"], t_wh)
                tok = tick(mms(psM[:, km, 0:8], [(QH[:, o["k"], c, 128 * qt:128 * qt + 128], nkb[:, c, :])
                                                 for c in range(4)], w), "pe.sn")
                need(V, tok, w_q)
                tsn = tick(V.tensor_copy(sn[:, kq, :], psM[:, km, 0:8]), "v.sn")
                Ms.give(km, tsn)
                return kq, tsn

            class H:
                pass

            def scores_c(t):
                o, k = hb[t.b], hb[t.b]["k"]
                if t.h == 0:
                    t.g.kq, t.g.tsn = null_scores(t.b, t.qt)
                kq = t.g.kq
                ks, w = SHs.take()
                need(PE, w, o["tq"], o["tk"])
                p0, c = 64 * (t.h % 2), t.h // 2
                t.tq = tick(PE.matmul(psS[:, ks, :], QH[p0:p0 + 64, k, c, 128 * t.qt:128 * t.qt + 128],
                                      KH[p0:p0 + 64, k, c, :], start=True, stop=True), "pe.S")
                need(V, t.tq, t.g.tsn)
                tok = tick(V.tensor_reduce(m0[:, kq, t.h:t.h + 1], psS[:, ks, :], X, ALU.max), "v.max")
                need(V, tok)
                tok = tick(V.tensor_scalar(nm[:, kq, t.h:t.h + 1], m0[:, kq, t.h:t.h + 1], sn[:, kq, t.h:t.h + 1], -1.0,
                                           ALU.max, ALU.mult), "v.nm")
                t.g.tnm = tok
                t.p, w = PHs.take()
                need(A, tok, w)
                t.exp = tick(A.activation(PH[:, t.p, :], psS[:, ks, :], ACT.Exp, bias=nm[:, kq, t.h:t.h + 1]), "a.exp")
                SHs.give(ks, t.exp)
                if t.h % 4 == 3:
                    q = slice(t.h - 3, t.h + 1)
                    need(V, tok)
                    tok = tick(V.tensor_tensor(pn[:, kq, q], sn[:, kq, q], nm[:, kq, q], ALU.add), "v.pn")
                    need(A, tok)
                    t.g.tpn = tick(A.activation(pn[:, kq, q], pn[:, kq, q], ACT.Exp), "a.pn")

            def trans_c(t):
                kt, w = Ts.take()
                need(PE, w, t.exp)
                for c in range(4):
                    m = PE.transpose(psT[:, kt, 128 * c:128 * c + 128], PH[:, t.p, 128 * c:128 * c + 128], ident[:, :])
                tok = tick(m, "pe.PT")
                PHs.give(t.p, tok)
                t.pt, w = PTs.take()
                need(A, tok, w)
                t.tp = tick(A.copy(PTH[:, t.pt, :, :], psT[:, kt, :].rearrange("p (c n) -> p c n", c=4)), "a.PT")
                Ts.give(kt, t.tp)

            def pv_c(t):
                o, k = hb[t.b], hb[t.b]["k"]
                g = t.g
                if t.h % 4 == 0:
                    _, w = Oh.take()
                    need(PE, w)
                j = t.h % 4
                need(PE, t.tp, o["tv"])
                for c in range(4):
                    m = PE.matmul(psS[:, 3, 65 * j:65 * j + 65], PTH[:, t.pt, c, :], VH[:, k, c, t.h, :],
                                  start=(c == 0), stop=(c == 3))
                tok = tick(m, "pe.PV")
                PTs.give(t.pt, tok)
                if j < 3:
                    return
                p = t.h // 4
                if p == 0:
                    g.o, w = Ons.take()
                    need(V, w)
                k2, w = O2s.take()
                need(V, g.tpn, w, tok)
                tk = tick(V.tensor_tensor(on2[:, k2, :, :], nvb[:, 4 * p:4 * p + 4, :], last(pn[:, g.kq, 4 * p:4 * p + 4], 65),
                                          ALU.mult), "v.on2")
                need(V, tk)
                tk = tick(V.tensor_tensor(on2[:, k2, :, :], psS[:, 3, 0:260].rearrange("p (h e) -> p h e", e=65),
                                          on2[:, k2, :, :], ALU.add), "v.on2")
                Oh.give(0, tk)
                kr, w = Rc.take()
                need(V, tk, w)
                tk = tick(V.reciprocal(rc[:, kr, 0:4], on2[:, k2, :, 64]), "v.rc")
                need(V, tk)
                g.on = tick(V.tensor_tensor(On[:, g.o, 256 * p:256 * p + 256].rearrange("p (h d) -> p h d", h=4),
                                            on2[:, k2, :, 0:64], last(rc[:, kr, 0:4], 64), ALU.mult), "v.On")
                Rc.give(kr, g.on)
                O2s.give(k2, g.on)
                if p == 1:
                    Qt.give(g.kq, g.on)

            def out_c(g):
                o, k = hb[g.b], hb[g.b]["k"]
                ot, w = OTs.take()
                te = turn4(On[:, g.o, :], g.on, lambda tok: Ons.give(g.o, tok), OT[:, ot, :, :], w, "OT")
                km, w = Ms.take()
                need(PE, te)
                tok = tick(mms(psM[:, km, :], [(OT[:, ot, c, :], Who[:, c, :]) for c in range(4)], w), "pe.Wo")
                OTs.give(ot, tok)
                ko, w = OHs.take()
                need(V, tok, w, o["f"], o["y"])
                th = tick(V.scalar_tensor_tensor(oh[:, ko, :], psM[:, km, :], fg[:, k, g.qt:g.qt + 1], yg[:, k, g.qt, :],
                                                 ALU.mult, ALU.add), "v.oh")
                Ms.give(km, th)
                need(G, th)
                c = 2 * g.b + g.qt
                ts = tick(G.indirect_dma_start(out, bass.IndirectOffsetOnAxis(idx[:, c:c + 1], 0), oh[:, ko, :], None),
                          f"sc{ko}", 16)
                OHs.give(ko, ts)
                if g.qt == 1:
                    Bs.give(k, g.last, th)

            Oh = Slots(1)
            bg = Later()
            bg.add(prep_c(0))
            bg.drain()
            made = {}
            seq = []
            for b in range(B):
                for qt in range(2):
                    g = H()
                    g.b, g.qt = b, qt
                    for h in range(8):
                        t = H()
                        t.g, t.b, t.qt, t.h = g, b, qt, h
                        seq.append(t)
            for n in range(len(seq) + 5):
                if n < len(seq):
                    t = seq[n]
                    if t.qt == 0 and t.h == 0:
                        if t.b:
                            bg.finish(made[t.b])
                    if t.qt == 0 and t.h == 5 and t.b + 1 < B:
                        made[t.b + 1] = bg.add(prep_c(t.b + 1))
                    scores_c(t)
                bg.piece()
                if 2 <= n < len(seq) + 2:
                    trans_c(seq[n - 2])
                bg.piece()
                if 3 <= n < len(seq) + 3:
                    t = seq[n - 3]
                    pv_c(t)
                    if t.h == 7:
                        t.g.last = ("pe.PV", fl.val["pe.PV"])
                if 4 <= n < len(seq) + 4 and seq[n - 4].h == 7:
                    out_c(seq[n - 4].g)
            done = fl.all()
        for e in (PE, V, A, G, SY):
            need(e, done)


def wT(w, np):
    w = np.asarray(w)
    o, i = w.shape
    return np.ascontiguousarray(w.T.reshape(i // 128, 128, o).transpose(1, 0, 2))


def rows(v, np, n=128):
    return np.ascontiguousarray(np.broadcast_to(np.asarray(v)[None], (n, v.shape[0])))


def layout(inp, np):
    g = {k: np.asarray(v) for k, v in inp.items()}
    d = {}
    col = lambda v: v.reshape(4, 128).T
    d["x"] = g["x"].reshape(B * S, D)
    for L in (0, 1):
        p = f"L{L}_xcond_"
        for w in "qkvo":
            d[f"w{w}{L}"] = wT(g[p + "W" + w], np)
        d[f"bo{L}"] = rows(g[p + "bo"], np)
        d[f"bv{L}"] = rows(g[p + "bv"], np, NK)
    d["bq"] = np.ascontiguousarray(np.stack([col(g["L0_xcond_bq"]), col(g["L1_xcond_bq"])], 1))
    kc = np.zeros((128, 16), np.float32)
    kc[:, 0:4], kc[:, 4:8] = col(g["L0_xcond_bk"]), col(g["L1_xcond_bk"])
    kc[:, 8:12] = g["condB_tau"][None]
    d["kcol"] = kc
    d["delta"] = np.ascontiguousarray(np.broadcast_to(g["fside_BxS2_0"][None], (128, B, NK)))
    d["ctxT"] = np.ascontiguousarray(g["ctx_1024"].reshape(B * NK, 4, 128).transpose(2, 1, 0))
    d["win"] = wT(np.concatenate([g["L0_ffn_Win"].T] * 2, 0), np)
    d["wout"] = np.concatenate([g["L0_ffn_Wout"]] * 2, 0)
    d["bout"] = rows(g["L0_ffn_bout"], np)
    pair = lambda w: w.reshape(64, 8, 2).transpose(2, 0, 1).reshape(128, 8)
    fc = np.zeros((128, 32), np.float32)
    fc[:, 0:8], fc[:, 8:16], fc[:, 16:24] = pair(g["L0_ffn_W1"]), pair(g["L0_ffn_b1"]), pair(g["L0_ffn_W2"])
    fc[:, 24] = np.concatenate([g["L0_ffn_bin_"]] * 2)
    fc[:, 25] = np.concatenate([g["L0_ffn_b2"]] * 2)
    d["fcol"] = fc
    d["rt"] = np.ascontiguousarray(np.broadcast_to(
        np.stack([g["L1_ffn_rt_q"][0], g["L1_ffn_rt_kv"][0]])[None], (128, 2, D)))
    d["c_ident"] = np.eye(128, dtype=np.float32)
    p = np.arange(128)
    d["c_grp"] = (p[:, None] // 16 == p[None] // 16).astype(np.float32)
    d["c_tri"] = ((p[:, None] // 16 == p[None] // 16) & (p[:, None] < p[None])).astype(np.float32)
    cols = np.zeros((128, 16), np.float32)
    for j in range(4):
        cols[:, j] = p + 128 * j
    cols[:, 4] = np.where(p < 64, LOGK[0], LOGK[1])
    cols[:, 5] = np.where(p < 64, NQ, NKV)
    d["cols"] = cols
    d["wqkv"] = wT(g["L1_ffn_Wqkv"], np)
    d["wlo"] = wT(g["L1_ffn_Wout_l"], np)
    d["lnwb"] = np.ascontiguousarray(np.concatenate([col(g["L1_ffn_ln_w"]), col(g["L1_ffn_ln_b"])], 1))
    d["nulq"] = rows(g["L1_ffn_null_q"], np)
    m = np.zeros((128, 3, 256), np.float32)
    m[:64, :, 192:] = -1e30
    m[64:, :, :64] = -1e30
    m[:, 1, :64] = -1e30
    m[:, 2, 192:] = -1e30
    d["c_mask"] = m
    d["wh"] = wT(g["L1_ffn_Wq"], np)
    d["wkv"] = wT(g["L1_ffn_Wkv"].reshape(8, 2, 64, D).transpose(1, 0, 2, 3).reshape(2 * D, D), np)
    d["who"] = wT(g["L1_ffn_Wout_h"], np)
    d["gam"] = np.ascontiguousarray(col(g["L1_ffn_gamma"]))
    nk = np.zeros((8, 64, 8), np.float32)
    for h in range(8):
        nk[h, :, h] = g["L1_ffn_null_kv"][0, h]
    d["nkb"] = np.ascontiguousarray(nk.reshape(4, 128, 8).transpose(1, 0, 2))
    nv = np.ones((128, 8, 65), np.float32)
    nv[:, :, :64] = g["L1_ffn_null_kv"][1][None]
    d["nvb"] = nv
    return d


def kernel(**inputs):
    import numpy as np
    import concourse.bacc as bacc
    from concourse.bass_utils import run_bass_kernel_spmd as run

    nc = bacc.Bacc("TRN2", target_bir_lowering=False, num_devices=1)
    arrays = {"in_" + k: v for k, v in layout(inputs, np).items()}
    args = {k[3:]: nc.dram_tensor(k, v.shape, mybir.dt.from_np(v.dtype), kind="ExternalInput").ap()
            for k, v in arrays.items()}
    out = nc.dram_tensor("out_0", (B * S, D), F, kind="ExternalOutput").ap()
    build(nc, args, out)
    r = run(nc, [arrays], core_ids=[0])
    return r.results[0]["out_0"].reshape(B, S, D)
```

```python
import math
from collections import deque
from contextlib import ExitStack

import concourse.bass as bass
from concourse import mybir

ALU = mybir.AluOpType
ACT = mybir.ActivationFunctionType
X = mybir.AxisListType.X
F = mybir.dt.float32
I32 = mybir.dt.int32

B, S, D = 4, 2048, 512
NK = 77
NQ, NKV = 256, 512
NT = B * S // 128
NB = NT // 4
ITERS = 50
OFF3 = (0, 103, 205)
SEGS = ((0, 0, 0, 77, 0, 0), (0, 1, 0, 26, 77, 33),
        (1, 1, 26, 51, 0, 0), (1, 2, 0, 52, 51, 33),
        (2, 2, 52, 25, 1, 0), (2, 3, 0, 77, 26, 33))
LOGK = (math.log(NQ * 9.0 / 8.0), math.log(NKV * 9.0 / 8.0))


class Flow:

    def __init__(self, nc, stack):
        self.nc, self.stack = nc, stack
        self.sem, self.val, self.seen = {}, {}, {}

    def tick(self, ins, name, by=1):
        if name not in self.sem:
            self.sem[name] = self.stack.enter_context(self.nc.semaphore(name))
            self.val[name] = 0
        ins.then_inc(self.sem[name], by)
        self.val[name] += by
        return (name, self.val[name])

    def need(self, eng, *tokens):
        for t in tokens:
            if t is None:
                continue
            if isinstance(t, list):
                self.need(eng, *t)
                continue
            name, v = t
            key = (str(eng.engine), name)
            if self.seen.get(key, 0) < v:
                eng.wait_ge(self.sem[name], v)
                self.seen[key] = v

    def all(self):
        return list(self.val.items())


class Slots:

    def __init__(self, n):
        self.ready = deque((k, []) for k in range(n))

    def take(self):
        assert self.ready, "taken before it was given back"
        return self.ready.popleft()

    def give(self, k, *toks):
        self.ready.append((k, list(toks)))


class Later:

    def __init__(self):
        self.q, self.turn = (deque(), deque()), 0

    def add(self, gen, which=0):
        self.q[which].append(gen)
        return gen

    def one(self, which):
        q = self.q[which]
        while q:
            try:
                next(q[0])
                return True
            except StopIteration:
                q.popleft()
        return False

    def piece(self):
        self.turn ^= 1
        return self.one(self.turn) or self.one(self.turn ^ 1)

    def finish(self, gen):
        while gen in self.q[0] or gen in self.q[1]:
            self.one(0 if gen in self.q[0] else 1)

    def drain(self):
        while self.piece():
            pass


def last(ap, n):
    return ap.unsqueeze(2).broadcast_to([ap.shape[0], ap.shape[1], n])


def mid(ap, n):
    return ap.unsqueeze(1).broadcast_to([ap.shape[0], n, ap.shape[1]])


def build(nc, a, out, parts="ABC"):
    PE, V, A, G, SY = nc.tensor, nc.vector, nc.scalar, nc.gpsimd, nc.sync
    with ExitStack() as top:
        fl = Flow(nc, top)
        tick, need = fl.tick, fl.need

        def dram(name, shape):
            return nc.dram_tensor(name, shape, F, kind="Internal").ap()

        X3d = dram("x3_scratch", (B * S, D))
        Yd = dram("y_scratch", (B * S, D))
        Vd = dram("v_scratch", (2, B, 16, NK, 33))
        cumd = dram("cum_scratch", (8, S))
        fd = dram("f_scratch", (2 * B * S, 1))

        def alloc(stack):
            return lambda name, shape, dt=F: stack.enter_context(nc.sbuf_tensor(name, shape, dt))

        def load(dst, src, name, eng=SY):
            return tick(eng.dma_start(dst, src), name, 16)

        sb = alloc(top)
        psS = top.enter_context(nc.psum_tensor("psS", [128, 4, 512], F))
        psT = top.enter_context(nc.psum_tensor("psT", [128, 2, 512], F))
        psM = top.enter_context(nc.psum_tensor("psM", [128, 2, 512], F))
        Ts, Ms = Slots(2), Slots(2)

        ident = sb("ident", [128, 128])
        grp = sb("grp", [128, 128])
        tri = sb("tri", [128, 128])
        mhalf = sb("mhalf", [128, 8])
        cols = sb("cols", [128, 16])
        scol = sb("scol", [128, 2, NT])
        mvx = sb("mvx", [128, NT, 2])
        rsx = sb("rsx", [128, NT])
        t_ident = load(ident[:, :], a["c_ident"], "ld.ident")
        t_mhalf = tick(G.memset(mhalf[:, :], -0.5), "g.mhalf")
        s_tok = []

        idx = sb("idx", [128, 24], I32)
        idxs = sb("idxs", [128, 24], I32)
        st = sb("st", [128, 2, 4, 6])
        mv = sb("mv", [128, 2, 4, 2])
        ve = sb("ve", [128, 2, 4])
        rs = sb("rs", [128, 2, 4])
        Ln = Slots(2)
        xn = sb("xn", [128, 3, D])
        Xn = Slots(3)
        On = sb("On", [128, 2, D])
        Ons = Slots(2)
        OT = sb("OT", [128, 2, 4, 128])
        OTs = Slots(2)
        rc = sb("rc", [128, 2, 8])
        Rc = Slots(2)

        def ln_stats(tiles, ready):
            k, w = Ln.take()
            need(V, w)
            for t in range(4):
                need(V, ready(t))
                tok = tick(V.bn_stats(st[:, k, t, :], tiles(t)), "v.bnstats")
            yield
            need(V, tok)
            for t in range(4):
                tok = tick(V.bn_aggr(mv[:, k, t, :], st[:, k, t, :]), "v.bnaggr")
            need(V, tok)
            tok = tick(V.tensor_scalar(ve[:, k, :], mv[:, k, :, 1], 1e-5, None, ALU.add), "v.vareps")
            need(G, tok, t_mhalf)
            tok = tick(G.tensor_tensor(rs[:, k, :], ve[:, k, :], mhalf[:, 0:4], ALU.pow), "g.rstd")
            yield
            return k, tok

        def ln_apply(k, t, x, t_rs, t_x):
            kx, w = Xn.take()
            need(V, w, t_rs, t_x)
            tok = tick(V.tensor_scalar(xn[:, kx, :], x, mv[:, k, t, 0:1], rs[:, k, t:t + 1],
                                       ALU.subtract, ALU.mult), "v.lnapply")
            if t == 3:
                Ln.give(k, tok)
            return kx, tok

        def turn4(src, t_src, give, dst, w_dst, name):
            kt, w = Ts.take()
            need(PE, w, t_src, t_ident)
            for c in range(4):
                m = PE.transpose(psT[:, kt, 128 * c:128 * c + 128], src[:, 128 * c:128 * c + 128], ident[:, :])
            tok = tick(m, "pe." + name)
            give(tok)
            need(A, tok, w_dst)
            te = tick(A.copy(dst, psT[:, kt, :].rearrange("p (c n) -> p c n", c=4)), "a." + name)
            Ts.give(kt, te)
            return te

        def mms(outp, pairs, w):
            need(PE, w)
            for i, (l, r) in enumerate(pairs):
                m = PE.matmul(outp, l, r, start=(i == 0), stop=(i == len(pairs) - 1))
            return m

        with ExitStack() as pa:
            sb = alloc(pa)
            Wq = [sb(f"Wq{L}", [128, 4, D]) for L in (0, 1)]
            Wo = [sb(f"Wo{L}", [128, 4, D]) for L in (0, 1)]
            bq = sb("bq", [128, 2, 4])
            bo = [sb(f"bo{L}", [128, D]) for L in (0, 1)]
            cF = sb("cF", [128, D])
            rt = sb("rt", [128, 2, D])
            KT = [sb(f"KT{L}", [128, 4, B * NK]) for L in (0, 1)]
            KB = [[sb(f"KB{L}{s}", [128, 4, 4 * NK]) for s in (0, 1)] for L in (0, 1)]
            VB = [[sb(f"VB{L}{s}", [103, 4, 3, 66]) for s in (0, 1)] for L in (0, 1)]
            Win = sb("Win", [128, 4, 128])
            Wout = sb("Wout", [128, D])
            fcol = sb("fcol", [128, 32])
            dlt = sb("dlt", [128, B, NK])
            XB = sb("XB", [128, 4, 4, D])
            xT = sb("xT", [128, 2, 4, D])
            QT = sb("QT", [128, 2, 4, D])
            Sb = sb("Sb", [128, 2, 16 * NK])
            PT = sb("PT", [103, 12, 128])
            mx = sb("mx", [128, 2, 16])
            sT = sb("sT", [128, 2, D])
            stage = sb("vstage", [NK, 16, 33])
            hh = sb("hh", [128, 2, D])
            acc = sb("acc", [128, D])
            junk = sb("junk", [128, D])
            zx = sb("zx", [128, D])
            sx = sb("sx", [128, 6])
            vx = sb("vx", [128, NT])
            XTs, QTs, Ss, STs, Hs, SPs = Slots(2), Slots(2), Slots(2), Slots(2), Slots(2), Slots(4)
            free = {"acc": [], "PT": [], "x": {}}

            ctxT = sb("ctxT", [128, 4, B * NK])
            kc = sb("kc", [128, 16])
            b2t = sb("b2t", [64, 128])

            t_c = load(ctxT[:, :, :], a["ctxT"], "ld.ctx")
            t_c = load(kc[:, :], a["kcol"], "ld.ctx")
            t_c = load(hh[0:NK, 0, :], a["bv0"], "ld.ctx")
            t_c = load(hh[0:NK, 1, :], a["bv1"], "ld.ctx")
            t_wk, t_wv, t_w, t_x = {}, {}, {}, {}
            xin = a["x"].rearrange("(n t p) d -> n p t d", t=4, p=128)

            def load_x(blk):
                need(SY, free["x"].get(blk - 4))
                return load(XB[:, blk % 4, :, :], xin[blk], f"ld.x{blk % 4}")

            wk, wv = XB[:, 2, :, :], XB[:, 3, :, :]

            def load_wkv(L, w_k, w_v):
                need(A, w_k)
                t_wk[L] = load(wk, a[f"wk{L}"], "ld.wk", A)
                need(A, w_v)
                t_wv[L] = load(wv, a[f"wv{L}"], "ld.wv", A)

            for k in (0, 1):
                Hs.take()
            load_wkv(0, [], [])
            t_x[0] = load_x(0)
            load(bq[:, :, :], a["bq"], "ld.small")
            load(fcol[:, :], a["fcol"], "ld.small")
            load(Wout[:, :], a["wout"], "ld.small")
            load(cF[:, :], a["bout"], "ld.small")
            load(dlt[:, :, :], a["delta"], "ld.small")
            t_small = load(cols[:, :], a["cols"], "ld.small")
            load(bo[0][:, :], a["bo0"], "ld.w0")
            load(Wq[0][:, :, :], a["wq0"], "ld.w0")
            t_w[0] = load(Wo[0][:, :, :], a["wo0"], "ld.w0")
            t_x[1] = load_x(1)
            load(Win[:, :, :], a["win"], "ld.w1")
            load(rt[:, :, :], a["rt"], "ld.w1")
            load(bo[1][:, :], a["bo1"], "ld.w1")
            load(Wq[1][:, :, :], a["wq1"], "ld.w1")
            t_w[1] = load(Wo[1][:, :, :], a["wo1"], "ld.w1")
            t_zero = []
            for L in (0, 1):
                for k in (0, 1):
                    tick(V.memset(KB[L][k][:, :, :], 0.0), "v.zero")
                    t_zero = tick(V.memset(VB[L][k][:, :, :, :], 0.0), "v.zero")
            t_one = tick(V.memset(stage[:, :, :], 1.0), "v.one")
            need(V, t_c)
            t_t = tick(V.tensor_scalar(kc[:, 12:16], kc[:, 8:12], 1.0 / math.sqrt(32.0), None, ALU.mult), "v.setup")
            tau = kc[:, 12:16]
            t_KT, t_V = {}, {}
            f_kv = {"stage": [t_one]}

            def setup_kv(L):
                for c in range(4):
                    km, w = Ms.take()
                    need(PE, t_wk[L], t_c)
                    tok = tick(mms(psM[:, km, 0:B * NK], [(wk[:, k, 128 * c:128 * c + 128], ctxT[:, k, :])
                                                          for k in range(4)], w), "pe.setup")
                    need(V, tok, t_t)
                    for b in range(B):
                        tok2 = tick(V.tensor_scalar(KT[L][:, c, NK * b:NK * b + NK], psM[:, km, NK * b:NK * b + NK],
                                                    kc[:, 4 * L + c:4 * L + c + 1], tau[:, b:b + 1],
                                                    ALU.add, ALU.mult), "v.KT")
                    Ms.give(km, tok2)
                    yield
                f_kv["k"] = tok
                t_KT[L] = tok2
                for b in range(B):
                    km, w = Ms.take()
                    need(PE, t_wv[L])
                    tok = tick(mms(psM[0:NK, km, :], [(ctxT[:, k, NK * b:NK * b + NK], wv[:, k, :])
                                                      for k in range(4)], w), "pe.setup")
                    need(V, tok, f_kv["stage"])
                    tok2 = tick(V.tensor_tensor(stage[:, :, 0:32],
                                                psM[0:NK, km, :].rearrange("p (h d) -> p h d", h=16),
                                                hh[0:NK, L, :].rearrange("p (h d) -> p h d", h=16), ALU.add), "v.V")
                    Ms.give(km, tok2)
                    need(SY, tok2)
                    tok2 = tick(SY.dma_start(Vd[L, b].rearrange("h k e -> k h e"), stage[:, :, :]), "st.V", 16)
                    f_kv["stage"] = [tok2]
                    t_V[L] = tok2
                    yield
                f_kv["v"] = tok

            def setup_rest():
                need(V, t_small)
                tok = tick(V.scalar_tensor_tensor(fcol[:, 8:16], fcol[:, 0:8], fcol[:, 24:25], fcol[:, 8:16],
                                                  ALU.mult, ALU.add), "v.setup")
                tok = tick(V.tensor_copy(b2t[:, :], fcol[0:64, 25:26].broadcast_to([64, 128])), "v.setup")
                km, w = Ms.take()
                need(PE, tok, t_small)
                tok = tick(mms(psM[:, km, :], [(b2t[:, :], Wout[0:64, :])], w), "pe.setup")
                need(V, tok)
                tok = tick(V.tensor_tensor(cF[:, :], psM[:, km, :], cF[:, :], ALU.add), "v.setup")
                Ms.give(km, tok)
                return tok

            need(V, t_small)
            t_d = tick(V.tensor_scalar(dlt[:, :, :], dlt[:, :, :], 1.0 / math.sqrt(32.0), None, ALU.mult), "v.setup")
            for _ in setup_kv(0):
                pass
            load_wkv(1, [f_kv["k"]], [f_kv["v"]])
            t_f = t_cF = setup_rest()

            KVs = {0: Slots(2), 1: Slots(2)}
            kv = {}

            def load_kv(L, b):
                k, w = KVs[L].take()
                need(V, w, t_zero, t_KT[L])
                for i in range(4):
                    tk = tick(V.tensor_copy(KB[L][k][32 * i:32 * i + 32, :, NK * i:NK * i + NK],
                                            KT[L][32 * i:32 * i + 32, :, NK * b:NK * b + NK]), f"v.KB{L}")
                yield
                need(SY, w, t_zero, t_V[L])
                for c, i, k0, n, r0, c0 in SEGS:
                    tv = load(VB[L][k][r0:r0 + n, :, c, c0:c0 + 33],
                              Vd[L, b].rearrange("(g i) k e -> i k g e", i=4)[i, k0:k0 + n], f"ld.VB{L}")
                kv[L, b] = (k, tk, tv)
                yield

            class Blk:
                pass

            blks = {}

            def prep(blk, L, row, t_row, proj):
                bk = blks[blk]
                xb = XB[:, blk % 4, :, :]
                k, t_rs = yield from ln_stats(lambda t: xb[:, t, :], lambda t: bk.ready[t])
                yield
                kx, w = XTs.take()
                ready = []

                def ln(t):
                    kn, tn = ln_apply(k, t, xb[:, t, :], t_rs, bk.ready[t])
                    need(G, tn, t_row)
                    ready.append(tick(G.tensor_tensor(xb[:, t, :], xb[:, t, :], row, ALU.add), "g.bias"))
                    return kn, tn

                nxt = ln(0)
                yield
                for t in range(4):
                    kn, tn = nxt
                    nxt = ln(t + 1) if t < 3 else None
                    te = turn4(xn[:, kn, :], tn, lambda tok, kn=kn: Xn.give(kn, tok),
                               xT[:, kx, :, 128 * t:128 * t + 128], w, "xT")
                    yield
                bk.ready = ready
                yield
                yield from proj(bk, kx, te)

            def qproj(L):
                def go(bk, kx, te):
                    kq, wq_ = QTs.take()
                    for c in range(4):
                        km, w = Ms.take()
                        need(PE, te, t_w[L])
                        tok = tick(mms(psM[:, km, :], [(Wq[L][:, k, 128 * c:128 * c + 128], xT[:, kx, k, :])
                                                       for k in range(4)], w), "pe.Q")
                        need(A, tok, wq_, t_small)
                        tq = tick(A.activation(QT[:, kq, c, :], psM[:, km, :], ACT.Identity, bias=bq[:, L, c:c + 1]), "a.Q")
                        Ms.give(km, tq)
                        yield
                    XTs.give(kx, tok)
                    bk.q = (kq, tq)
                return go

            def ffn(bk, kx, te):
                ks, w1 = STs.take()
                km, w = Ms.take()
                need(PE, te, t_w[1])
                tok = tick(mms(psM[:, km, :], [(Win[:, k, :], xT[:, kx, k, :]) for k in range(4)], w), "pe.win")
                XTs.give(kx, tok)
                need(A, tok, w1)
                ts = tick(A.copy(sT[:, ks, :], psM[:, km, :]), "a.sT")
                Ms.give(km, ts)
                yield
                need(A, ts, t_f)
                need(V, free["acc"])
                for j in range(8):
                    kh, w = Hs.take()
                    need(A, w)
                    th = tick(A.activation(hh[:, kh, :], sT[:, ks, :], ACT.Relu, bias=fcol[:, 8 + j:9 + j],
                                           scale=fcol[:, j:j + 1]), "a.relu")
                    need(V, th)
                    if j == 0:
                        ta = tick(V.tensor_scalar(acc[:, :], hh[:, kh, :], fcol[:, 16:17], None, ALU.mult), "v.acc")
                    else:
                        need(V, ta)
                        ta = tick(V.scalar_tensor_tensor(acc[:, :], hh[:, kh, :], fcol[:, 16 + j:17 + j], acc[:, :],
                                                         ALU.mult, ALU.add), "v.acc")
                    Hs.give(kh, ta)
                    if j % 2:
                        yield
                STs.give(ks, th)
                yield
                for t in range(4):
                    km, w = Ms.take()
                    need(PE, ta)
                    tok = tick(mms(psM[:, km, :], [(acc[:, 128 * t:128 * t + 128], Wout[:, :])], w), "pe.wout")
                    need(V, tok, bk.ready[t])
                    x = XB[:, bk.i % 4, t, :]
                    bk.ready[t] = tick(V.tensor_tensor(x, psM[:, km, :], x, ALU.add), "v.x")
                    Ms.give(km, bk.ready[t])
                    yield
                free["acc"] = [tok]

            class Tile:
                pass

            def scores(t, gs):
                L, bk, b = t.L, t.bk, t.b
                if t.tl == 0:
                    need(PE, bk.q[1])
                kb, tk, tv = kv[L, b]
                if gs[0] == 0:
                    t.s, t.ws = Ss.take()
                w_s = t.ws
                kq = bk.q[0]
                for g in gs:
                    kp, w = SPs.take()
                    need(PE, tk)
                    t.tq = tick(mms(psS[:, kp, 0:308], [(QT[:, kq, g, 128 * t.tl:128 * t.tl + 128],
                                                         KB[L][kb][:, g, :])], w), "pe.S")
                    need(V, t.tq, w_s, t_d)
                    tok = tick(V.tensor_tensor(Sb[:, t.s, 308 * g:308 * g + 308].rearrange("p (i k) -> p i k", i=4),
                                               psS[:, kp, 0:308].rearrange("p (i k) -> p i k", i=4),
                                               mid(dlt[:, b, :], 4), ALU.add), "v.Sadd")
                    SPs.give(kp, tok)
                if gs[-1] != 3:
                    return
                if t.tl == 3:
                    QTs.give(kq, t.tq)
                sv = Sb[:, t.s, :].rearrange("p (h k) -> p h k", h=16)
                need(V, tok)
                tok = tick(V.tensor_reduce(mx[:, t.s, :], sv, X, ALU.max), "v.max")
                need(G, tok)
                t.sub = tick(G.tensor_tensor(sv, sv, last(mx[:, t.s, :], NK), ALU.subtract), "g.sub")

            def softexp(t):
                need(A, t.sub)
                t.exp = tick(A.activation(Sb[:, t.s, :], Sb[:, t.s, :], ACT.Exp), "a.exp")

            def ptrans(t, g):
                kt, w = Ts.take()
                need(PE, w, t.exp)
                for c in range(3):
                    o = 308 * g + OFF3[c]
                    m = PE.transpose(psT[0:103, kt, 128 * c:128 * c + 128], Sb[:, t.s, o:o + 103], ident[:, :])
                tok = tick(m, "pe.PT")
                if g == 3:
                    Ss.give(t.s, tok)
                need(A, tok, free["PT"])
                t.pt = tick(A.copy(PT[:, 3 * g:3 * g + 3, :],
                                   psT[0:103, kt, 0:384].rearrange("p (c n) -> p c n", c=3)), "a.PT")
                Ts.give(kt, t.pt)

            def pv(t, hf):
                kb, tk, tv = kv[t.L, t.b]
                if hf == 0:
                    t.o, t.wo_ = Ons.take()
                w_o = t.wo_
                km, w = Ms.take()
                need(PE, w, t.pt, tv)
                for j in range(2):
                    g = 2 * hf + j
                    for c in range(3):
                        o = 132 * j + 33 * c
                        m = PE.matmul(psM[:, km, o:o + 66], PT[:, 3 * g + c, :], VB[t.L][kb][:, g, c, :],
                                      start=(j == 0 and c == 0), stop=(j == 1 and c == 2), skip_group_check=True)
                tok = tick(m, "pe.PV")
                ov = psM[:, km, 0:264].rearrange("p (h e) -> p h e", e=33)
                kr, wr = Rc.take()
                need(V, tok, w_o, wr)
                tr = tick(V.reciprocal(rc[:, kr, :], ov[:, :, 32]), "v.rc")
                need(V, tr)
                t.on = tick(V.tensor_tensor(On[:, t.o, 256 * hf:256 * hf + 256].rearrange("p (h d) -> p h d", h=8),
                                            ov[:, :, 0:32], last(rc[:, kr, :], 32), ALU.mult), "v.On")
                Rc.give(kr, t.on)
                Ms.give(km, t.on)
                if hf == 0:
                    return
                free["PT"] = [tok]
                if t.lastkv:
                    KVs[t.L].give(kb, tok, t.tq)

            def otrans(t):
                t.ot, w = OTs.take()
                t.te = turn4(On[:, t.o, :], t.on, lambda tok: Ons.give(t.o, tok), OT[:, t.ot, :, :], w, "OT")

            def wo(t, part):
                if part == 0:
                    t.km, w = Ms.take()
                    need(PE, w, t.te, t_w[t.L])
                km = t.km
                for c in (2 * part, 2 * part + 1):
                    m = PE.matmul(psM[:, km, :], OT[:, t.ot, c, :], Wo[t.L][:, c, :], start=(c == 0), stop=(c == 3))
                if part == 0:
                    return
                tok = tick(m, "pe.Wo")
                OTs.give(t.ot, tok)
                bk = t.bk
                x = XB[:, bk.i % 4, t.tl, :]
                need(V, tok, bk.ready[t.tl])
                tx = tick(V.tensor_tensor(x, psM[:, km, :], x, ALU.add), "v.x")
                Ms.give(km, tx)
                if t.L == 0:
                    bk.new[t.tl] = tx
                    if t.tl == 3:
                        bk.ready = bk.new
                    return
                n = 4 * bk.i + t.tl
                need(SY, tx, x3_tok.get(n - 8))
                x3_tok[n] = tick(SY.dma_start(X3d[128 * n:128 * n + 128, :], x), f"st.x3{n % 8}", 16)
                need(V, tx, free.get("sx"))
                tok = tick(V.bn_stats(sx[:, :], x), "v.sx")
                need(V, tok)
                tok = tick(V.bn_aggr(mvx[:, n, :], sx[:, :]), "v.sx")
                need(V, tok)
                tok = tick(V.tensor_scalar(vx[:, n:n + 1], mvx[:, n, 1:2], 1e-5, None, ALU.add), "v.sx")
                free["sx"] = [tok]
                need(G, tok, t_mhalf)
                t.rx = tick(G.tensor_tensor(rsx[:, n:n + 1], vx[:, n:n + 1], mhalf[:, 0:1], ALU.pow), "g.rx")

            def route_scores(t):
                if t.L == 0:
                    return
                n = 4 * t.bk.i + t.tl
                x = XB[:, t.bk.i % 4, t.tl, :]
                need(V, t.rx, free.get("junk"), t_w[1])
                ts = tick(V.tensor_scalar(zx[:, :], x, mvx[:, n, 0:1], rsx[:, n:n + 1], ALU.subtract, ALU.mult), "v.s")
                for r in range(2):
                    need(V, ts)
                    ts = tick(V.tensor_tensor_reduce(junk[:, :], zx[:, :], rt[:, r, :], 1.0, 0.0, ALU.mult, ALU.add,
                                                     scol[:, r, n:n + 1]), "v.s")
                free["junk"] = [ts]
                s_tok[:] = [ts]
                free["x"].setdefault(t.bk.i, []).extend([x3_tok[n], ts])

            x3_tok = {}
            units = [(0, 0), (0, 1)]
            for i in range(NB):
                units.append((1, i))
                if i + 2 < NB:
                    units.append((0, i + 2))
            for i in range(NB):
                blks[i] = Blk()
                blks[i].i, blks[i].new = i, [None] * 4
            seq = []
            for L, i in units:
                for tl in range(4):
                    t = Tile()
                    t.L, t.bk, t.tl, t.b = L, blks[i], tl, i // 4
                    t.lastkv = tl == 3 and i % 4 == 3
                    seq.append(t)
            bg = Later()
            made = {}

            def queue_first(i):
                if i % 4 == 0:
                    bg.add(load_kv(0, i // 4))
                blks[i].ready = [t_x[i]] * 4
                if i == 2:
                    bg.finish(made_kv)
                if 3 <= i + 1 < NB:
                    t_x[i + 1] = load_x(i + 1)
                made[0, i] = bg.add(prep(i, 0, bo[0][:, :], t_w[0], qproj(0)))

            def queue_second(i):
                if i % 4 == 0:
                    bg.add(load_kv(1, i // 4), 1)
                bg.add(prep(i, 0, cF[:, :], t_cF, ffn), 1)
                made[1, i] = bg.add(prep(i, 1, bo[1][:, :], t_w[1], qproj(1)), 1)

            queue_first(0)
            bg.finish(made[0, 0])
            bg.add(setup_kv(1), 1)

            def free_wkv():
                free["x"][-2], free["x"][-1] = [f_kv["k"]], [f_kv["v"]]
                t_x[2] = load_x(2)
                Hs.give(0, *f_kv["stage"])
                Hs.give(1, *f_kv["stage"])
                yield

            made_kv = bg.add(free_wkv(), 1)
            for n in range(len(seq) + 3):
                cur = seq[n] if n < len(seq) else None
                p1 = seq[n - 1] if 1 <= n <= len(seq) else None
                p2 = seq[n - 2] if 2 <= n < len(seq) + 2 else None
                if n >= 3:
                    route_scores(seq[n - 3])
                if cur is not None:
                    if cur.tl == 0:
                        bg.finish(made[cur.L, cur.bk.i])
                        if n // 4 + 1 < len(units) and units[n // 4 + 1][0] == 0:
                            queue_first(units[n // 4 + 1][1])
                    scores(cur, (0,))
                if cur is not None:
                    scores(cur, (1,))
                if p2 is not None:
                    otrans(p2)
                if p1 is not None:
                    ptrans(p1, 0)
                if cur is not None:
                    scores(cur, (2,))
                if p1 is not None:
                    ptrans(p1, 1)
                if cur is not None:
                    scores(cur, (3,))
                bg.piece()
                if p1 is not None:
                    ptrans(p1, 2)
                bg.piece()
                if p1 is not None:
                    ptrans(p1, 3)
                if p2 is not None:
                    wo(p2, 0)
                    wo(p2, 1)
                    if p2.L == 0 and p2.tl == 3:
                        queue_second(p2.bk.i)
                bg.piece()
                if p1 is not None:
                    pv(p1, 0)
                bg.piece()
                if p1 is not None:
                    pv(p1, 1)
                if cur is not None:
                    softexp(cur)
                bg.piece()
                bg.piece()
            bg.drain()
            done = fl.all()
        for e in (PE, V, A, G, SY):
            need(e, done)
        if "B" not in parts:
            return
        with ExitStack() as pb:
            sb = alloc(pb)
            Wl = sb("Wl", [128, 4, 3 * D])
            Wlo = sb("Wlo", [128, 4, D])
            bl = sb("bl", [128, 8])
            bvl = sb("bvl", [128, D])
            msk = sb("msk", [128, 3, 256])
            nulq = sb("nulq", [128, D])
            lnwb = sb("lnwb", [128, 8])
            XL = sb("XL", [128, 12, D])
            xU = sb("xU", [128, 4, 576])
            QU = sb("QU", [128, 3, 4, D])
            KU = sb("KU", [128, 3, 4, 640])
            VU = sb("VU", [128, 12, 8, 65])
            Sw = sb("Sw", [128, 2, 2048])
            PU = sb("PU", [128, 16, 128])
            mw = sb("mw", [128, 2, 8])
            yo = sb("yo", [128, 2, D])
            route = sb("route", [128, 4, 128])
            sr, zr, er = route[:, 0, :], route[:, 1, :], route[:, 2, :]
            junk2 = route[:, :, :].rearrange("p a b -> p (a b)").bitcast(mybir.dt.uint8)
            rcol = sb("rcol", [128, 16])
            comb = sb("comb", [128, NT])
            idxf = sb("idxf", [128, 24])
            cb = sb("cb", [128, S])
            QUs, KUs, VUs, Sws, SPs, Yos = Slots(3), Slots(3), Slots(12), Slots(2), Slots(2), Slots(2)
            free = {"PU": []}

            load(Wl[:, :, :], a["wqkv"], "ld.wl")
            load(lnwb[:, :], a["lnwb"], "ld.wl")
            t_wl = load(grp[:, :], a["c_grp"], "ld.wl")
            load(Wlo[:, :, :], a["wlo"], "ld.wl2")
            load(msk[:, :, :], a["c_mask"], "ld.wl2")
            load(tri[:, :], a["c_tri"], "ld.wl2")
            t_wl2 = load(nulq[:, :], a["nulq"], "ld.wl2")
            xt = {}
            xlfree = {}

            def load_xl(n):
                k = n % 12
                need(SY, xlfree.get(n - 12))
                xt[n] = load(XL[:, k, :], X3d[128 * n:128 * n + 128, :], f"ld.xl{k}")

            for n in range(8):
                load_xl(n)
            tz = tick(V.memset(VU[:, :, :, :], 1.0), "v.setup2")
            need(V, t_wl)
            for k in range(4):
                tl_ = tick(V.tensor_copy(Sw[:, 0, 128 * k:128 * k + 128], lnwb[:, 4 + k:5 + k].broadcast_to([128, 128])), "v.setup2")
            km, w = Ms.take()
            need(PE, tl_, t_wl)
            tok = tick(mms(psM[:, km, :], [(Sw[:, 0, 128 * k:128 * k + 128], Wl[:, k, 2 * D:3 * D]) for k in range(4)], w),
                       "pe.setup2")
            need(V, tok)
            t_bv = tick(V.tensor_copy(bvl[:, :], psM[:, km, :]), "v.setup2")
            Ms.give(km, t_bv)
            km, w = Ms.take()
            need(PE, w)
            for c in range(8):
                for k in range(4):
                    m = PE.matmul(psM[:, km, c:c + 1], Wl[:, k, 128 * c:128 * c + 128], lnwb[:, 4 + k:5 + k],
                                  start=(k == 0), stop=(k == 3))
            tok = tick(m, "pe.setup2")
            need(V, tok)
            t_bl = tick(V.tensor_scalar(bl[:, 0:4], psM[:, km, 0:4], 0.125, None, ALU.mult), "v.setup2")
            t_bl = tick(V.tensor_copy(bl[:, 4:8], psM[:, km, 4:8]), "v.setup2")
            Ms.give(km, t_bl)
            for k in range(4):
                t_wls = tick(V.tensor_scalar(Wl[:, k, :], Wl[:, k, :], lnwb[:, k:k + 1], None, ALU.mult), "v.setup2")

            tok = tick(V.tensor_tensor(comb[:, :], rsx[:, :], rsx[:, :], ALU.mult), "v.setup2")
            need(V, tok)
            tok = tick(V.tensor_tensor(comb[:, :], comb[:, :], mvx[:, :, 1], ALU.mult), "v.setup2")
            need(V, tok)
            tok = tick(V.tensor_scalar(comb[:, :], comb[:, :], 1e-5, None, ALU.add), "v.setup2")
            need(G, tok)
            tok = tick(G.tensor_tensor(comb[:, :], comb[:, :], mhalf[:, 0:1].broadcast_to([128, NT]), ALU.pow), "g.comb")
            need(V, tok)
            t_comb = tick(V.tensor_tensor(comb[:, :], comb[:, :], rsx[:, :], ALU.mult), "v.setup2")
            xu = {"read": [], "tail": None}
            vt = {}
            blocks = {}

            def prep_b(bi):
                i = bi % 4
                o = {}
                blocks[bi] = o
                need(G, xu["read"], xu["tail"])
                if i == 0:
                    t_tail = tick(G.memset(xU[:, :, 0:64], 0.0), "g.tail")
                else:
                    t_tail = tick(G.tensor_copy(xU[:, :, 0:64], xU[:, :, 512:576]), "g.tail")
                def ln(n):
                    kn, w = Xn.take()
                    need(V, w, t_comb, xt[n])
                    return kn, tick(V.tensor_scalar(xn[:, kn, :], XL[:, n % 12, :], mvx[:, n, 0:1], comb[:, n:n + 1],
                                                    ALU.subtract, ALU.mult), "v.lnapply")

                nxt = ln(4 * bi)
                yield
                for t in range(4):
                    kn, tn = nxt
                    nxt = ln(4 * bi + t + 1) if t < 3 else None
                    te = turn4(xn[:, kn, :], tn, lambda tok, kn=kn: Xn.give(kn, tok),
                               xU[:, :, 64 + 128 * t:192 + 128 * t], [t_tail] + xu["read"], "xT")
                    yield
                xu["tail"] = te
                yield
                kq, wq_ = QUs.take()
                for c in range(4):
                    km, w = Ms.take()
                    need(PE, te, t_wls)
                    tok = tick(mms(psM[:, km, :], [(Wl[:, k, 128 * c:128 * c + 128], xU[:, k, 64:576])
                                                   for k in range(4)], w), "pe.Q")
                    need(A, tok, wq_, t_bl)
                    tq = tick(A.activation(QU[:, kq, c, :], psM[:, km, :], ACT.Identity, bias=bl[:, c:c + 1],
                                           scale=0.125), "a.Q")
                    Ms.give(km, tq)
                    yield
                kk, wk_ = KUs.take()
                for c in range(4):
                    km, w = Ms.take()
                    need(PE, w)
                    tok = tick(mms(psM[:, km, :], [(Wl[:, k, D + 128 * c:D + 128 * c + 128], xU[:, k, 64:576])
                                                   for k in range(4)], w), "pe.K")
                    need(A, tok, wk_)
                    tk = tick(A.activation(KU[:, kk, c, 64:576], psM[:, km, :], ACT.Identity, bias=bl[:, 4 + c:5 + c]),
                              "a.K")
                    Ms.give(km, tk)
                    yield
                need(G, tk, wk_)
                if i == 0:
                    te1 = tick(G.memset(KU[:, kk, :, 0:64], 0.0), "g.edge")
                else:
                    pk = blocks[bi - 1]["k"]
                    tick(G.tensor_copy(KU[:, pk, :, 576:640], KU[:, kk, :, 64:128]), "g.edge")
                    te1 = tick(G.tensor_copy(KU[:, kk, :, 0:64], KU[:, pk, :, 512:576]), "g.edge")
                    blocks[bi - 1]["tk"].append(te1)
                if i == 3:
                    te1 = tick(G.memset(KU[:, kk, :, 576:640], 0.0), "g.edge")
                o["tk"] = [tk, te1]
                o["q"], o["tq"], o["k"] = kq, tq, kk
                for j in range(5 if i == 3 else 4):
                    M = 128 if j < 4 else 64
                    kv_, wv_ = VUs.take()
                    km, w = Ms.take()
                    need(PE, te, t_tail)
                    tok = tick(mms(psM[0:M, km, :], [(xU[:, k, 128 * j:128 * j + M], Wl[:, k, 2 * D:3 * D])
                                                     for k in range(4)], w), "pe.V")
                    need(V, tok, wv_, t_bv, tz)
                    tv = tick(V.tensor_tensor(VU[0:M, kv_, :, 0:64],
                                              psM[0:M, km, :].rearrange("p (h d) -> p h d", h=8),
                                              bvl[0:M, :].rearrange("p (h d) -> p h d", h=8), ALU.add), "v.V")
                    Ms.give(km, tv)
                    vt[bi // 4, 4 * i + j] = (kv_, tv)
                    yield
                xu["read"] = [tok]

            class W:
                pass

            def scores_b(t, p):
                o = blocks[t.n // 4]
                tl = t.n % 4
                if p == 0:
                    t.s, t.ws = Sws.take()
                w_s = t.ws
                which = 1 if t.n % 16 == 0 else 2 if t.n % 16 == 15 else 0
                ks, w = SPs.take()
                need(PE, w, o["tq"], o["tk"])
                for k in range(2):
                    c = 2 * p + k
                    for h in range(2):
                        m = PE.matmul(psS[:, 2 * ks + h, 256 * k:256 * k + 256],
                                      QU[64 * h:64 * h + 64, o["q"], c, 128 * tl:128 * tl + 128],
                                      KU[64 * h:64 * h + 64, o["k"], c, 128 * tl:128 * tl + 256],
                                      start=True, stop=True)
                t.tq = tick(m, "pe.S")
                need(V, t.tq, w_s, t_wl2)
                tok = tick(V.tensor_tensor(Sw[:, t.s, 1024 * p:1024 * p + 1024].rearrange("p (j n) -> p j n", j=4),
                                           psS[:, 2 * ks:2 * ks + 2, :].rearrange("p b (k n) -> p (b k) n", k=2),
                                           mid(msk[:, which, :], 4), ALU.add), "v.Sadd")
                SPs.give(ks, tok)
                if p == 0:
                    return
                if tl == 3:
                    QUs.give(o["q"], t.tq)
                    KUs.give(o["k"], t.tq)
                sv = Sw[:, t.s, :].rearrange("p (h n) -> p h n", h=8)
                need(V, tok)
                tok = tick(V.tensor_reduce(mw[:, t.s, :], sv, X, ALU.max), "v.max")
                need(G, tok)
                t.sub = tick(G.tensor_tensor(sv, sv, last(mw[:, t.s, :], 256), ALU.subtract), "g.sub")

            def exp_b(t):
                need(A, t.sub)
                t.exp = tick(A.activation(Sw[:, t.s, :], Sw[:, t.s, :], ACT.Exp), "a.exp")

            def ptrans_b(t, q):
                kt, w = Ts.take()
                need(PE, w, t.exp)
                for c in range(4):
                    o = 512 * q + 128 * c
                    m = PE.transpose(psT[:, kt, 128 * c:128 * c + 128], Sw[:, t.s, o:o + 128], ident[:, :])
                tok = tick(m, "pe.PT")
                if q == 3:
                    Sws.give(t.s, tok)
                need(A, tok, free["PU"])
                t.pt = tick(A.copy(PU[:, 4 * q:4 * q + 4, :], psT[:, kt, :].rearrange("p (c n) -> p c n", c=4)), "a.PT")
                Ts.give(kt, t.pt)

            def pv_b(t, p):
                b, j = t.n // 16, t.n % 16
                v0, v1 = vt[b, j], vt[b, j + 1]
                if p == 0:
                    t.o, t.wo_ = Ons.take()
                w_o = t.wo_
                km, w = Ms.take()
                need(PE, w, t.pt, v0[1], v1[1])
                for jj in range(4):
                    bank, k = jj % 2, jj // 2
                    pos = 4 * p + 2 * bank + k
                    for ck, v in ((0, v0), (1, v1)):
                        m = PE.matmul(psM[:, km, 65 * jj:65 * jj + 65], PU[:, 2 * pos + ck, :],
                                      VU[:, v[0], 4 * p + jj, :], start=(ck == 0), stop=(ck == 1))
                tok = tick(m, "pe.PV")
                ov = psM[:, km, 0:260].rearrange("p (h e) -> p h e", e=65)
                kr, wr = Rc.take()
                need(V, tok, w_o, wr)
                tr = tick(V.reciprocal(rc[:, kr, 0:4], ov[:, :, 64]), "v.rc")
                need(V, tr)
                t.on = tick(V.tensor_tensor(On[:, t.o, 256 * p:256 * p + 256].rearrange("p (h d) -> p h d", h=4),
                                            ov[:, :, 0:64], last(rc[:, kr, 0:4], 64), ALU.mult), "v.On")
                Rc.give(kr, t.on)
                Ms.give(km, t.on)
                if p == 0:
                    return
                free["PU"] = [tok]
                VUs.give(v0[0], tok)
                if j == 15:
                    VUs.give(v1[0], tok)

            def wo_b(t, part):
                if part == 0:
                    t.km, w = Ms.take()
                    need(PE, w, t.te, t_wl2)
                km = t.km
                for c in (2 * part, 2 * part + 1):
                    m = PE.matmul(psM[:, km, :], OT[:, t.ot, c, :], Wlo[:, c, :], start=(c == 0), stop=(c == 3))
                if part == 0:
                    return
                tok = tick(m, "pe.Wo")
                OTs.give(t.ot, tok)
                x = XL[:, t.n % 12, :]
                need(V, tok)
                ty = tick(V.tensor_tensor(x, psM[:, km, :], x, ALU.add), "v.y")
                Ms.give(km, ty)
                need(SY, ty)
                t_st = tick(SY.dma_start(Yd[128 * t.n:128 * t.n + 128, :], x), f"st.y{t.n % 12}", 16)
                ko, w = Yos.take()
                need(G, ty, w, t_wl2)
                to = tick(G.tensor_tensor(yo[:, ko, :], x, nulq[:, :], ALU.add), "g.yo")
                need(SY, to)
                Yos.give(ko, tick(SY.dma_start(out[128 * t.n:128 * t.n + 128, :], yo[:, ko, :]), f"st.o{ko}", 16))
                xlfree[t.n] = [t_st, to]

            idx_tok = {}

            def routing():
                kt, w = Ts.take()
                need(PE, w, s_tok, t_ident)
                tok = tick(PE.transpose(psT[:, kt, 0:128], scol[:, :, :].rearrange("p r n -> p (r n)"), ident[:, :]), "pe.rt")
                need(V, tok)
                tok = tick(V.tensor_copy(sr[:, :], psT[:, kt, 0:128]), "v.rt")
                Ts.give(kt, tok)
                need(V, tok)
                tok = tick(V.tensor_reduce(rcol[:, 0:1], sr[:, :], X, ALU.max), "v.rt")
                smax, na, M, part, lnv, T, cand, dd, sel = (rcol[:, i:i + 1] for i in (1, 2, 3, 4, 5, 6, 7, 8, 9))
                logk, kcol = cols[:, 4:5], cols[:, 5:6]
                yield
                kt, w = Ts.take()
                need(PE, w, tok)
                tok = tick(PE.transpose(psT[0:1, kt, 0:128], rcol[:, 0:1], ident[:, :]), "pe.rt")
                need(V, tok)
                tok = tick(V.tensor_reduce(er[0:1, 0:8], psT[0:1, kt, 0:128].rearrange("o (g i) -> o g i", i=16), X,
                                           ALU.max), "v.rt")
                Ts.give(kt, tok)
                need(V, tok)
                tok = tick(V.tensor_copy(zr[0:1, :].rearrange("o (g i) -> o g i", i=16), last(er[0:1, 0:8], 16)), "v.rt")
                yield
                kt, w = Ts.take()
                need(PE, w, tok)
                tok = tick(PE.matmul(psT[:, kt, 0:1], zr[0:1, :], ident[0:1, 0:1], start=True, stop=True), "pe.rt")
                need(V, tok)
                tok = tick(V.tensor_copy(smax, psT[:, kt, 0:1]), "v.rt")
                Ts.give(kt, tok)
                tok2 = tick(V.tensor_scalar(na, logk, -1.0, math.log(S), ALU.mult, ALU.add), "v.rt")
                need(V, tok, tok2)
                yield
                for it in range(1, ITERS):
                    tok = tick(V.tensor_tensor(M, smax, na, ALU.min), "v.rt")
                    need(V, tok)
                    tok = tick(V.tensor_scalar(zr[:, :], sr[:, :], na, M, ALU.min, ALU.subtract), "v.rt")
                    need(A, tok)
                    yield
                    te = tick(A.activation(er[:, :], zr[:, :], ACT.Exp, accum_out=part), "a.rt")
                    yield
                    km, w = Ms.take()
                    need(PE, te, w)
                    tok = tick(PE.matmul(psM[:, km, 0:1], grp[:, :], part, start=True, stop=True), "pe.rt")
                    need(A, tok)
                    tl2 = tick(A.activation(lnv, psM[:, km, 0:1], ACT.Ln), "a.rt")
                    Ms.give(km, tl2)
                    yield
                    need(V, tl2)
                    tok = tick(V.tensor_scalar(na, lnv, M, logk, ALU.add, ALU.subtract), "v.rt")
                    need(V, tok)
                tok = tick(V.tensor_scalar(zr[:, :], sr[:, :], na, None, ALU.subtract), "v.rt")
                need(V, tok)
                tok = tick(V.tensor_scalar(er[:, :], zr[:, :], 0.0, None, ALU.max), "v.rt")
                need(V, tok)
                tok = tick(V.tensor_tensor(zr[:, :], zr[:, :], er[:, :], ALU.subtract), "v.rt")
                yield
                need(A, tok)
                tok = tick(A.activation(sr[:, :], zr[:, :], ACT.Exp), "a.rt")
                need(V, tok)
                yield
                tok = tick(V.memset(T, 0.0), "v.rt")
                for bit in range(29, -1, -1):
                    need(V, tok)
                    tok = tick(V.tensor_scalar(cand.bitcast(I32), T.bitcast(I32), 1 << bit, None, ALU.bitwise_or), "v.rt")
                    need(V, tok)
                    tok = tick(V.tensor_scalar(zr[:, :], sr[:, :], cand, 0.0, ALU.is_ge, ALU.add, accum_out=part), "v.rt")
                    tok2 = tick(V.tensor_tensor(dd, cand, T, ALU.subtract), "v.rt")
                    yield
                    km, w = Ms.take()
                    need(PE, tok, w)
                    tok = tick(PE.matmul(psM[:, km, 0:1], grp[:, :], part, start=True, stop=True), "pe.rt")
                    need(V, tok, tok2)
                    tok = tick(V.tensor_scalar(sel, psM[:, km, 0:1], kcol, None, ALU.is_ge), "v.rt")
                    Ms.give(km, tok)
                    need(V, tok)
                    tok = tick(V.scalar_tensor_tensor(T, dd, sel, T, ALU.mult, ALU.add), "v.rt")
                need(V, tok)
                tok = tick(V.tensor_scalar(zr[:, :], sr[:, :], T, 0.0, ALU.is_gt, ALU.add, accum_out=rcol[:, 10:11]), "v.rt")
                tok = tick(V.tensor_scalar(er[:, :], sr[:, :], T, 0.0, ALU.is_equal, ALU.add, accum_out=rcol[:, 11:12]),
                           "v.rt")
                yield
                km, w = Ms.take()
                need(PE, tok, w)
                PE.matmul(psM[:, km, 0:1], grp[:, :], rcol[:, 10:11], start=True, stop=True)
                tok = tick(PE.matmul(psM[:, km, 1:2], tri[:, :], rcol[:, 11:12], start=True, stop=True), "pe.rt")
                need(V, tok)
                tok = tick(V.tensor_scalar(rcol[:, 12:13], psM[:, km, 0:1], -1.0, kcol, ALU.mult, ALU.add), "v.rt")
                need(V, tok)
                tok = tick(V.tensor_tensor(rcol[:, 13:14], rcol[:, 12:13], psM[:, km, 1:2], ALU.subtract), "v.rt")
                Ms.give(km, tok)
                yield
                t1 = tick(V.memset(cb[:, 128:256], 1.0), "v.rt")
                need(V, t1)
                tok = tick(V.tensor_tensor_scan(cb[:, 0:128], cb[:, 128:256], er[:, :], 0.0, ALU.mult, ALU.add), "v.rt")
                need(V, tok)
                tok = tick(V.tensor_scalar(cb[:, 0:128], cb[:, 0:128], rcol[:, 13:14], None, ALU.is_le), "v.rt")
                need(V, tok)
                tok = tick(V.tensor_tensor(er[:, :], er[:, :], cb[:, 0:128], ALU.mult), "v.rt")
                need(V, tok)
                tok = tick(V.tensor_tensor(er[:, :], er[:, :], zr[:, :], ALU.add), "v.rt")
                need(V, tok)
                tok = tick(V.tensor_tensor_scan(cb[:, 0:128], cb[:, 128:256], er[:, :], 0.0, ALU.mult, ALU.add), "v.rt")
                t1 = tick(V.tensor_scalar(zr[:, :], sr[:, :], -1.0, 1.0, ALU.mult, ALU.add), "v.rt")
                need(V, t1, tok)
                tf = tick(V.tensor_tensor(zr[:, :], zr[:, :], sr[:, :], ALU.add), "v.rt")
                yield
                km, w = Ms.take()
                need(PE, tok, w)
                tok = tick(PE.matmul(psM[:, km, 0:1], tri[:, :], cb[:, 127:128], start=True, stop=True), "pe.rt")
                need(V, tok)
                tok = tick(V.tensor_scalar(er[:, :], cb[:, 0:128], psM[:, km, 0:1], None, ALU.add), "v.rt")
                Ms.give(km, tok)
                need(SY, tok, tf)
                tick(SY.dma_start(cumd.rearrange("g (i n) -> (g i) n", i=16), er[:, :]), "st.rt", 16)
                t_f = tick(SY.dma_start(fd.rearrange("(p n) o -> p (n o)", n=128), zr[:, :]), "st.rt", 16)
                need(SY, t_f, tok)
                yield
                tb = []
                for g in range(8):
                    r, b = g // 4, g % 4
                    need(SY, tb)
                    tl_ = load(cb[:, :], cumd[g:g + 1, :].broadcast_to([128, S]), "ld.cb")
                    yield
                    for j in range((2, 4)[r]):
                        c = (2 * b + j) if r == 0 else (8 + 4 * b + j)
                        need(V, tl_)
                        tok = tick(V.tensor_scalar(Jk, cb[:, :], cols[:, j:j + 1], 0.0, ALU.is_le, ALU.add,
                                                   accum_out=idxf[:, c:c + 1]), "v.idx")
                        tb = [tok]
                        need(V, tok)
                        yield
                    c0 = 2 * b if r == 0 else 8 + 4 * b
                    c1 = c0 + (2, 4)[r]
                    tok = tick(V.tensor_scalar(idxf[:, c0:c1], idxf[:, c0:c1], float(S * b), None, ALU.add), "v.idx")
                    need(V, tok)
                    tick(V.tensor_copy(idx[:, c0:c1], idxf[:, c0:c1]), "v.idx")
                    tok = tick(V.tensor_scalar(idxf[:, c0:c1], idxf[:, c0:c1], float(B * S * r), None, ALU.add), "v.idx")
                    need(V, tok)
                    tok = tick(V.tensor_copy(idxs[:, c0:c1], idxf[:, c0:c1]), "v.idx")
                    tb.append(tok)
                    idx_tok[0] = tok
                    yield

            Jk = junk2
            bg, rt_ = Later(), Later()
            rt_.add(routing())
            bg.add(prep_b(0))
            bg.drain()
            made = {1: bg.add(prep_b(1))}
            tiles = []
            for n in range(NT):
                t = W()
                t.n = n
                tiles.append(t)
            for n in range(8, 9):
                load_xl(n)
            for n in range(NT + 2):
                cur = tiles[n] if n < NT else None
                p1 = tiles[n - 1] if 1 <= n <= NT else None
                p2 = tiles[n - 2] if n >= 2 else None
                if cur is not None:
                    if n % 4 == 2:
                        bi = (n + 2) // 4
                        if bi < NB:
                            bg.finish(made[bi])
                        if bi + 1 < NB:
                            made[bi + 1] = bg.add(prep_b(bi + 1))
                    if n + 9 < NT:
                        load_xl(n + 9)
                    scores_b(cur, 0)
                if p2 is not None:
                    p2.ot, w = OTs.take()
                    p2.te = turn4(On[:, p2.o, :], p2.on, lambda tok: Ons.give(p2.o, tok), OT[:, p2.ot, :, :], w, "OT")
                rt_.piece()
                if cur is not None:
                    scores_b(cur, 1)
                if p1 is not None:
                    ptrans_b(p1, 0)
                bg.piece()
                rt_.piece()
                if p1 is not None:
                    ptrans_b(p1, 1)
                bg.piece()
                rt_.piece()
                if p1 is not None:
                    ptrans_b(p1, 2)
                if p2 is not None:
                    wo_b(p2, 0)
                if p1 is not None:
                    ptrans_b(p1, 3)
                if p2 is not None:
                    wo_b(p2, 1)
                bg.piece()
                rt_.piece()
                if p1 is not None:
                    pv_b(p1, 0)
                bg.piece()
                rt_.piece()
                if p1 is not None:
                    pv_b(p1, 1)
                if cur is not None:
                    exp_b(cur)
                bg.piece()
                rt_.piece()
            bg.drain()
            rt_.drain()
            done = fl.all()
        for e in (PE, V, A, G, SY):
            need(e, done)
        if "C" not in parts:
            return

        with ExitStack() as pc:
            sb = alloc(pc)
            Wh = sb("Wh", [128, 4, D])
            Wkv = sb("Wkv", [128, 4, 2 * D])
            Who = sb("Who", [128, 4, D])
            gam = sb("gam", [128, 4])
            nkb = sb("nkb", [128, 4, 8])
            nvb = sb("nvb", [128, 8, 65])
            XH = sb("XH", [128, 6, D])
            yg = sb("yg", [128, 2, 2, D])
            fg = sb("fg", [128, 2, 6])
            ss = sb("ss", [128, 2, 8])
            sq = sb("sq", [128, D])
            sth = sb("sth", [128, 6, 6])
            mvh = sb("mvh", [128, 6, 2])
            rsh = sb("rsh", [128, 6])
            xh = sb("xh", [128, 4, 768])
            QH = sb("QH", [128, 2, 4, 256])
            KH = sb("KH", [128, 2, 4, 512])
            VH = sb("VH", [128, 2, 4, 8, 65])
            PH = sb("PH", [128, 3, D])
            PTH = sb("PTH", [128, 2, 4, 128])
            sn = sb("sn", [128, 2, 8])
            nm = sb("nm", [128, 2, 8])
            m0 = sb("m0", [128, 2, 8])
            pn = sb("pn", [128, 2, 8])
            on2 = sb("on2", [128, 2, 4, 65])
            oh = sb("oh", [128, 2, D])
            half = sb("half", [128, 8])
            Bs, XHs, PHs, PTs, Qt, O2s, SHs, OHs = (Slots(2), Slots(6), Slots(3), Slots(2), Slots(2), Slots(2), Slots(3),
                                                    Slots(2))
            load(Wh[:, :, :], a["wh"], "ld.wh")
            load(Wkv[:, :, :], a["wkv"], "ld.wh")
            load(Who[:, :, :], a["who"], "ld.wh")
            load(nkb[:, :, :], a["nkb"], "ld.wh")
            load(nvb[:, :, :], a["nvb"], "ld.wh")
            t_wh = load(gam[:, :], a["gam"], "ld.wh")
            t_half = tick(G.memset(half[:, :], 0.5), "g.half")
            tzh = tick(V.memset(VH[:, :, :, :, :], 1.0), "v.setup3")
            need(V, t_wh)
            for k in range(4):
                tick(V.tensor_scalar(Wh[:, k, :], Wh[:, k, :], gam[:, k:k + 1], None, ALU.mult), "v.setup3")
                t_g = tick(V.tensor_scalar(Wkv[:, k, :], Wkv[:, k, :], gam[:, k:k + 1], None, ALU.mult), "v.setup3")
            xhr = {"read": []}
            hb = {}

            def gather(dst, src, col, name):
                return tick(G.indirect_dma_start(dst, None, src, bass.IndirectOffsetOnAxis(col, 0)), name, 16)

            def prep_c(b):
                o = {}
                hb[b] = o
                k, wb = Bs.take()
                o["k"] = k
                ci = [2 * b, 2 * b + 1] + [8 + 4 * b + j for j in range(4)]
                need(G, wb)
                o["f"], o["y"] = [], []
                slots = []
                for j in range(6):
                    kx, w = XHs.take()
                    need(G, w)
                    tg = gather(XH[:, kx, :], X3d, idx[:, ci[j]:ci[j] + 1], f"gx{kx}")
                    tf = gather(fg[:, k, j:j + 1], fd, idxs[:, ci[j]:ci[j] + 1], f"gf{k}{j}")
                    o["f"].append(tf)
                    slots.append((kx, tg))
                    if j < 2:
                        o["y"].append(gather(yg[:, k, j, :], Yd, idx[:, ci[j]:ci[j] + 1], f"gy{k}{j}"))
                yield
                need(V, wb)
                for j, (kx, tg) in enumerate(slots):
                    need(V, tg)
                    tok = tick(V.bn_stats(sth[:, j, :], XH[:, kx, :]), "v.bnstats")
                need(V, tok)
                for j in range(6):
                    tok = tick(V.bn_aggr(mvh[:, j, :], sth[:, j, :]), "v.bnaggr")
                need(V, tok)
                tok = tick(V.tensor_scalar(rsh[:, :], mvh[:, :, 1], 1e-5, None, ALU.add), "v.vareps")
                need(G, tok)
                t_rs = tick(G.tensor_tensor(rsh[:, :], rsh[:, :], mhalf[:, 0:6], ALU.pow), "g.rstd")
                yield
                need(V, t_rs)
                for j, (kx, tg) in enumerate(slots):
                    slots[j] = (kx, tick(V.tensor_scalar(XH[:, kx, :], XH[:, kx, :], mvh[:, j, 0:1], rsh[:, j:j + 1],
                                                         ALU.subtract, ALU.mult), "v.zh"))
                yield
                need(A, wb)
                for j, (kx, tg) in enumerate(slots):
                    need(A, tg, ta if j else None)
                    ta = tick(A.activation(sq[:, :], XH[:, kx, :], ACT.Square, accum_out=ss[:, k, j:j + 1]), "a.sq")
                need(G, ta, t_half)
                tok = tick(G.tensor_tensor(ss[:, k, 0:6], ss[:, k, 0:6], half[:, 0:6], ALU.pow), "g.norm")
                need(V, tok)
                tok = tick(V.tensor_scalar(ss[:, k, 0:6], ss[:, k, 0:6], 1e-12, None, ALU.max), "v.norm")
                need(V, tok)
                tok = tick(V.reciprocal(ss[:, k, 0:6], ss[:, k, 0:6]), "v.norm")
                need(V, tok)
                t_n = tick(V.tensor_scalar(ss[:, k, 0:6], ss[:, k, 0:6], math.sqrt(float(D)), None, ALU.mult), "v.norm")
                yield
                for j, (kx, tg) in enumerate(slots):
                    kn, w = Xn.take()
                    need(V, w, t_n, tg)
                    tn = tick(V.tensor_scalar(xn[:, kn, :], XH[:, kx, :], ss[:, k, j:j + 1], None, ALU.mult), "v.rms")
                    XHs.give(kx, tn)
                    te = turn4(xn[:, kn, :], tn, lambda tok, kn=kn: Xn.give(kn, tok),
                               xh[:, :, 128 * j:128 * j + 128], xhr["read"], "xT")
                    yield
                for c in range(4):
                    km, w = Ms.take()
                    need(PE, te, t_g)
                    tok = tick(mms(psM[:, km, 0:256], [(Wh[:, i, 128 * c:128 * c + 128], xh[:, i, 0:256])
                                                       for i in range(4)], w), "pe.Q")
                    need(A, tok, wb)
                    o["tq"] = tick(A.mul(QH[:, k, c, :], psM[:, km, 0:256], 0.125), "a.Q")
                    Ms.give(km, o["tq"])
                    yield
                for c in range(4):
                    km, w = Ms.take()
                    tok = tick(mms(psM[:, km, :],
                                   [(Wkv[:, i, 128 * c:128 * c + 128],
                                     xh[:, i, 256:768]) for i in range(4)], w), "pe.K")
                    need(A, tok, wb)
                    o["tk"] = tick(A.copy(KH[:, k, c, :], psM[:, km, :]), "a.K")
                    Ms.give(km, o["tk"])
                    yield
                for j in range(4):
                    km, w = Ms.take()
                    tok = tick(mms(psM[:, km, :],
                                   [(xh[:, i, 256 + 128 * j:384 + 128 * j],
                                     Wkv[:, i, D:2 * D]) for i in range(4)], w),
                               "pe.V")
                    need(V, tok, wb, tzh, o["f"])
                    o["tv"] = tick(V.tensor_scalar(VH[:, k, j, :, 0:64], psM[:, km, :].rearrange("p (h d) -> p h d", h=8),
                                                   fg[:, k, 2 + j:3 + j], None, ALU.mult), "v.V")
                    Ms.give(km, o["tv"])
                    yield
                xhr["read"] = [tok]

            def null_scores(b, qt):
                o = hb[b]
                kq, w_q = Qt.take()
                km, w = Ms.take()
                need(PE, o["tq"], t_wh)
                tok = tick(mms(psM[:, km, 0:8], [(QH[:, o["k"], c, 128 * qt:128 * qt + 128], nkb[:, c, :])
                                                 for c in range(4)], w), "pe.sn")
                need(V, tok, w_q)
                tsn = tick(V.tensor_copy(sn[:, kq, :], psM[:, km, 0:8]), "v.sn")
                Ms.give(km, tsn)
                return kq, tsn

            class H:
                pass

            def scores_c(t):
                o, k = hb[t.b], hb[t.b]["k"]
                if t.h == 0:
                    t.g.kq, t.g.tsn = null_scores(t.b, t.qt)
                kq = t.g.kq
                ks, w = SHs.take()
                need(PE, w, o["tq"], o["tk"])
                p0, c = 64 * (t.h % 2), t.h // 2
                t.tq = tick(PE.matmul(psS[:, ks, :], QH[p0:p0 + 64, k, c, 128 * t.qt:128 * t.qt + 128],
                                      KH[p0:p0 + 64, k, c, :], start=True, stop=True), "pe.S")
                need(V, t.tq, t.g.tsn)
                tok = tick(V.tensor_reduce(m0[:, kq, t.h:t.h + 1], psS[:, ks, :], X, ALU.max), "v.max")
                need(V, tok)
                tok = tick(V.tensor_scalar(nm[:, kq, t.h:t.h + 1], m0[:, kq, t.h:t.h + 1], sn[:, kq, t.h:t.h + 1], -1.0,
                                           ALU.max, ALU.mult), "v.nm")
                t.g.tnm = tok
                t.p, w = PHs.take()
                need(A, tok, w)
                t.exp = tick(A.activation(PH[:, t.p, :], psS[:, ks, :], ACT.Exp, bias=nm[:, kq, t.h:t.h + 1]), "a.exp")
                SHs.give(ks, t.exp)
                if t.h % 4 == 3:
                    q = slice(t.h - 3, t.h + 1)
                    need(V, tok)
                    tok = tick(V.tensor_tensor(pn[:, kq, q], sn[:, kq, q], nm[:, kq, q], ALU.add), "v.pn")
                    need(A, tok)
                    t.g.tpn = tick(A.activation(pn[:, kq, q], pn[:, kq, q], ACT.Exp), "a.pn")

            def trans_c(t):
                kt, w = Ts.take()
                need(PE, w, t.exp)
                for c in range(4):
                    m = PE.transpose(psT[:, kt, 128 * c:128 * c + 128], PH[:, t.p, 128 * c:128 * c + 128], ident[:, :])
                tok = tick(m, "pe.PT")
                PHs.give(t.p, tok)
                t.pt, w = PTs.take()
                need(A, tok, w)
                t.tp = tick(A.copy(PTH[:, t.pt, :, :], psT[:, kt, :].rearrange("p (c n) -> p c n", c=4)), "a.PT")
                Ts.give(kt, t.tp)

            def pv_c(t):
                o, k = hb[t.b], hb[t.b]["k"]
                g = t.g
                if t.h % 4 == 0:
                    _, w = Oh.take()
                    need(PE, w)
                j = t.h % 4
                need(PE, t.tp, o["tv"])
                for c in range(4):
                    m = PE.matmul(psS[:, 3, 65 * j:65 * j + 65], PTH[:, t.pt, c, :], VH[:, k, c, t.h, :],
                                  start=(c == 0), stop=(c == 3))
                tok = tick(m, "pe.PV")
                PTs.give(t.pt, tok)
                if j < 3:
                    return
                p = t.h // 4
                if p == 0:
                    g.o, w = Ons.take()
                    need(V, w)
                k2, w = O2s.take()
                need(V, g.tpn, w, tok)
                tk = tick(V.tensor_tensor(on2[:, k2, :, :], nvb[:, 4 * p:4 * p + 4, :], last(pn[:, g.kq, 4 * p:4 * p + 4], 65),
                                          ALU.mult), "v.on2")
                need(V, tk)
                tk = tick(V.tensor_tensor(on2[:, k2, :, :], psS[:, 3, 0:260].rearrange("p (h e) -> p h e", e=65),
                                          on2[:, k2, :, :], ALU.add), "v.on2")
                Oh.give(0, tk)
                kr, w = Rc.take()
                need(V, tk, w)
                tk = tick(V.reciprocal(rc[:, kr, 0:4], on2[:, k2, :, 64]), "v.rc")
                need(V, tk)
                g.on = tick(V.tensor_tensor(On[:, g.o, 256 * p:256 * p + 256].rearrange("p (h d) -> p h d", h=4),
                                            on2[:, k2, :, 0:64], last(rc[:, kr, 0:4], 64), ALU.mult), "v.On")
                Rc.give(kr, g.on)
                O2s.give(k2, g.on)
                if p == 1:
                    Qt.give(g.kq, g.on)

            def out_c(g):
                o, k = hb[g.b], hb[g.b]["k"]
                ot, w = OTs.take()
                te = turn4(On[:, g.o, :], g.on, lambda tok: Ons.give(g.o, tok), OT[:, ot, :, :], w, "OT")
                km, w = Ms.take()
                need(PE, te)
                tok = tick(mms(psM[:, km, :], [(OT[:, ot, c, :], Who[:, c, :]) for c in range(4)], w), "pe.Wo")
                OTs.give(ot, tok)
                ko, w = OHs.take()
                need(V, tok, w, o["f"], o["y"])
                th = tick(V.scalar_tensor_tensor(oh[:, ko, :], psM[:, km, :], fg[:, k, g.qt:g.qt + 1], yg[:, k, g.qt, :],
                                                 ALU.mult, ALU.add), "v.oh")
                Ms.give(km, th)
                need(G, th)
                c = 2 * g.b + g.qt
                ts = tick(G.indirect_dma_start(out, bass.IndirectOffsetOnAxis(idx[:, c:c + 1], 0), oh[:, ko, :], None),
                          f"sc{ko}", 16)
                OHs.give(ko, ts)
                if g.qt == 1:
                    Bs.give(k, g.last, th)

            Oh = Slots(1)
            bg = Later()
            bg.add(prep_c(0))
            bg.drain()
            made = {}
            seq = []
            for b in range(B):
                for qt in range(2):
                    g = H()
                    g.b, g.qt = b, qt
                    for h in range(8):
                        t = H()
                        t.g, t.b, t.qt, t.h = g, b, qt, h
                        seq.append(t)
            for n in range(len(seq) + 5):
                if n < len(seq):
                    t = seq[n]
                    if t.qt == 0 and t.h == 0:
                        if t.b:
                            bg.finish(made[t.b])
                    if t.qt == 0 and t.h == 5 and t.b + 1 < B:
                        made[t.b + 1] = bg.add(prep_c(t.b + 1))
                    scores_c(t)
                bg.piece()
                if 2 <= n < len(seq) + 2:
                    trans_c(seq[n - 2])
                bg.piece()
                if 3 <= n < len(seq) + 3:
                    t = seq[n - 3]
                    pv_c(t)
                    if t.h == 7:
                        t.g.last = ("pe.PV", fl.val["pe.PV"])
                if 4 <= n < len(seq) + 4 and seq[n - 4].h == 7:
                    out_c(seq[n - 4].g)
            done = fl.all()
        for e in (PE, V, A, G, SY):
            need(e, done)


def wT(w, np):
    w = np.asarray(w)
    o, i = w.shape
    return np.ascontiguousarray(w.T.reshape(i // 128, 128, o).transpose(1, 0, 2))


def rows(v, np, n=128):
    return np.ascontiguousarray(np.broadcast_to(np.asarray(v)[None], (n, v.shape[0])))


def layout(inp, np):
    g = {k: np.asarray(v) for k, v in inp.items()}
    d = {}
    col = lambda v: v.reshape(4, 128).T
    d["x"] = g["x"].reshape(B * S, D)
    for L in (0, 1):
        p = f"L{L}_xcond_"
        for w in "qkvo":
            d[f"w{w}{L}"] = wT(g[p + "W" + w], np)
        d[f"bo{L}"] = rows(g[p + "bo"], np)
        d[f"bv{L}"] = rows(g[p + "bv"], np, NK)
    d["bq"] = np.ascontiguousarray(np.stack([col(g["L0_xcond_bq"]), col(g["L1_xcond_bq"])], 1))
    kc = np.zeros((128, 16), np.float32)
    kc[:, 0:4], kc[:, 4:8] = col(g["L0_xcond_bk"]), col(g["L1_xcond_bk"])
    kc[:, 8:12] = g["condB_tau"][None]
    d["kcol"] = kc
    d["delta"] = np.ascontiguousarray(np.broadcast_to(g["fside_BxS2_0"][None], (128, B, NK)))
    d["ctxT"] = np.ascontiguousarray(g["ctx_1024"].reshape(B * NK, 4, 128).transpose(2, 1, 0))
    d["win"] = wT(np.concatenate([g["L0_ffn_Win"].T] * 2, 0), np)
    d["wout"] = np.concatenate([g["L0_ffn_Wout"]] * 2, 0)
    d["bout"] = rows(g["L0_ffn_bout"], np)
    pair = lambda w: w.reshape(64, 8, 2).transpose(2, 0, 1).reshape(128, 8)
    fc = np.zeros((128, 32), np.float32)
    fc[:, 0:8], fc[:, 8:16], fc[:, 16:24] = pair(g["L0_ffn_W1"]), pair(g["L0_ffn_b1"]), pair(g["L0_ffn_W2"])
    fc[:, 24] = np.concatenate([g["L0_ffn_bin_"]] * 2)
    fc[:, 25] = np.concatenate([g["L0_ffn_b2"]] * 2)
    d["fcol"] = fc
    d["rt"] = np.ascontiguousarray(np.broadcast_to(
        np.stack([g["L1_ffn_rt_q"][0], g["L1_ffn_rt_kv"][0]])[None], (128, 2, D)))
    d["c_ident"] = np.eye(128, dtype=np.float32)
    p = np.arange(128)
    d["c_grp"] = (p[:, None] // 16 == p[None] // 16).astype(np.float32)
    d["c_tri"] = ((p[:, None] // 16 == p[None] // 16) & (p[:, None] < p[None])).astype(np.float32)
    cols = np.zeros((128, 16), np.float32)
    for j in range(4):
        cols[:, j] = p + 128 * j
    cols[:, 4] = np.where(p < 64, LOGK[0], LOGK[1])
    cols[:, 5] = np.where(p < 64, NQ, NKV)
    d["cols"] = cols
    d["wqkv"] = wT(g["L1_ffn_Wqkv"], np)
    d["wlo"] = wT(g["L1_ffn_Wout_l"], np)
    d["lnwb"] = np.ascontiguousarray(np.concatenate([col(g["L1_ffn_ln_w"]), col(g["L1_ffn_ln_b"])], 1))
    d["nulq"] = rows(g["L1_ffn_null_q"], np)
    m = np.zeros((128, 3, 256), np.float32)
    m[:64, :, 192:] = -1e30
    m[64:, :, :64] = -1e30
    m[:, 1, :64] = -1e30
    m[:, 2, 192:] = -1e30
    d["c_mask"] = m
    d["wh"] = wT(g["L1_ffn_Wq"], np)
    d["wkv"] = wT(g["L1_ffn_Wkv"].reshape(8, 2, 64, D).transpose(1, 0, 2, 3).reshape(2 * D, D), np)
    d["who"] = wT(g["L1_ffn_Wout_h"], np)
    d["gam"] = np.ascontiguousarray(col(g["L1_ffn_gamma"]))
    nk = np.zeros((8, 64, 8), np.float32)
    for h in range(8):
        nk[h, :, h] = g["L1_ffn_null_kv"][0, h]
    d["nkb"] = np.ascontiguousarray(nk.reshape(4, 128, 8).transpose(1, 0, 2))
    nv = np.ones((128, 8, 65), np.float32)
    nv[:, :, :64] = g["L1_ffn_null_kv"][1][None]
    d["nvb"] = nv
    return d


def kernel(**inputs):
    import numpy as np
    import concourse.bacc as bacc
    from concourse.bass_utils import run_bass_kernel_spmd as run

    nc = bacc.Bacc("TRN2", target_bir_lowering=False, num_devices=1)
    arrays = {"in_" + k: v for k, v in layout(inputs, np).items()}
    args = {k[3:]: nc.dram_tensor(k, v.shape, mybir.dt.from_np(v.dtype), kind="ExternalInput").ap()
            for k, v in arrays.items()}
    out = nc.dram_tensor("out_0", (B * S, D), F, kind="ExternalOutput").ap()
    build(nc, args, out)
    r = run(nc, [arrays], core_ids=[0])
    return r.results[0]["out_0"].reshape(B, S, D)
```

```python
import math
from collections import deque
from contextlib import ExitStack

import concourse.bass as bass
from concourse import mybir

ALU = mybir.AluOpType
ACT = mybir.ActivationFunctionType
X = mybir.AxisListType.X
F = mybir.dt.float32
I32 = mybir.dt.int32
R = mybir.dt.float32r

B, S, D = 4, 2048, 512
NK = 77
NQ, NKV = 256, 512
NT = B * S // 128
NB = NT // 4
ITERS = 50
OFF3 = (0, 103, 205)
SEGS = ((0, 0, 0, 77, 0, 0), (0, 1, 0, 26, 77, 33),
        (1, 1, 26, 51, 0, 0), (1, 2, 0, 52, 51, 33),
        (2, 2, 52, 25, 1, 0), (2, 3, 0, 77, 26, 33))
LOGK = (math.log(NQ * 9.0 / 8.0), math.log(NKV * 9.0 / 8.0))


class Flow:

    def __init__(self, nc, stack):
        self.nc, self.stack = nc, stack
        self.sem, self.val, self.seen = {}, {}, {}

    def tick(self, ins, name, by=1):
        if name not in self.sem:
            self.sem[name] = self.stack.enter_context(self.nc.semaphore(name))
            self.val[name] = 0
        ins.then_inc(self.sem[name], by)
        self.val[name] += by
        return (name, self.val[name])

    def need(self, eng, *tokens):
        for t in tokens:
            if t is None:
                continue
            if isinstance(t, list):
                self.need(eng, *t)
                continue
            name, v = t
            key = (str(eng.engine), name)
            if self.seen.get(key, 0) < v:
                eng.wait_ge(self.sem[name], v)
                self.seen[key] = v

    def all(self):
        return list(self.val.items())


class Slots:

    def __init__(self, n):
        self.reset(range(n) if isinstance(n, int) else n)

    def reset(self, ids):
        self.ready = deque((k, []) for k in ids)

    def take(self):
        assert self.ready, "taken before it was given back"
        return self.ready.popleft()

    def give(self, k, *toks):
        self.ready.append((k, list(toks)))


class Later:

    def __init__(self):
        self.q, self.turn = (deque(), deque()), 0

    def add(self, gen, which=0):
        self.q[which].append(gen)
        return gen

    def one(self, which):
        q = self.q[which]
        while q:
            try:
                next(q[0])
                return True
            except StopIteration:
                q.popleft()
        return False

    def piece(self):
        self.turn ^= 1
        return self.one(self.turn) or self.one(self.turn ^ 1)

    def finish(self, gen):
        while gen in self.q[0] or gen in self.q[1]:
            self.one(0 if gen in self.q[0] else 1)

    def drain(self):
        while self.piece():
            pass


def last(ap, n):
    return ap.unsqueeze(2).broadcast_to([ap.shape[0], ap.shape[1], n])


def mid(ap, n):
    return ap.unsqueeze(1).broadcast_to([ap.shape[0], n, ap.shape[1]])


def build(nc, a, out):
    PE, V, A, G, SY = nc.tensor, nc.vector, nc.scalar, nc.gpsimd, nc.sync
    with ExitStack() as top:
        fl = Flow(nc, top)
        tick, need = fl.tick, fl.need

        def dram(name, shape):
            return nc.dram_tensor(name, shape, F, kind="Internal").ap()

        X3d = dram("x3_scratch", (B * S, D))
        X2d = dram("x2_scratch", (B * S, D))
        Yd = dram("y_scratch", (B * S, D))
        Vd = dram("v_scratch", (2, B, 16, NK, 33))
        cumd = dram("cum_scratch", (8, S))
        fd = dram("f_scratch", (2 * B * S, 1))

        def alloc(stack):
            return lambda name, shape, dt=F: stack.enter_context(nc.sbuf_tensor(name, shape, dt))

        def load(dst, src, name, eng=SY):
            return tick(eng.dma_start(dst, src), name, 16)

        sb = alloc(top)
        ps = top.enter_context(nc.psum_tensor("ps", [128, 8, 512], F))
        Ts = Ms = Slots(8)

        ident = sb("ident", [128, 128])
        grp = sb("grp", [128, 128])
        tri = sb("tri", [128, 128])
        mhalf = sb("mhalf", [128, 8])
        cols = sb("cols", [128, 16])
        scol = sb("scol", [128, 2, NT])
        mvx = sb("mvx", [128, NT, 2])
        rsx = sb("rsx", [128, NT])
        comb = sb("comb", [128, NT])
        lnwb = sb("lnwb", [128, 8])
        gam = sb("gam", [128, 4])
        t_ident = load(ident[:, :], a["c_ident"], "ld.ident")
        t_mhalf = tick(G.memset(mhalf[:, :], -0.5), "g.mhalf")
        s_tok = []

        idx = sb("idx", [128, 24], I32)
        idxs = sb("idxs", [128, 24], I32)
        st = sb("st", [128, 2, 4, 6])
        mv = sb("mv", [128, 2, 4, 2])
        ve = sb("ve", [128, 2, 4])
        nm_ = sb("nm_", [128, 2, 4])
        rs = sb("rs", [128, 2, 4])
        Ln = Slots(2)
        xn = sb("xn", [128, 3, D])
        Xn = Slots(3)
        On = sb("On", [128, 2, D])
        Ons = Slots(2)
        OTs = Slots(2)
        rc = sb("rc", [128, 2, 8])
        Rc = Slots(2)

        def ln_stats(tiles, ready):
            k, w = Ln.take()
            need(V, w)
            for t in range(4):
                need(V, ready(t))
                tok = tick(V.bn_stats(st[:, k, t, :], tiles(t)), "v.bnstats")
            yield
            need(V, tok)
            for t in range(4):
                tok = tick(V.bn_aggr(mv[:, k, t, :], st[:, k, t, :]), "v.bnaggr")
            need(V, tok)
            tick(V.tensor_scalar(nm_[:, k, :], mv[:, k, :, 0], -1.0, None, ALU.mult), "v.vareps")
            tok = tick(V.tensor_scalar(ve[:, k, :], mv[:, k, :, 1], 1e-5, None, ALU.add), "v.vareps")
            need(G, tok, t_mhalf)
            tok = tick(G.tensor_tensor(rs[:, k, :], ve[:, k, :], mhalf[:, 0:4], ALU.pow), "g.rstd")
            need(G, tok)
            tok = tick(G.tensor_tensor(nm_[:, k, :], nm_[:, k, :], rs[:, k, :], ALU.mult), "g.rstd")
            yield
            return k, tok

        def ln_apply(k, t, x, t_rs, t_x):
            kx, w = Xn.take()
            need(A, w, t_rs, t_x)
            tok = tick(A.activation(xn[:, kx, :], x, ACT.Identity, bias=nm_[:, k, t:t + 1], scale=rs[:, k, t:t + 1]),
                       "a.lnapply")
            if t == 3:
                Ln.give(k, tok)
            return kx, tok

        def split(hi, lo, src, *w):
            need(A, *w)
            need(V, tick(A.copy(hi, src), "a.hi"), *w)
            return tick(V.tensor_tensor(lo, src, hi.bitcast(F), ALU.subtract), "v.lo")

        def turn4(src, t_src, give, dst, w_dst, name, lo=None):
            kt, w = Ts.take()
            need(PE, w, t_src, t_ident)
            for c in range(4):
                m = PE.transpose(ps[:, kt, 128 * c:128 * c + 128], src[:, 128 * c:128 * c + 128], ident[:, :])
            tok = tick(m, "pe." + name)
            give(tok)
            res = ps[:, kt, :].rearrange("p (c n) -> p c n", c=4)
            if lo is None:
                need(A, tok, w_dst)
                te = tick(A.copy(dst, res), "a." + name)
            else:
                need(A, tok, w_dst)
                th = tick(A.copy(dst, res), "a.hi")

                def low():
                    need(V, th, tok, w_dst)
                    te = tick(V.tensor_tensor(lo, res, dst.bitcast(F), ALU.subtract), "v.lo")
                    Ts.give(kt, te)
                    return te
                return low
            Ts.give(kt, te)
            return te

        def mms(outp, pairs, w):
            need(PE, w)
            for i, (l, r) in enumerate(pairs):
                m = PE.matmul(outp, l, r, start=(i == 0), stop=(i == len(pairs) - 1))
            return m

        def mms3(outp, parts, w, first=True, final=True):
            need(PE, w)
            for i, (lh, ll, rh, rl) in enumerate(parts):
                PE.matmul(outp, lh, rh, start=(first and i == 0), stop=False)
                PE.matmul(outp, lh, rl, start=False, stop=False)
                m = PE.matmul(outp, ll, rh, start=False, stop=(final and i == len(parts) - 1))
            return m

        bo = sb("bo", [128, D])
        bl = sb("bl", [128, 8])
        def arena(name, size):
            base = -(-nc.sbuf_base // 32) * 32
            top.enter_context(nc.sbuf_tensor(name, [128, size], F))
            return lambda name, off, shape, dt=F: nc.alloc_sbuf_tensor_at(name, shape, dt, offset=base + 4 * off)

        at = arena("arena_x", 8192)
        xT = [at(f"xT{i}", 4096 * i, [128, 2, 4, D], R) for i in (0, 1)]
        raw = at("raw", 0, [128, 4, 3 * D])
        QU, Sw = at("QU", 0, [128, 2, 4, D]), at("Sw", 4096, [128, 2, 2048])
        hi = [at("Wkv0", 0, [128, 4, 2 * D], R), at("Wh0", 4096, [128, 4, D], R), at("Who0", 6144, [128, 4, D], R)]

        with ExitStack() as pa:
            sb = alloc(pa)
            Wq = [sb(f"Wq{i}", [128, 4, D], R) for i in (0, 1)]
            Wo = [sb(f"Wo{i}", [128, 4, D], R) for i in (0, 1)]
            Win = [sb(f"Win{i}", [128, 4, 128], R) for i in (0, 1)]
            OTp = [sb(f"OTp{i}", [128, 2, 4, 128], R) for i in (0, 1)]
            bq = sb("bq", [128, 2, 4])
            cF = sb("cF", [128, D])
            rt = sb("rt", [128, 2, D])
            KT = [sb(f"KT{L}", [128, 4, B * NK]) for L in (0, 1)]
            KB = [sb(f"KB{s}", [128, 4, 4 * NK]) for s in (0, 1)]
            VB = [sb(f"VB{s}", [103, 4, 3, 66]) for s in (0, 1)]
            Wout = sb("Wout", [128, D])
            fcol = sb("fcol", [128, 32])
            dlt = sb("dlt", [128, B, NK])
            XB = sb("XB", [128, 4, 4, D])
            QT = sb("QT", [128, 2, 4, D])
            Sb = sb("Sb", [128, 2, 16 * NK])
            PT = sb("PT", [103, 12, 128])
            mx = sb("mx", [128, 2, 16])
            sTa = sb("sTa", [128, 3 * D])
            sT = sTa[:, 0:2 * D].rearrange("p (s n) -> p s n", s=2)
            acc = sTa[:, 2 * D:3 * D]
            stage = sb("vstage", [NK, 16, 33])
            hh = sb("hh", [128, 2, D])
            junk = sb("junk", [128, D])
            zx = sb("zx", [128, D])
            sx = sb("sx", [128, 6])
            vx = sb("vx", [128, NT])
            nmx = sb("nmx", [128, NT])
            XTs, QTs, Ss, STs, Hs, XBs = Slots(2), Slots(2), Slots(2), Slots(2), Slots(2), Slots(2)
            free = {"acc": [], "PT": []}

            ctxT = sTa[:, 0:4 * B * NK].rearrange("p (k n) -> p k n", k=4)
            b2t = sTa[0:64, 4 * B * NK:4 * B * NK + 128]
            kc = sb("kc", [128, 16])

            t_c = load(ctxT[:, :, :], a["ctxT"], "ld.ctx")
            t_c = load(kc[:, :], a["kcol"], "ld.ctx")
            t_c = load(hh[0:NK, 0, :], a["bv0"], "ld.ctx")
            t_c = load(hh[0:NK, 1, :], a["bv1"], "ld.ctx")
            t_wk, t_wv, t_w, t_x = {}, {}, {}, {}
            xin = a["x"].rearrange("(n t p) d -> n p t d", t=4, p=128)

            X2 = X2d.rearrange("(n t p) d -> n p t d", t=4, p=128)
            x2_tok = {}
            xslot = {}

            def load_x(L, i):
                k, w = XBs.take()
                need(SY, w, x2_tok.get(i) if L else None)
                xslot[L, i] = k
                t_x[L, i] = load(XB[:, k, :, :], X2[i] if L else xin[i], f"ld.x{k}")

            wk, wv = XB[:, 2, :, :], XB[:, 3, :, :]

            def load_wkv(L, w_k, w_v):
                need(A, w_k)
                t_wk[L] = load(wk, a[f"wk{L}"], "ld.wk", A)
                need(A, w_v)
                t_wv[L] = load(wv, a[f"wv{L}"], "ld.wv", A)

            for k in (0, 1):
                Hs.take()
                QTs.take()
                STs.take()
            load_wkv(0, [], [])
            load_x(0, 0)
            t_wq = load(QT[:, 0, :, :], a["wq0"], "ld.wq")
            load(bq[:, :, :], a["bq"], "ld.small")
            load(fcol[:, :], a["fcol"], "ld.small")
            load(Wout[:, :], a["wout"], "ld.small")
            load(cF[:, :], a["bout"], "ld.small")
            load(bo[:, :], a["bo0"], "ld.small")
            load(dlt[:, :, :], a["delta"], "ld.small")
            load(lnwb[:, :], a["lnwb"], "ld.small")
            load(gam[:, :], a["gam"], "ld.small")
            load(grp[:, :], a["c_grp"], "ld.small")
            load(tri[:, :], a["c_tri"], "ld.small")
            t_small = load(cols[:, :], a["cols"], "ld.small")
            t_wo = load(QT[:, 1, :, :], a["wo0"], "ld.wo")
            load_x(0, 1)
            t_win = load(zx[:, :].rearrange("p (k m) -> p k m", k=4), a["win"], "ld.win")
            t_rt = load(rt[:, :, :], a["rt"], "ld.w1")
            t_bo = [t_small]
            t_zero = []
            for k in (0, 1):
                tick(V.memset(KB[k][:, :, :], 0.0), "v.zero")
                t_zero = tick(V.memset(VB[k][:, :, :, :], 0.0), "v.zero")
            t_one = tick(V.memset(stage[:, :, :], 1.0), "v.one")
            need(V, t_c)
            t_t = tick(V.tensor_scalar(kc[:, 12:16], kc[:, 8:12], 1.0 / math.sqrt(32.0), None, ALU.mult), "v.setup")
            tau = kc[:, 12:16]
            t_KT, t_V = {}, {}
            f_kv = {"stage": [t_one]}

            def setup_kv(L):
                for c in range(4):
                    km, w = Ms.take()
                    need(PE, t_wk[L], t_c)
                    tok = tick(mms(ps[:, km, 0:B * NK], [(wk[:, k, 128 * c:128 * c + 128], ctxT[:, k, :])
                                                          for k in range(4)], w), "pe.setup")
                    need(V, tok, t_t)
                    for b in range(B):
                        tok2 = tick(V.tensor_scalar(KT[L][:, c, NK * b:NK * b + NK], ps[:, km, NK * b:NK * b + NK],
                                                    kc[:, 4 * L + c:4 * L + c + 1], tau[:, b:b + 1],
                                                    ALU.add, ALU.mult), "v.KT")
                    Ms.give(km, tok2)
                    yield
                f_kv["k"] = tok
                t_KT[L] = tok2
                for b in range(B):
                    km, w = Ms.take()
                    need(PE, t_wv[L])
                    tok = tick(mms(ps[0:NK, km, :], [(ctxT[:, k, NK * b:NK * b + NK], wv[:, k, :])
                                                      for k in range(4)], w), "pe.setup")
                    need(V, tok, f_kv["stage"])
                    tok2 = tick(V.tensor_tensor(stage[:, :, 0:32],
                                                ps[0:NK, km, :].rearrange("p (h d) -> p h d", h=16),
                                                hh[0:NK, L, :].rearrange("p (h d) -> p h d", h=16), ALU.add), "v.V")
                    Ms.give(km, tok2)
                    need(SY, tok2)
                    tok2 = tick(SY.dma_start(Vd[L, b].rearrange("h k e -> k h e"), stage[:, :, :]), "st.V", 16)
                    f_kv["stage"] = [tok2]
                    t_V[L] = tok2
                    yield
                f_kv["v"] = tok

            def setup_rest():
                need(V, t_small)
                tok = tick(V.scalar_tensor_tensor(fcol[:, 8:16], fcol[:, 0:8], fcol[:, 24:25], fcol[:, 8:16],
                                                  ALU.mult, ALU.add), "v.setup")
                tok = tick(V.tensor_copy(b2t[:, :], fcol[0:64, 25:26].broadcast_to([64, 128])), "v.setup")
                km, w = Ms.take()
                need(PE, tok, t_small)
                tok = tick(mms(ps[:, km, :], [(b2t[:, :], Wout[0:64, :])], w), "pe.setup")
                need(V, tok)
                tok = tick(V.tensor_tensor(cF[:, :], ps[:, km, :], cF[:, :], ALU.add), "v.setup")
                Ms.give(km, tok)
                return tok

            need(V, t_small)
            t_d = tick(V.tensor_scalar(dlt[:, :, :], dlt[:, :, :], 1.0 / math.sqrt(32.0), None, ALU.mult), "v.setup")
            for _ in setup_kv(0):
                pass
            load_wkv(1, [f_kv["k"]], [f_kv["v"]])

            def split_w(parts, src, name, *w):
                for k in range(4):
                    t_w[name] = split(parts[0][:, k, :], parts[1][:, k, :], src[:, k, :], *w)
                return t_w[name]

            QTs.give(0, split_w(Wq, QT[:, 0, :, :], "q", t_wq))
            t_f = t_cF = setup_rest()
            QTs.give(1, split_w(Wo, QT[:, 1, :, :], "o", t_wo))
            split_w(Win, zx[:, :].rearrange("p (k m) -> p k m", k=4), "in", t_win)

            KVs = Slots(2)
            kv = {}

            def load_kv(L, b):
                k, w = KVs.take()
                need(V, w, t_zero, t_KT[L])
                for i in range(4):
                    tk = tick(V.tensor_copy(KB[k][32 * i:32 * i + 32, :, NK * i:NK * i + NK],
                                            KT[L][32 * i:32 * i + 32, :, NK * b:NK * b + NK]), "v.KB")
                yield
                need(SY, w, t_zero, t_V[L])
                for c, i, k0, n, r0, c0 in SEGS:
                    tv = load(VB[k][r0:r0 + n, :, c, c0:c0 + 33],
                              Vd[L, b].rearrange("(g i) k e -> i k g e", i=4)[i, k0:k0 + n], "ld.VB")
                kv[L, b] = (k, tk, tv)
                yield

            class Blk:
                pass

            blks = {}

            def prep(L, i, row, t_row, proj):
                bk = blks[L, i]
                xb = XB[:, bk.x, :, :]
                k, t_rs = yield from ln_stats(lambda t: xb[:, t, :], lambda t: bk.ready[t])
                yield
                kx, w = XTs.take()
                ready = []

                def ln(t):
                    kn, tn = ln_apply(k, t, xb[:, t, :], t_rs, bk.ready[t])
                    need(G, tn, t_row)
                    ready.append(tick(G.tensor_tensor(xb[:, t, :], xb[:, t, :], row, ALU.add), "g.bias"))
                    return kn, tn

                nxt = ln(0)
                yield
                for t in range(4):
                    kn, tn = nxt
                    nxt = ln(t + 1) if t < 3 else None
                    low = turn4(xn[:, kn, :], tn, lambda tok, kn=kn: Xn.give(kn, tok),
                                xT[0][:, kx, :, 128 * t:128 * t + 128], w, "xT",
                                xT[1][:, kx, :, 128 * t:128 * t + 128])
                    te = low()
                    yield
                bk.ready = ready
                yield
                yield from proj(bk, kx, te)

            def qproj(L):
                def go(bk, kx, te):
                    kq, wq_ = QTs.take()
                    for c in range(4):
                        km, w = Ms.take()
                        need(PE, te, t_w["q"])
                        tok = tick(mms3(ps[:, km, :], [(Wq[0][:, k, 128 * c:128 * c + 128],
                                                        Wq[1][:, k, 128 * c:128 * c + 128],
                                                        xT[0][:, kx, k, :], xT[1][:, kx, k, :])
                                                       for k in range(4)], w), "pe.Q")
                        need(A, tok, wq_, t_small)
                        tq = tick(A.activation(QT[:, kq, c, :], ps[:, km, :], ACT.Identity, bias=bq[:, L, c:c + 1]), "a.Q")
                        Ms.give(km, tq)
                        yield
                    XTs.give(kx, tok)
                    bk.q = (kq, tq)
                return go

            def ffn(bk, kx, te):
                ks, w1 = STs.take()
                km, w = Ms.take()
                need(PE, te, t_w["in"])
                tok = tick(mms3(ps[:, km, :], [(Win[0][:, k, :], Win[1][:, k, :], xT[0][:, kx, k, :], xT[1][:, kx, k, :])
                                               for k in range(4)], w), "pe.win")
                XTs.give(kx, tok)
                need(A, tok, w1)
                ts = tick(A.copy(sT[:, ks, :], ps[:, km, :]), "a.sT")
                Ms.give(km, ts)
                yield
                need(A, ts, t_f)
                need(V, free["acc"])
                for j in range(9):
                    if j < 8:
                        kh, w = Hs.take()
                        need(A, w)
                        th = tick(A.activation(hh[:, kh, :], sT[:, ks, :], ACT.Relu, bias=fcol[:, 8 + j:9 + j],
                                               scale=fcol[:, j:j + 1]), "a.relu")
                        new = (kh, th)
                    if j:
                        kh, t_h = old
                        need(V, t_h)
                        if j == 1:
                            ta = tick(V.tensor_scalar(acc, hh[:, kh, :], fcol[:, 16:17], None, ALU.mult), "v.acc")
                        else:
                            need(V, ta)
                            ta = tick(V.scalar_tensor_tensor(acc, hh[:, kh, :], fcol[:, 15 + j:16 + j], acc,
                                                             ALU.mult, ALU.add), "v.acc")
                        Hs.give(kh, ta)
                    old = new
                    if j % 2 == 0:
                        yield
                STs.give(ks, th)
                yield
                for t in range(4):
                    km, w = Ms.take()
                    need(PE, ta)
                    tok = tick(mms(ps[:, km, :], [(acc[:, 128 * t:128 * t + 128], Wout[:, :])], w), "pe.wout")
                    need(V, tok, bk.ready[t])
                    x = XB[:, bk.x, t, :]
                    bk.ready[t] = tick(V.tensor_tensor(x, ps[:, km, :], x, ALU.add), "v.x")
                    Ms.give(km, bk.ready[t])
                    yield
                free["acc"] = [tok]
                need(SY, bk.ready)
                x2_tok[bk.i] = tick(SY.dma_start(X2[bk.i], XB[:, bk.x, :, :]), f"st.x2{bk.i % 2}", 16)
                XBs.give(bk.x, x2_tok[bk.i])

            class Tile:
                pass

            def scores(t, gs):
                L, bk, b = t.L, t.bk, t.b
                if t.tl == 0:
                    need(PE, bk.q[1])
                kb, tk, tv = kv[L, b]
                if gs[0] == 0:
                    t.s, t.ws = Ss.take()
                w_s = t.ws
                kq = bk.q[0]
                for g in gs:
                    kp, w = Ms.take()
                    need(PE, tk)
                    t.tq = tick(mms(ps[:, kp, 0:308], [(QT[:, kq, g, 128 * t.tl:128 * t.tl + 128],
                                                         KB[kb][:, g, :])], w), "pe.S")
                    need(V, t.tq, w_s, t_d)
                    tok = tick(V.tensor_tensor(Sb[:, t.s, 308 * g:308 * g + 308].rearrange("p (i k) -> p i k", i=4),
                                               ps[:, kp, 0:308].rearrange("p (i k) -> p i k", i=4),
                                               mid(dlt[:, b, :], 4), ALU.add), "v.Sadd")
                    Ms.give(kp, tok)
                if gs[-1] != 3:
                    return
                if t.tl == 3:
                    QTs.give(kq, t.tq)
                sv = Sb[:, t.s, :].rearrange("p (h k) -> p h k", h=16)
                need(V, tok)
                tok = tick(V.tensor_reduce(mx[:, t.s, :], sv, X, ALU.max), "v.max")
                need(G, tok)
                t.sub = tick(G.tensor_tensor(sv, sv, last(mx[:, t.s, :], NK), ALU.subtract), "g.sub")

            def softexp(t):
                need(A, t.sub)
                t.exp = tick(A.activation(Sb[:, t.s, :], Sb[:, t.s, :], ACT.Exp), "a.exp")

            def ptrans(t, g):
                kt, w = Ts.take()
                need(PE, w, t.exp)
                for c in range(3):
                    o = 308 * g + OFF3[c]
                    m = PE.transpose(ps[0:103, kt, 128 * c:128 * c + 128], Sb[:, t.s, o:o + 103], ident[:, :])
                tok = tick(m, "pe.PT")
                if g == 3:
                    Ss.give(t.s, tok)
                need(A, tok, free["PT"])
                t.pt = tick(A.copy(PT[:, 3 * g:3 * g + 3, :],
                                   ps[0:103, kt, 0:384].rearrange("p (c n) -> p c n", c=3)), "a.PT")
                Ts.give(kt, t.pt)

            def pv(t, hf):
                kb, tk, tv = kv[t.L, t.b]
                if hf == 0:
                    t.o, t.wo_ = Ons.take()
                w_o = t.wo_
                km, w = Ms.take()
                need(PE, w, t.pt, tv)
                for j in range(2):
                    g = 2 * hf + j
                    for c in range(3):
                        o = 132 * j + 33 * c
                        m = PE.matmul(ps[:, km, o:o + 66], PT[:, 3 * g + c, :], VB[kb][:, g, c, :],
                                      start=(j == 0 and c == 0), stop=(j == 1 and c == 2), skip_group_check=True)
                tok = tick(m, "pe.PV")
                ov = ps[:, km, 0:264].rearrange("p (h e) -> p h e", e=33)
                kr, wr = Rc.take()
                need(V, tok, w_o, wr)
                tr = tick(V.reciprocal(rc[:, kr, :], ov[:, :, 32]), "v.rc")
                need(V, tr)
                t.on = tick(V.tensor_tensor(On[:, t.o, 256 * hf:256 * hf + 256].rearrange("p (h d) -> p h d", h=8),
                                            ov[:, :, 0:32], last(rc[:, kr, :], 32), ALU.mult), "v.On")
                Rc.give(kr, t.on)
                Ms.give(km, t.on)
                if hf == 0:
                    return
                free["PT"] = [tok]
                if t.lastkv:
                    KVs.give(kb, tok, t.tq)

            def otrans(t):
                t.ot, w = OTs.take()
                t.te = turn4(On[:, t.o, :], t.on, lambda tok: Ons.give(t.o, tok), OTp[0][:, t.ot, :, :], w, "OT",
                             OTp[1][:, t.ot, :, :])()

            def wo(t, part):
                if part == 0:
                    t.km, w = Ms.take()
                    need(PE, w, t.te, t_w["o"])
                km = t.km
                m = mms3(ps[:, km, :], [(OTp[0][:, t.ot, c, :], OTp[1][:, t.ot, c, :], Wo[0][:, c, :], Wo[1][:, c, :])
                                        for c in (2 * part, 2 * part + 1)], None, part == 0, part == 1)
                if part == 0:
                    return
                tok = tick(m, "pe.Wo")
                OTs.give(t.ot, tok)
                bk = t.bk
                x = XB[:, bk.x, t.tl, :]
                need(V, tok, bk.ready[t.tl])
                tx = tick(V.tensor_tensor(x, ps[:, km, :], x, ALU.add), "v.x")
                Ms.give(km, tx)
                if t.L == 0:
                    bk.new[t.tl] = tx
                    if t.tl == 3:
                        bk.ready = bk.new
                    return
                n = 4 * bk.i + t.tl
                need(SY, tx, x3_tok.get(n - 8))
                x3_tok[n] = tick(SY.dma_start(X3d[128 * n:128 * n + 128, :], x), f"st.x3{n % 8}", 16)
                need(V, tx, free.get("sx"))
                tok = tick(V.bn_stats(sx[:, :], x), "v.sx")
                need(V, tok)
                tok = tick(V.bn_aggr(mvx[:, n, :], sx[:, :]), "v.sx")
                need(V, tok)
                tick(V.tensor_scalar(nmx[:, n:n + 1], mvx[:, n, 0:1], -1.0, None, ALU.mult), "v.sx")
                tok = tick(V.tensor_scalar(vx[:, n:n + 1], mvx[:, n, 1:2], 1e-5, None, ALU.add), "v.sx")
                free["sx"] = [tok]
                need(G, tok, t_mhalf)
                t.rx = tick(G.tensor_tensor(rsx[:, n:n + 1], vx[:, n:n + 1], mhalf[:, 0:1], ALU.pow), "g.rx")
                need(G, t.rx)
                t.rx = tick(G.tensor_tensor(nmx[:, n:n + 1], nmx[:, n:n + 1], rsx[:, n:n + 1], ALU.mult), "g.rx")

            def route_scores(t):
                if t.L == 0:
                    return
                n = 4 * t.bk.i + t.tl
                x = XB[:, t.bk.x, t.tl, :]
                need(A, t.rx, free.get("junk"))
                ts = tick(A.activation(zx[:, :], x, ACT.Identity, bias=nmx[:, n:n + 1], scale=rsx[:, n:n + 1]), "a.s")
                need(V, t_rt)
                for r in range(2):
                    need(V, ts)
                    ts = tick(V.tensor_tensor_reduce(junk[:, :], zx[:, :], rt[:, r, :], 1.0, 0.0, ALU.mult, ALU.add,
                                                     scol[:, r, n:n + 1]), "v.s")
                free["junk"] = [ts]
                s_tok[:] = [ts]
                t.bk.done += [x3_tok[n], ts]
                if t.tl == 3:
                    XBs.give(t.bk.x, *t.bk.done)
                    q = slice(n - 3, n + 1)
                    tok = tick(V.tensor_tensor(comb[:, q], rsx[:, q], rsx[:, q], ALU.mult), "v.comb")
                    need(V, tok)
                    tok = tick(V.tensor_tensor(comb[:, q], comb[:, q], mvx[:, q, 1], ALU.mult), "v.comb")
                    need(V, tok)
                    tok = tick(V.tensor_scalar(comb[:, q], comb[:, q], 1e-5, None, ALU.add), "v.comb")
                    need(G, tok)
                    tok = tick(G.tensor_tensor(comb[:, q], comb[:, q], mhalf[:, 0:4], ALU.pow), "g.comb")
                    need(G, tok)
                    tick(G.tensor_tensor(comb[:, q], comb[:, q], rsx[:, q], ALU.mult), "g.comb")

            x3_tok = {}
            units = [(L, i) for L in (0, 1) for i in range(NB)]
            for L, i in units:
                bk = blks[L, i] = Blk()
                bk.i, bk.new, bk.done = i, [None] * 4, []
            seq = []
            for L, i in units:
                for tl in range(4):
                    t = Tile()
                    t.L, t.bk, t.tl, t.b = L, blks[L, i], tl, i // 4
                    t.lastkv = tl == 3 and i % 4 == 3
                    seq.append(t)
            bg = Later()
            made, fed = {}, {}

            def queue_prep(L, i):
                if i % 4 == 0:
                    bg.add(load_kv(L, i // 4))
                blks[L, i].x = xslot[L, i]
                blks[L, i].ready = [t_x[L, i]] * 4
                made[L, i] = bg.add(prep(L, i, bo[:, :], t_bo, qproj(L)))

            def free_wkv():
                XBs.give(2, f_kv["k"])
                XBs.give(3, f_kv["v"])
                load_x(0, 2)
                free["acc"] = [f_kv["v"]]
                for k in (0, 1):
                    Hs.give(k, *f_kv["stage"])
                    STs.give(k, f_kv["v"])
                yield

            def new_q():
                k, t = wstage.pop()
                for c in range(4):
                    t_w["q"] = split(Wq[0][:, c, :], Wq[1][:, c, :], XB[:, k, c, :], t, ("pe.Q", fl.val["pe.Q"]))
                need(SY, t_w["q"], ("g.bias", fl.val["g.bias"]))
                t_bo[:] = [load(bo[:, :], a["bo1"], "ld.bo")]
                wstage.append((k, load(XB[:, k, :, :], a["wo1"], "ld.wo")))
                yield

            def new_o():
                k, t = wstage.pop()
                for c in range(4):
                    t_w["o"] = split(Wo[0][:, c, :], Wo[1][:, c, :], XB[:, k, c, :], t, ("pe.Wo", fl.val["pe.Wo"]))
                XBs.give(k, t_w["o"])

            def window_bias():
                for k in range(4):
                    tok = tick(G.tensor_copy(cF[:, 128 * k:128 * k + 128],
                                             lnwb[:, 4 + k:5 + k].broadcast_to([128, 128])), "g.setup2")
                yield
                yield
                for c in range(8):
                    if c % 4 == 0:
                        km, w = Ms.take()
                        need(PE, w, t_raw)
                    for k in range(4):
                        m = PE.matmul(ps[:, km, c:c + 1], raw[:, k, 128 * c:128 * c + 128], lnwb[:, 4 + k:5 + k],
                                      start=(k == 0), stop=(k == 3))
                    if c % 4 == 3:
                        tc = tick(m, "pe.setup2")
                        need(V, tc)
                        tc = tick(V.tensor_scalar(bl[:, c - 3:c + 1], ps[:, km, c - 3:c + 1], (0.125, 1.0)[c // 4], None,
                                                  ALU.mult), "v.setup2")
                        Ms.give(km, tc)
                    yield
                km, w = Ms.take()
                need(PE, tok)
                tok = tick(mms(ps[:, km, :], [(cF[:, 128 * k:128 * k + 128], raw[:, k, 2 * D:3 * D])
                                              for k in range(4)], w), "pe.setup2")
                need(V, tok, ("g.bias", fl.val["g.bias"]))
                Ms.give(km, tick(V.tensor_copy(bo[:, :], ps[:, km, :]), "v.setup2"))
                yield

            wstage = []
            queue_prep(0, 0)
            bg.finish(made[0, 0])
            bg.add(setup_kv(1), 1)
            made_kv = bg.add(free_wkv(), 1)
            debt = 0.0

            def pieces():
                nonlocal debt
                debt += rate / 7
                while debt >= 1:
                    debt -= 1
                    bg.piece()

            for n in range(len(seq) + 3):
                rate = 8.5 if n < 4 * (NB + 1) else 3.5
                cur = seq[n] if n < len(seq) else None
                p1 = seq[n - 1] if 1 <= n <= len(seq) else None
                p2 = seq[n - 2] if 2 <= n < len(seq) + 2 else None
                if n >= 3:
                    route_scores(seq[n - 3])
                if cur is not None:
                    L, i = cur.L, cur.bk.i
                    if cur.tl == 0:
                        bg.finish(made[L, i])
                        if (L, i) == (0, NB - 1):
                            bg.finish(fed[NB - 3])
                            load_x(1, 0)
                            bg.add(new_q())
                        elif (L, i) == (1, 0):
                            bg.finish(fed[NB - 2])
                            load_x(1, 1)
                        if n // 4 + 1 < len(units):
                            queue_prep(*units[n // 4 + 1])
                    elif cur.tl == 2 and L == 0 and 1 <= i <= NB - 2:
                        bg.finish(made_kv if i == 1 else fed[i - 2])
                        if i < NB - 2:
                            load_x(0, i + 2)
                        else:
                            k, w = XBs.take()
                            need(SY, w)
                            wstage.append((k, load(XB[:, k, :, :], a["wq1"], "ld.wq")))
                    elif cur.tl == 1 and (L, i) == (1, NB - 1):
                        for _ in (0, 1):
                            need(SY, XTs.take()[1])
                        t_raw = [load(raw[:, k, :], a["wqkv"][:, k, :], f"ld.raw{k}") for k in range(4)]
                        bg.add(window_bias())
                    elif cur.tl == 3 and L == 1 and i + 2 < NB:
                        load_x(1, i + 2)
                    scores(cur, (0,))
                if cur is not None:
                    scores(cur, (1,))
                if p2 is not None:
                    otrans(p2)
                if p1 is not None:
                    ptrans(p1, 0)
                if cur is not None:
                    scores(cur, (2,))
                if p1 is not None:
                    ptrans(p1, 1)
                if cur is not None:
                    scores(cur, (3,))
                pieces()
                if p1 is not None:
                    ptrans(p1, 2)
                pieces()
                if p1 is not None:
                    ptrans(p1, 3)
                if p2 is not None:
                    wo(p2, 0)
                    wo(p2, 1)
                    if p2.L == 0 and p2.tl == 3:
                        i = p2.bk.i
                        fed[i] = bg.add(prep(0, i, cF[:, :], t_cF, ffn), 1)
                        if i == NB - 1:
                            new_o()
                pieces()
                if p1 is not None:
                    pv(p1, 0)
                pieces()
                if p1 is not None:
                    pv(p1, 1)
                if cur is not None:
                    softexp(cur)
                pieces()
                pieces()
            bg.drain()
            done = fl.all()
        for e in (PE, V, A, G, SY):
            need(e, done)
        at = arena("arena_w", 12288)
        Wl = [at(f"Wl{i}", 6144 * i, [128, 4, 3 * D], R) for i in (0, 1)]
        places = (("Wkv", 0, 2 * D), ("Wh", 4096, D), ("Who", 6144, D))
        wc = [at(n + "r", o, [128, 4, m]) for n, o, m in places]
        lo = [at(n + "1", o, [128, 4, m], R) for n, o, m in places]
        XH = at("XH", 8192, [128, 8, D])
        fg = alloc(top)("fg", [128, 3, 6])
        ss = alloc(top)("ss", [128, 3, 8])
        sth = alloc(top)("sth", [128, 6, 6])
        mvh = alloc(top)("mvh", [128, 6, 2])
        rsh = alloc(top)("rsh", [128, 6])
        half = alloc(top)("half", [128, 8])
        t_half = tick(G.memset(half[:, :], 0.5), "g.half")
        with ExitStack() as pb:
            sb = alloc(pb)
            OT = sb("OT", [128, 2, 4, 128])
            Ts, Ms = Slots((4, 5)), Slots((6, 7))
            xU = [sb(f"xU{i}", [128, 4, 576], R) for i in (0, 1)]
            Wlo = sb("Wlo", [128, 4, D])
            msk = sb("msk", [128, 3, 256])
            nulq = sb("nulq", [128, D])
            XL = sb("XL", [128, 6, D])
            XY = sb("XY", [128, 3, D])
            KU = sb("KU", [128, 2, 4, 640])
            VU = sb("VU", [128, 11, 8, 65])
            PU = sb("PU", [128, 16, 128])
            mw = sb("mw", [128, 2, 8])
            yo = sb("yo", [128, 2, D])
            route = sb("route", [128, 4, 128])
            sr, zr, er = route[:, 0, :], route[:, 1, :], route[:, 2, :]
            Jk = route[:, :, :].rearrange("p a b -> p (a b)").bitcast(mybir.dt.uint8)[:, 0:512]
            rcol = sb("rcol", [128, 16])
            idxf = sb("idxf", [128, 24])
            cb = sb("cb", [128, 512])
            idx4 = scol[:, :, :].rearrange("p r n -> p (r n)")[:, 0:96].rearrange("p (c q) -> p c q", q=4)
            QUs, KUs, VUs, Sws, SPs, Yos = Slots(2), Slots(2), Slots(11), Slots(2), Slots(2), Slots(2)
            free = {"PU": []}

            for k in (0, 1):
                QUs.take()
                Sws.take()
            xt = {}
            xy, xyfree = {}, {}

            def load_xl(n, *w):
                need(SY, *w)
                xt[n] = load(XL[:, n % 6, :], X3d[128 * n:128 * n + 128, :], f"ld.xl{n % 6}")

            def load_xy(n):
                need(SY, xyfree.get(n - 3))
                xy[n] = load(XY[:, n % 3, :], X3d[128 * n:128 * n + 128, :], f"ld.xy{n % 3}")

            for n in range(6):
                load_xl(n)
            load(Wlo[:, :, :], a["wlo"], "ld.wl2")
            load(msk[:, :, :], a["c_mask"], "ld.wl2")
            t_wl2 = load(nulq[:, :], a["nulq"], "ld.wl2")
            xu = {"read": [], "tail": None}
            vt = {}
            blocks = {}

            def prep_b(bi):
                i = bi % 4
                o = {}
                blocks[bi] = o
                need(G, xu["read"], xu["tail"])
                if i == 0:
                    for x in xU:
                        t_tail = tick(G.memset(x[:, :, 0:64].bitcast(F), 0.0), "g.tail")
                else:
                    for x in xU:
                        t_tail = tick(G.tensor_copy(x[:, :, 0:64], x[:, :, 512:576]), "g.tail")
                def ln(n):
                    kn, w = Xn.take()
                    need(V, w, xt[n])
                    tn = tick(V.tensor_scalar(xn[:, kn, :], XL[:, n % 6, :], mvx[:, n, 0:1], comb[:, n:n + 1],
                                              ALU.subtract, ALU.mult), "v.lnapply")
                    if n + 6 < NT:
                        load_xl(n + 6, tn)
                    return kn, tn

                nxt = ln(4 * bi)
                yield
                for t in range(4):
                    kn, tn = nxt
                    nxt = ln(4 * bi + t + 1) if t < 3 else None
                    te = turn4(xn[:, kn, :], tn, lambda tok, kn=kn: Xn.give(kn, tok),
                               xU[0][:, :, 64 + 128 * t:192 + 128 * t], [t_tail] + xu["read"], "xT",
                               xU[1][:, :, 64 + 128 * t:192 + 128 * t])()
                    yield
                xu["tail"] = te
                yield
                kq, wq_ = QUs.take()
                for c in range(4):
                    km, w = Ms.take()
                    need(PE, te, t_wls)
                    tok = tick(mms3(ps[:, km, :], [(Wl[0][:, k, 128 * c:128 * c + 128],
                                                    Wl[1][:, k, 128 * c:128 * c + 128],
                                                    xU[0][:, k, 64:576], xU[1][:, k, 64:576])
                                                   for k in range(4)], w), "pe.Q")
                    need(A, tok, wq_)
                    tq = tick(A.activation(QU[:, kq, c, :], ps[:, km, :], ACT.Identity, bias=bl[:, c:c + 1],
                                           scale=0.125), "a.Q")
                    Ms.give(km, tq)
                    yield
                kk, wk_ = KUs.take()
                for c in range(4):
                    km, w = Ms.take()
                    need(PE, w)
                    tok = tick(mms3(ps[:, km, :], [(Wl[0][:, k, D + 128 * c:D + 128 * c + 128],
                                                    Wl[1][:, k, D + 128 * c:D + 128 * c + 128],
                                                    xU[0][:, k, 64:576], xU[1][:, k, 64:576])
                                                   for k in range(4)], w), "pe.K")
                    need(A, tok, wk_)
                    tk = tick(A.activation(KU[:, kk, c, 64:576], ps[:, km, :], ACT.Identity, bias=bl[:, 4 + c:5 + c]),
                              "a.K")
                    Ms.give(km, tk)
                    yield
                need(G, tk, wk_)
                if i == 0:
                    te1 = tick(G.memset(KU[:, kk, :, 0:64], 0.0), "g.edge")
                else:
                    pk = blocks[bi - 1]["k"]
                    tick(G.tensor_copy(KU[:, pk, :, 576:640], KU[:, kk, :, 64:128]), "g.edge")
                    te1 = tick(G.tensor_copy(KU[:, kk, :, 0:64], KU[:, pk, :, 512:576]), "g.edge")
                    blocks[bi - 1]["tk"].append(te1)
                if i == 3:
                    te1 = tick(G.memset(KU[:, kk, :, 576:640], 0.0), "g.edge")
                o["tk"] = [tk, te1]
                o["q"], o["tq"], o["k"] = kq, tq, kk
                for j in range(5 if i == 3 else 4):
                    M = 128 if j < 4 else 64
                    kv_, wv_ = VUs.take()
                    km, w = Ms.take()
                    need(PE, te, t_tail)
                    tok = tick(mms3(ps[0:M, km, :], [(xU[0][:, k, 128 * j:128 * j + M], xU[1][:, k, 128 * j:128 * j + M],
                                                      Wl[0][:, k, 2 * D:3 * D], Wl[1][:, k, 2 * D:3 * D])
                                                     for k in range(4)], w), "pe.V")
                    need(V, tok, wv_, tz)
                    tv = tick(V.tensor_tensor(VU[0:M, kv_, :, 0:64],
                                              ps[0:M, km, :].rearrange("p (h d) -> p h d", h=8),
                                              bo[0:M, :].rearrange("p (h d) -> p h d", h=8), ALU.add), "v.V")
                    Ms.give(km, tv)
                    vt[bi // 4, 4 * i + j] = (kv_, tv)
                    yield
                xu["read"] = [tok]

            tz = tick(G.memset(VU[:, :, :, :], 1.0), "g.setup2")
            first = prep_b(0)
            for _ in range(2):
                next(first)
            for k in range(4):
                next(first)
                need(A, t_raw)
                th = tick(A.mul(Wl[0][:, k, :], raw[:, k, :], lnwb[:, k:k + 1]), "a.setup2")
                need(V, t_raw, th)
                t_wls = tick(V.scalar_tensor_tensor(Wl[1][:, k, :], raw[:, k, :], lnwb[:, k:k + 1],
                                                    Wl[0][:, k, :].bitcast(F), ALU.mult, ALU.subtract), "v.setup2")
            for k in (0, 1):
                QUs.give(k, t_wls)
                Sws.give(k, t_wls)

            class W:
                pass

            def scores_b(t, p):
                o = blocks[t.n // 4]
                tl = t.n % 4
                if p == 0:
                    t.s, t.ws = Sws.take()
                w_s = t.ws
                which = 1 if t.n % 16 == 0 else 2 if t.n % 16 == 15 else 0
                ks, w = SPs.take()
                need(PE, w, o["tq"], o["tk"])
                for k in range(2):
                    c = 2 * p + k
                    for h in range(2):
                        m = PE.matmul(ps[:, 2 * ks + h, 256 * k:256 * k + 256],
                                      QU[64 * h:64 * h + 64, o["q"], c, 128 * tl:128 * tl + 128],
                                      KU[64 * h:64 * h + 64, o["k"], c, 128 * tl:128 * tl + 256],
                                      start=True, stop=True)
                t.tq = tick(m, "pe.S")
                need(V, t.tq, w_s, t_wl2)
                tok = tick(V.tensor_tensor(Sw[:, t.s, 1024 * p:1024 * p + 1024].rearrange("p (j n) -> p j n", j=4),
                                           ps[:, 2 * ks:2 * ks + 2, :].rearrange("p b (k n) -> p (b k) n", k=2),
                                           mid(msk[:, which, :], 4), ALU.add), "v.Sadd")
                SPs.give(ks, tok)
                if p == 0:
                    return
                if tl == 3:
                    QUs.give(o["q"], t.tq)
                    KUs.give(o["k"], t.tq)
                sv = Sw[:, t.s, :].rearrange("p (h n) -> p h n", h=8)
                need(V, tok)
                tok = tick(V.tensor_reduce(mw[:, t.s, :], sv, X, ALU.max), "v.max")
                need(G, tok)
                t.sub = tick(G.tensor_tensor(sv, sv, last(mw[:, t.s, :], 256), ALU.subtract), "g.sub")

            def exp_b(t):
                need(A, t.sub)
                t.exp = tick(A.activation(Sw[:, t.s, :], Sw[:, t.s, :], ACT.Exp), "a.exp")

            def ptrans_b(t, q):
                kt, w = Ts.take()
                need(PE, w, t.exp)
                for c in range(4):
                    o = 512 * q + 128 * c
                    m = PE.transpose(ps[:, kt, 128 * c:128 * c + 128], Sw[:, t.s, o:o + 128], ident[:, :])
                tok = tick(m, "pe.PT")
                if q == 3:
                    Sws.give(t.s, tok)
                need(A, tok, free["PU"])
                t.pt = tick(A.copy(PU[:, 4 * q:4 * q + 4, :], ps[:, kt, :].rearrange("p (c n) -> p c n", c=4)), "a.PT")
                Ts.give(kt, t.pt)

            def pv_b(t, p):
                b, j = t.n // 16, t.n % 16
                v0, v1 = vt[b, j], vt[b, j + 1]
                if p == 0:
                    t.o, t.wo_ = Ons.take()
                w_o = t.wo_
                km, w = Ms.take()
                need(PE, w, t.pt, v0[1], v1[1])
                for jj in range(4):
                    bank, k = jj % 2, jj // 2
                    pos = 4 * p + 2 * bank + k
                    for ck, v in ((0, v0), (1, v1)):
                        m = PE.matmul(ps[:, km, 65 * jj:65 * jj + 65], PU[:, 2 * pos + ck, :],
                                      VU[:, v[0], 4 * p + jj, :], start=(ck == 0), stop=(ck == 1))
                tok = tick(m, "pe.PV")
                ov = ps[:, km, 0:260].rearrange("p (h e) -> p h e", e=65)
                kr, wr = Rc.take()
                need(V, tok, w_o, wr)
                tr = tick(V.reciprocal(rc[:, kr, 0:4], ov[:, :, 64]), "v.rc")
                need(V, tr)
                t.on = tick(V.tensor_tensor(On[:, t.o, 256 * p:256 * p + 256].rearrange("p (h d) -> p h d", h=4),
                                            ov[:, :, 0:64], last(rc[:, kr, 0:4], 64), ALU.mult), "v.On")
                Rc.give(kr, t.on)
                Ms.give(km, t.on)
                if p == 0:
                    return
                free["PU"] = [tok]
                VUs.give(v0[0], tok)
                if j == 15:
                    VUs.give(v1[0], tok)

            def wo_b(t, part):
                if part == 0:
                    t.km, w = Ms.take()
                    need(PE, w, t.te, t_wl2)
                km = t.km
                for c in (2 * part, 2 * part + 1):
                    m = PE.matmul(ps[:, km, :], OT[:, t.ot, c, :], Wlo[:, c, :], start=(c == 0), stop=(c == 3))
                if part == 0:
                    return
                tok = tick(m, "pe.Wo")
                OTs.give(t.ot, tok)
                x = XY[:, t.n % 3, :]
                need(V, tok, xy[t.n])
                ty = tick(V.tensor_tensor(x, ps[:, km, :], x, ALU.add), "v.y")
                Ms.give(km, ty)
                need(SY, ty)
                t_st = tick(SY.dma_start(Yd[128 * t.n:128 * t.n + 128, :], x), f"st.y{t.n % 3}", 16)
                ko, w = Yos.take()
                need(G, ty, w, t_wl2)
                to = tick(G.tensor_tensor(yo[:, ko, :], x, nulq[:, :], ALU.add), "g.yo")
                need(SY, to)
                Yos.give(ko, tick(SY.dma_start(out[128 * t.n:128 * t.n + 128, :], yo[:, ko, :]), f"st.o{ko}", 16))
                xyfree[t.n] = [t_st, to]

            idx_tok = {}

            def routing():
                kt, w = Ts.take()
                need(PE, w, s_tok, t_ident)
                tok = tick(PE.transpose(ps[:, kt, 0:128], scol[:, :, :].rearrange("p r n -> p (r n)"), ident[:, :]), "pe.rt")
                need(V, tok)
                tok = tick(V.tensor_copy(sr[:, :], ps[:, kt, 0:128]), "v.rt")
                Ts.give(kt, tok)
                need(V, tok)
                tok = tick(V.tensor_reduce(rcol[:, 0:1], sr[:, :], X, ALU.max), "v.rt")
                smax, na, M, part, lnv, T, cand, dd, sel = (rcol[:, i:i + 1] for i in (1, 2, 3, 4, 5, 6, 7, 8, 9))
                logk, kcol = cols[:, 4:5], cols[:, 5:6]
                yield
                kt, w = Ts.take()
                need(PE, w, tok)
                tok = tick(PE.transpose(ps[0:1, kt, 0:128], rcol[:, 0:1], ident[:, :]), "pe.rt")
                need(V, tok)
                tok = tick(V.tensor_reduce(er[0:1, 0:8], ps[0:1, kt, 0:128].rearrange("o (g i) -> o g i", i=16), X,
                                           ALU.max), "v.rt")
                Ts.give(kt, tok)
                need(V, tok)
                tok = tick(V.tensor_copy(zr[0:1, :].rearrange("o (g i) -> o g i", i=16), last(er[0:1, 0:8], 16)), "v.rt")
                yield
                kt, w = Ts.take()
                need(PE, w, tok)
                tok = tick(PE.matmul(ps[:, kt, 0:1], zr[0:1, :], ident[0:1, 0:1], start=True, stop=True), "pe.rt")
                need(V, tok)
                tok = tick(V.tensor_copy(smax, ps[:, kt, 0:1]), "v.rt")
                Ts.give(kt, tok)
                tok2 = tick(V.tensor_scalar(na, logk, -1.0, math.log(S), ALU.mult, ALU.add), "v.rt")
                need(V, tok, tok2)
                yield
                for it in range(1, ITERS):
                    tok = tick(V.tensor_tensor(M, smax, na, ALU.min), "v.rt")
                    need(V, tok)
                    tok = tick(V.tensor_scalar(zr[:, :], sr[:, :], na, M, ALU.min, ALU.subtract), "v.rt")
                    need(A, tok)
                    yield
                    te = tick(A.activation(er[:, :], zr[:, :], ACT.Exp, accum_out=part), "a.rt")
                    yield
                    km, w = Ms.take()
                    need(PE, te, w)
                    tok = tick(PE.matmul(ps[:, km, 0:1], grp[:, :], part, start=True, stop=True), "pe.rt")
                    need(A, tok)
                    tl2 = tick(A.activation(lnv, ps[:, km, 0:1], ACT.Ln), "a.rt")
                    Ms.give(km, tl2)
                    yield
                    need(V, tl2)
                    tok = tick(V.tensor_scalar(na, lnv, M, logk, ALU.add, ALU.subtract), "v.rt")
                    need(V, tok)
                tok = tick(V.tensor_scalar(zr[:, :], sr[:, :], na, None, ALU.subtract), "v.rt")
                need(V, tok)
                tok = tick(V.tensor_scalar(er[:, :], zr[:, :], 0.0, None, ALU.max), "v.rt")
                need(V, tok)
                tok = tick(V.tensor_tensor(zr[:, :], zr[:, :], er[:, :], ALU.subtract), "v.rt")
                yield
                need(A, tok)
                tok = tick(A.activation(sr[:, :], zr[:, :], ACT.Exp), "a.rt")
                need(V, tok)
                yield
                tok = tick(V.memset(T, 0.0), "v.rt")
                for bit in range(29, -1, -1):
                    need(V, tok)
                    tok = tick(V.tensor_scalar(cand.bitcast(I32), T.bitcast(I32), 1 << bit, None, ALU.bitwise_or), "v.rt")
                    need(V, tok)
                    tok = tick(V.tensor_scalar(zr[:, :], sr[:, :], cand, 0.0, ALU.is_ge, ALU.add, accum_out=part), "v.rt")
                    tok2 = tick(V.tensor_tensor(dd, cand, T, ALU.subtract), "v.rt")
                    yield
                    km, w = Ms.take()
                    need(PE, tok, w)
                    tok = tick(PE.matmul(ps[:, km, 0:1], grp[:, :], part, start=True, stop=True), "pe.rt")
                    need(V, tok, tok2)
                    tok = tick(V.tensor_scalar(sel, ps[:, km, 0:1], kcol, None, ALU.is_ge), "v.rt")
                    Ms.give(km, tok)
                    need(V, tok)
                    tok = tick(V.scalar_tensor_tensor(T, dd, sel, T, ALU.mult, ALU.add), "v.rt")
                need(V, tok)
                tok = tick(V.tensor_scalar(zr[:, :], sr[:, :], T, 0.0, ALU.is_gt, ALU.add, accum_out=rcol[:, 10:11]), "v.rt")
                tok = tick(V.tensor_scalar(er[:, :], sr[:, :], T, 0.0, ALU.is_equal, ALU.add, accum_out=rcol[:, 11:12]),
                           "v.rt")
                yield
                km, w = Ms.take()
                need(PE, tok, w)
                PE.matmul(ps[:, km, 0:1], grp[:, :], rcol[:, 10:11], start=True, stop=True)
                tok = tick(PE.matmul(ps[:, km, 1:2], tri[:, :], rcol[:, 11:12], start=True, stop=True), "pe.rt")
                need(V, tok)
                tok = tick(V.tensor_scalar(rcol[:, 12:13], ps[:, km, 0:1], -1.0, kcol, ALU.mult, ALU.add), "v.rt")
                need(V, tok)
                tok = tick(V.tensor_tensor(rcol[:, 13:14], rcol[:, 12:13], ps[:, km, 1:2], ALU.subtract), "v.rt")
                Ms.give(km, tok)
                yield
                t1 = tick(V.memset(cb[:, 128:256], 1.0), "v.rt")
                need(V, t1)
                tok = tick(V.tensor_tensor_scan(cb[:, 0:128], cb[:, 128:256], er[:, :], 0.0, ALU.mult, ALU.add), "v.rt")
                need(V, tok)
                tok = tick(V.tensor_scalar(cb[:, 0:128], cb[:, 0:128], rcol[:, 13:14], None, ALU.is_le), "v.rt")
                need(V, tok)
                tok = tick(V.tensor_tensor(er[:, :], er[:, :], cb[:, 0:128], ALU.mult), "v.rt")
                need(V, tok)
                tok = tick(V.tensor_tensor(er[:, :], er[:, :], zr[:, :], ALU.add), "v.rt")
                need(V, tok)
                tok = tick(V.tensor_tensor_scan(cb[:, 0:128], cb[:, 128:256], er[:, :], 0.0, ALU.mult, ALU.add), "v.rt")
                t1 = tick(V.tensor_scalar(zr[:, :], sr[:, :], -1.0, 1.0, ALU.mult, ALU.add), "v.rt")
                need(V, t1, tok)
                tf = tick(V.tensor_tensor(zr[:, :], zr[:, :], sr[:, :], ALU.add), "v.rt")
                yield
                km, w = Ms.take()
                need(PE, tok, w)
                tok = tick(PE.matmul(ps[:, km, 0:1], tri[:, :], cb[:, 127:128], start=True, stop=True), "pe.rt")
                need(V, tok)
                tok = tick(V.tensor_scalar(er[:, :], cb[:, 0:128], ps[:, km, 0:1], None, ALU.add), "v.rt")
                Ms.give(km, tok)
                need(SY, tok, tf)
                tick(SY.dma_start(cumd.rearrange("g (i n) -> (g i) n", i=16), er[:, :]), "st.rt", 16)
                t_f = tick(SY.dma_start(fd.rearrange("(p n) o -> p (n o)", n=128), zr[:, :]), "st.rt", 16)
                need(SY, t_f, tok)
                yield
                tb = []
                for g in range(8):
                    r, b = g // 4, g % 4
                    need(SY, tb)
                    for q in range(4):
                        need(SY, tb)
                        tl_ = load(cb[:, :], cumd[g:g + 1, 512 * q:512 * q + 512].broadcast_to([128, 512]), "ld.cb")
                        yield
                        yield
                        for j in range((2, 4)[r]):
                            c = (2 * b + j) if r == 0 else (8 + 4 * b + j)
                            need(V, tl_)
                            tok = tick(V.tensor_scalar(Jk, cb[:, :], cols[:, j:j + 1], 0.0, ALU.is_le, ALU.add,
                                                       accum_out=idx4[:, c, q:q + 1]), "v.idx")
                            need(V, tok)
                            if j % 2:
                                yield
                        tb = [tok]
                    c0 = 2 * b if r == 0 else 8 + 4 * b
                    c1 = c0 + (2, 4)[r]
                    tok = tick(V.tensor_reduce(idxf[:, c0:c1], idx4[:, c0:c1, :], X, ALU.add), "v.idx")
                    need(V, tok)
                    tok = tick(V.tensor_scalar(idxf[:, c0:c1], idxf[:, c0:c1], float(S * b), None, ALU.add), "v.idx")
                    need(V, tok)
                    tick(V.tensor_copy(idx[:, c0:c1], idxf[:, c0:c1]), "v.idx")
                    tok = tick(V.tensor_scalar(idxf[:, c0:c1], idxf[:, c0:c1], float(B * S * r), None, ALU.add), "v.idx")
                    need(V, tok)
                    tok = tick(V.tensor_copy(idxs[:, c0:c1], idxf[:, c0:c1]), "v.idx")
                    tb.append(tok)
                    idx_tok[0] = tok
                    yield

            Gs, XHs, hb = Slots(3), Slots(6), {}

            def gather(dst, src, col, name):
                return tick(G.indirect_dma_start(dst, None, src, bass.IndirectOffsetOnAxis(col, 0)), name, 16)

            def gather_c(b):
                o = {}
                hb[b] = o
                k, wb = Gs.take()
                o["kf"] = k
                ci = [2 * b, 2 * b + 1] + [8 + 4 * b + j for j in range(4)]
                need(G, wb)
                o["f"] = []
                slots = []
                for j in range(6):
                    kx, w = XHs.take()
                    need(G, w)
                    tg = gather(XH[:, kx, :], X3d, idx[:, ci[j]:ci[j] + 1], f"gx{kx}")
                    tf = gather(fg[:, k, j:j + 1], fd, idxs[:, ci[j]:ci[j] + 1], f"gf{k}{j}")
                    o["f"].append(tf)
                    slots.append((kx, tg))
                    if j % 2 and not b:
                        for _ in range(4):
                            yield
                yield
                yield
                need(V, wb)
                for j, (kx, tg) in enumerate(slots):
                    need(V, tg)
                    tok = tick(V.bn_stats(sth[:, j, :], XH[:, kx, :]), "v.bnstats")
                need(V, tok)
                for j in range(6):
                    tok = tick(V.bn_aggr(mvh[:, j, :], sth[:, j, :]), "v.bnaggr")
                need(V, tok)
                tok = tick(V.tensor_scalar(rsh[:, :], mvh[:, :, 1], 1e-5, None, ALU.add), "v.vareps")
                need(G, tok)
                t_rs = tick(G.tensor_tensor(rsh[:, :], rsh[:, :], mhalf[:, 0:6], ALU.pow), "g.rstd")
                yield
                need(V, t_rs)
                for j, (kx, tg) in enumerate(slots):
                    slots[j] = (kx, tick(V.tensor_scalar(XH[:, kx, :], XH[:, kx, :], mvh[:, j, 0:1], rsh[:, j:j + 1],
                                                         ALU.subtract, ALU.mult), "v.zh"))
                yield
                need(A, wb)
                for j, (kx, tg) in enumerate(slots):
                    need(A, tg, ta if j else None)
                    ta = tick(A.activation(XH[:, 7, :], XH[:, kx, :], ACT.Square, accum_out=ss[:, k, j:j + 1]), "a.sq")
                need(G, ta, t_half)
                tok = tick(G.tensor_tensor(ss[:, k, 0:6], ss[:, k, 0:6], half[:, 0:6], ALU.pow), "g.norm")
                need(V, tok)
                tok = tick(V.tensor_scalar(ss[:, k, 0:6], ss[:, k, 0:6], 1e-12, None, ALU.max), "v.norm")
                need(V, tok)
                tok = tick(V.reciprocal(ss[:, k, 0:6], ss[:, k, 0:6]), "v.norm")
                need(V, tok)
                t_n = tick(V.tensor_scalar(ss[:, k, 0:6], ss[:, k, 0:6], math.sqrt(float(D)), None, ALU.mult), "v.norm")
                o["slots"], o["tn"] = slots, t_n
                yield
            bg, rt_ = Later(), Later()
            rt_.add(routing())
            bg.add(first)
            bg.drain()
            made = {1: bg.add(prep_b(1))}
            tiles = []
            for n in range(NT):
                t = W()
                t.n = n
                tiles.append(t)
            for n in range(NT + 2):
                cur = tiles[n] if n < NT else None
                p1 = tiles[n - 1] if 1 <= n <= NT else None
                p2 = tiles[n - 2] if n >= 2 else None
                if n == NT - 4:
                    while rt_.piece():
                        pass
                    need(SY, xu["read"], ("pe.K", fl.val["pe.K"]))
                    for x, name in zip(wc, ("wkv", "wh", "who")):
                        t_wh = load(x[:, :, :], a[name], "ld.wh")
                    need(G, xu["read"])
                    bg.add(gather_c(0))
                if cur is not None:
                    if n % 4 == 3 and n // 4 + 1 < NB:
                        bg.finish(made[n // 4 + 1])
                    load_xy(n)
                    scores_b(cur, 0)
                if p2 is not None:
                    p2.ot, w = OTs.take()
                    p2.te = turn4(On[:, p2.o, :], p2.on, lambda tok: Ons.give(p2.o, tok), OT[:, p2.ot, :, :], w, "OT")
                rt_.piece()
                if cur is not None:
                    scores_b(cur, 1)
                    if n % 4 == 3 and n // 4 + 2 < NB:
                        made[n // 4 + 2] = bg.add(prep_b(n // 4 + 2))
                if p1 is not None:
                    ptrans_b(p1, 0)
                rt_.piece()
                if p1 is not None:
                    ptrans_b(p1, 1)
                bg.piece()
                rt_.piece()
                if p1 is not None:
                    ptrans_b(p1, 2)
                if p2 is not None:
                    wo_b(p2, 0)
                if p1 is not None:
                    ptrans_b(p1, 3)
                if p2 is not None:
                    wo_b(p2, 1)
                bg.piece()
                rt_.piece()
                if p1 is not None:
                    pv_b(p1, 0)
                bg.piece()
                rt_.piece()
                if p1 is not None:
                    pv_b(p1, 1)
                if cur is not None:
                    exp_b(cur)
                bg.piece()
                rt_.piece()
            bg.drain()
            rt_.drain()
            done = fl.all()
        for e in (PE, V, A, G, SY):
            need(e, done)

        with ExitStack() as pc:
            sb = alloc(pc)
            OTh = [sb(f"OTh{i}", [128, 2, 4, 128], R) for i in (0, 1)]
            Wkv, Wh, Who = ((h, l, w) for h, l, w in zip(hi, lo, wc))
            nkb = sb("nkb", [128, 4, 8])
            nvb = sb("nvb", [128, 8, 65])
            yg = sb("yg", [128, 3, 2, D])
            xh = [sb(f"xh{i}", [128, 4, 768], R) for i in (0, 1)]
            QH = sb("QH", [128, 2, 4, 256])
            KH = sb("KH", [128, 2, 4, 512])
            VH = sb("VH", [128, 2, 4, 8, 65])
            PH = sb("PH", [128, 3, D])
            PTH = sb("PTH", [128, 2, 4, 128])
            sn = sb("sn", [128, 2, 8])
            nm = sb("nm", [128, 2, 8])
            m0 = sb("m0", [128, 2, 8])
            pn = sb("pn", [128, 2, 8])
            on2 = sb("on2", [128, 2, 4, 65])
            oh = sb("oh", [128, 2, D])
            Bs, PHs, PTs, Qt, O2s, SHs, OHs = (Slots(2), Slots(3), Slots(2), Slots(2), Slots(2), Slots(3),
                                                    Slots(2))
            load(nkb[:, :, :], a["nkb"], "ld.nul")
            t_nul = load(nvb[:, :, :], a["nvb"], "ld.nul")
            tzh = tick(G.memset(VH[:, :, :, :, :], 1.0), "g.setup3")
            t_g = {}

            def split_h(parts, scale):
                for k in range(4):
                    h, l, w = (x[:, k, :] for x in parts)
                    need(A, t_wh)
                    th = tick(A.mul(h, w, gam[:, k:k + 1]) if scale else A.copy(h, w), "a.setup3")
                    need(V, t_wh, th)
                    if scale:
                        tok = tick(V.scalar_tensor_tensor(l, w, gam[:, k:k + 1], h.bitcast(F),
                                                          ALU.mult, ALU.subtract), "v.setup3")
                    else:
                        tok = tick(V.tensor_tensor(l, w, h.bitcast(F), ALU.subtract), "v.setup3")
                return tok

            xhr = {"read": []}

            def prep_c(b):
                o = hb[b]
                kf, slots, t_n = o["kf"], o["slots"], o["tn"]

                def rms(j):
                    kx, tg = slots[j]
                    kn, w = Xn.take()
                    need(V, w, t_n, tg)
                    tn = tick(V.tensor_scalar(xn[:, kn, :], XH[:, kx, :], ss[:, kf, j:j + 1], None, ALU.mult), "v.rms")
                    XHs.give(kx, tn)
                    return kn, tn

                nxt = rms(0)
                for j in range(6):
                    kn, tn = nxt
                    if j < 5:
                        nxt = rms(j + 1)
                    te = turn4(xn[:, kn, :], tn, lambda tok, kn=kn: Xn.give(kn, tok),
                               xh[0][:, :, 128 * j:128 * j + 128], xhr["read"], "xT",
                               xh[1][:, :, 128 * j:128 * j + 128])()
                    yield
                yield
                k, wb = Bs.take()
                o["k"] = k
                o["y"] = [gather(yg[:, kf, j, :], Yd, idx[:, 2 * b + j:2 * b + j + 1], f"gy{kf}{j}") for j in (0, 1)]
                for c in range(4):
                    km, w = Ms.take()
                    need(PE, te, t_g["q"])
                    tok = tick(mms3(ps[:, km, 0:256], [(Wh[0][:, i, 128 * c:128 * c + 128], Wh[1][:, i, 128 * c:128 * c + 128],
                                                        xh[0][:, i, 0:256], xh[1][:, i, 0:256])
                                                       for i in range(4)], w), "pe.Q")
                    need(A, tok, wb)
                    o["tq"] = tick(A.mul(QH[:, k, c, :], ps[:, km, 0:256], 0.125), "a.Q")
                    Ms.give(km, o["tq"])
                    yield
                for c in range(4):
                    km, w = Ms.take()
                    need(PE, t_g["kv"])
                    tok = tick(mms3(ps[:, km, :], [(Wkv[0][:, i, 128 * c:128 * c + 128],
                                                    Wkv[1][:, i, 128 * c:128 * c + 128],
                                                    xh[0][:, i, 256:768], xh[1][:, i, 256:768])
                                                   for i in range(4)], w), "pe.K")
                    need(A, tok, wb)
                    o["tk"] = tick(A.copy(KH[:, k, c, :], ps[:, km, :]), "a.K")
                    Ms.give(km, o["tk"])
                    yield
                for j in range(4):
                    km, w = Ms.take()
                    q = slice(256 + 128 * j, 384 + 128 * j)
                    tok = tick(mms3(ps[:, km, :], [(xh[0][:, i, q], xh[1][:, i, q],
                                                    Wkv[0][:, i, D:2 * D], Wkv[1][:, i, D:2 * D])
                                                   for i in range(4)], w), "pe.V")
                    need(V, tok, wb, tzh, o["f"])
                    o["tv"] = tick(V.tensor_scalar(VH[:, k, j, :, 0:64], ps[:, km, :].rearrange("p (h d) -> p h d", h=8),
                                                   fg[:, kf, 2 + j:3 + j], None, ALU.mult), "v.V")
                    Ms.give(km, o["tv"])
                    yield
                xhr["read"] = [tok]

            def null_scores(b, qt):
                o = hb[b]
                kq, w_q = Qt.take()
                km, w = Ms.take()
                need(PE, o["tq"], t_nul)
                tok = tick(mms(ps[:, km, 0:8], [(QH[:, o["k"], c, 128 * qt:128 * qt + 128], nkb[:, c, :])
                                                 for c in range(4)], w), "pe.sn")
                need(V, tok, w_q)
                tsn = tick(V.tensor_copy(sn[:, kq, :], ps[:, km, 0:8]), "v.sn")
                Ms.give(km, tsn)
                return kq, tsn

            class H:
                pass

            def scores_c(t):
                o, k = hb[t.b], hb[t.b]["k"]
                if t.h == 0:
                    t.g.kq, t.g.tsn = null_scores(t.b, t.qt)
                kq = t.g.kq
                ks, w = SHs.take()
                need(PE, w, o["tq"], o["tk"])
                p0, c = 64 * (t.h % 2), t.h // 2
                t.tq = tick(PE.matmul(ps[:, ks, :], QH[p0:p0 + 64, k, c, 128 * t.qt:128 * t.qt + 128],
                                      KH[p0:p0 + 64, k, c, :], start=True, stop=True), "pe.S")
                need(V, t.tq, t.g.tsn)
                tok = tick(V.tensor_reduce(m0[:, kq, t.h:t.h + 1], ps[:, ks, :], X, ALU.max), "v.max")
                need(V, tok)
                tok = tick(V.tensor_scalar(nm[:, kq, t.h:t.h + 1], m0[:, kq, t.h:t.h + 1], sn[:, kq, t.h:t.h + 1], -1.0,
                                           ALU.max, ALU.mult), "v.nm")
                t.g.tnm = tok
                t.p, w = PHs.take()
                need(A, tok, w)
                t.exp = tick(A.activation(PH[:, t.p, :], ps[:, ks, :], ACT.Exp, bias=nm[:, kq, t.h:t.h + 1]), "a.exp")
                SHs.give(ks, t.exp)
                if t.h % 4 == 3:
                    q = slice(t.h - 3, t.h + 1)
                    need(V, tok)
                    tok = tick(V.tensor_tensor(pn[:, kq, q], sn[:, kq, q], nm[:, kq, q], ALU.add), "v.pn")
                    need(A, tok)
                    t.g.tpn = tick(A.activation(pn[:, kq, q], pn[:, kq, q], ACT.Exp), "a.pn")

            def trans_c(t):
                kt, w = Ts.take()
                need(PE, w, t.exp)
                for c in range(4):
                    m = PE.transpose(ps[:, kt, 128 * c:128 * c + 128], PH[:, t.p, 128 * c:128 * c + 128], ident[:, :])
                tok = tick(m, "pe.PT")
                PHs.give(t.p, tok)
                t.pt, w = PTs.take()
                need(A, tok, w)
                t.tp = tick(A.copy(PTH[:, t.pt, :, :], ps[:, kt, :].rearrange("p (c n) -> p c n", c=4)), "a.PT")
                Ts.give(kt, t.tp)

            def pv_c(t):
                o, k = hb[t.b], hb[t.b]["k"]
                g = t.g
                if t.h % 4 == 0:
                    _, w = Oh.take()
                    need(PE, w)
                j = t.h % 4
                need(PE, t.tp, o["tv"])
                for c in range(4):
                    m = PE.matmul(ps[:, 3, 65 * j:65 * j + 65], PTH[:, t.pt, c, :], VH[:, k, c, t.h, :],
                                  start=(c == 0), stop=(c == 3))
                tok = tick(m, "pe.PV")
                PTs.give(t.pt, tok)
                if j < 3:
                    return
                p = t.h // 4
                if p == 0:
                    g.o, w = Ons.take()
                    need(V, w)
                k2, w = O2s.take()
                need(V, g.tpn, w, tok, t_nul)
                tk = tick(V.tensor_tensor(on2[:, k2, :, :], nvb[:, 4 * p:4 * p + 4, :], last(pn[:, g.kq, 4 * p:4 * p + 4], 65),
                                          ALU.mult), "v.on2")
                need(V, tk)
                tk = tick(V.tensor_tensor(on2[:, k2, :, :], ps[:, 3, 0:260].rearrange("p (h e) -> p h e", e=65),
                                          on2[:, k2, :, :], ALU.add), "v.on2")
                Oh.give(0, tk)
                kr, w = Rc.take()
                need(V, tk, w)
                tk = tick(V.reciprocal(rc[:, kr, 0:4], on2[:, k2, :, 64]), "v.rc")
                need(V, tk)
                g.on = tick(V.tensor_tensor(On[:, g.o, 256 * p:256 * p + 256].rearrange("p (h d) -> p h d", h=4),
                                            on2[:, k2, :, 0:64], last(rc[:, kr, 0:4], 64), ALU.mult), "v.On")
                Rc.give(kr, g.on)
                O2s.give(k2, g.on)
                if p == 1:
                    Qt.give(g.kq, g.on)

            def out_c(g):
                o, k = hb[g.b], hb[g.b]["kf"]
                ot, w = OTs.take()
                te = turn4(On[:, g.o, :], g.on, lambda tok: Ons.give(g.o, tok), OTh[0][:, ot, :, :], w, "OT",
                           OTh[1][:, ot, :, :])()
                km, w = Ms.take()
                need(PE, te, t_g["o"])
                tok = tick(mms3(ps[:, km, :], [(OTh[0][:, ot, c, :], OTh[1][:, ot, c, :], Who[0][:, c, :], Who[1][:, c, :])
                                               for c in range(4)], w), "pe.Wo")
                OTs.give(ot, tok)
                ko, w = OHs.take()
                need(V, tok, w, o["f"], o["y"])
                th = tick(V.scalar_tensor_tensor(oh[:, ko, :], ps[:, km, :], fg[:, k, g.qt:g.qt + 1], yg[:, k, g.qt, :],
                                                 ALU.mult, ALU.add), "v.oh")
                Ms.give(km, th)
                need(G, th)
                c = 2 * g.b + g.qt
                ts = tick(G.indirect_dma_start(out, bass.IndirectOffsetOnAxis(idx[:, c:c + 1], 0), oh[:, ko, :], None),
                          f"sc{ko}", 16)
                OHs.give(ko, ts)
                if g.qt == 1:
                    Bs.give(o["k"], g.last)
                    Gs.give(k, th)

            Oh = Slots(1)
            bg = Later()
            bg.add(prep_c(0))
            t_g["q"] = split_h(Wh, True)
            for _ in range(8):
                bg.piece()
            t_g["kv"] = split_h(Wkv, True)
            t_g["o"] = split_h(Who, False)
            bg.drain()
            made = {}
            debt, rate = 0.0, 29 / 16
            seq = []
            for b in range(B):
                for qt in range(2):
                    g = H()
                    g.b, g.qt = b, qt
                    for h in range(8):
                        t = H()
                        t.g, t.b, t.qt, t.h = g, b, qt, h
                        seq.append(t)

            def half_step():
                nonlocal debt
                debt += rate / 2
                while debt >= 1:
                    debt -= 1
                    bg.piece()

            for n in range(len(seq) + 5):
                if n < len(seq):
                    t = seq[n]
                    if t.qt == 0 and t.h == 0:
                        if t.b:
                            bg.finish(made[t.b])
                        if t.b + 1 < B:
                            bg.add(gather_c(t.b + 1))
                            made[t.b + 1] = bg.add(prep_c(t.b + 1))
                    scores_c(t)
                half_step()
                if 2 <= n < len(seq) + 2:
                    trans_c(seq[n - 2])
                half_step()
                if 3 <= n < len(seq) + 3:
                    t = seq[n - 3]
                    pv_c(t)
                    if t.h == 7:
                        t.g.last = ("pe.PV", fl.val["pe.PV"])
                if 4 <= n < len(seq) + 4 and seq[n - 4].h == 7:
                    out_c(seq[n - 4].g)
            done = fl.all()
        for e in (PE, V, A, G, SY):
            need(e, done)


def wT(w, np):
    w = np.asarray(w)
    o, i = w.shape
    return np.ascontiguousarray(w.T.reshape(i // 128, 128, o).transpose(1, 0, 2))


def rows(v, np, n=128):
    return np.ascontiguousarray(np.broadcast_to(np.asarray(v)[None], (n, v.shape[0])))


def layout(inp, np):
    g = {k: np.asarray(v) for k, v in inp.items()}
    d = {}
    col = lambda v: v.reshape(4, 128).T
    d["x"] = g["x"].reshape(B * S, D)
    for L in (0, 1):
        p = f"L{L}_xcond_"
        for w in "qkvo":
            d[f"w{w}{L}"] = wT(g[p + "W" + w], np)
        d[f"bo{L}"] = rows(g[p + "bo"], np)
        d[f"bv{L}"] = rows(g[p + "bv"], np, NK)
    d["bq"] = np.ascontiguousarray(np.stack([col(g["L0_xcond_bq"]), col(g["L1_xcond_bq"])], 1))
    kc = np.zeros((128, 16), np.float32)
    kc[:, 0:4], kc[:, 4:8] = col(g["L0_xcond_bk"]), col(g["L1_xcond_bk"])
    kc[:, 8:12] = g["condB_tau"][None]
    d["kcol"] = kc
    d["delta"] = np.ascontiguousarray(np.broadcast_to(g["fside_BxS2_0"][None], (128, B, NK)))
    d["ctxT"] = np.ascontiguousarray(g["ctx_1024"].reshape(B * NK, 4, 128).transpose(2, 1, 0))
    d["win"] = wT(np.concatenate([g["L0_ffn_Win"].T] * 2, 0), np)
    d["wout"] = np.concatenate([g["L0_ffn_Wout"]] * 2, 0)
    d["bout"] = rows(g["L0_ffn_bout"], np)
    pair = lambda w: w.reshape(64, 8, 2).transpose(2, 0, 1).reshape(128, 8)
    fc = np.zeros((128, 32), np.float32)
    fc[:, 0:8], fc[:, 8:16], fc[:, 16:24] = pair(g["L0_ffn_W1"]), pair(g["L0_ffn_b1"]), pair(g["L0_ffn_W2"])
    fc[:, 24] = np.concatenate([g["L0_ffn_bin_"]] * 2)
    fc[:, 25] = np.concatenate([g["L0_ffn_b2"]] * 2)
    d["fcol"] = fc
    d["rt"] = np.ascontiguousarray(np.broadcast_to(
        np.stack([g["L1_ffn_rt_q"][0], g["L1_ffn_rt_kv"][0]])[None], (128, 2, D)))
    d["c_ident"] = np.eye(128, dtype=np.float32)
    p = np.arange(128)
    d["c_grp"] = (p[:, None] // 16 == p[None] // 16).astype(np.float32)
    d["c_tri"] = ((p[:, None] // 16 == p[None] // 16) & (p[:, None] < p[None])).astype(np.float32)
    cols = np.zeros((128, 16), np.float32)
    for j in range(4):
        cols[:, j] = p + 128 * j
    cols[:, 4] = np.where(p < 64, LOGK[0], LOGK[1])
    cols[:, 5] = np.where(p < 64, NQ, NKV)
    d["cols"] = cols
    d["wqkv"] = wT(g["L1_ffn_Wqkv"], np)
    d["wlo"] = wT(g["L1_ffn_Wout_l"], np)
    d["lnwb"] = np.ascontiguousarray(np.concatenate([col(g["L1_ffn_ln_w"]), col(g["L1_ffn_ln_b"])], 1))
    d["nulq"] = rows(g["L1_ffn_null_q"], np)
    m = np.zeros((128, 3, 256), np.float32)
    m[:64, :, 192:] = -1e30
    m[64:, :, :64] = -1e30
    m[:, 1, :64] = -1e30
    m[:, 2, 192:] = -1e30
    d["c_mask"] = m
    d["wh"] = wT(g["L1_ffn_Wq"], np)
    d["wkv"] = wT(g["L1_ffn_Wkv"].reshape(8, 2, 64, D).transpose(1, 0, 2, 3).reshape(2 * D, D), np)
    d["who"] = wT(g["L1_ffn_Wout_h"], np)
    d["gam"] = np.ascontiguousarray(col(g["L1_ffn_gamma"]))
    nk = np.zeros((8, 64, 8), np.float32)
    for h in range(8):
        nk[h, :, h] = g["L1_ffn_null_kv"][0, h]
    d["nkb"] = np.ascontiguousarray(nk.reshape(4, 128, 8).transpose(1, 0, 2))
    nv = np.ones((128, 8, 65), np.float32)
    nv[:, :, :64] = g["L1_ffn_null_kv"][1][None]
    d["nvb"] = nv
    return d


def kernel(**inputs):
    import numpy as np
    import concourse.bacc as bacc
    from concourse.bass_utils import run_bass_kernel_spmd as run

    nc = bacc.Bacc("TRN2", target_bir_lowering=False, num_devices=1)
    arrays = {"in_" + k: v for k, v in layout(inputs, np).items()}
    args = {k[3:]: nc.dram_tensor(k, v.shape, mybir.dt.from_np(v.dtype), kind="ExternalInput").ap()
            for k, v in arrays.items()}
    out = nc.dram_tensor("out_0", (B * S, D), F, kind="ExternalOutput").ap()
    build(nc, args, out)
    r = run(nc, [arrays], core_ids=[0])
    return r.results[0]["out_0"].reshape(B, S, D)
```
